# Optimizing a Trainium2 kernel written in Bass

```python
import numpy as np
import jax
import jax.numpy as jnp

def _softmax(x, axis=-1):
    return jax.nn.softmax(x, axis=axis)

def _gelu(x):
    return jax.nn.gelu(x, approximate=True)

def _silu(x):
    return jax.nn.silu(x)

def _sigmoid(x):
    return jax.nn.sigmoid(x)

def _layernorm(x, axis=-1, eps=1e-05):
    m = jnp.mean(x, axis=axis, keepdims=True)
    v = jnp.var(x, axis=axis, keepdims=True)
    return (x - m) / jnp.sqrt(v + eps)

def _scatter_add(tgt, idx, src, axis=0):
    return tgt.at[idx].add(src)

def _segment_sum(src, seg, n):
    return jax.ops.segment_sum(src, seg, n)
kernel_name = 'mk_early_fusion_d1_tok_img512_r4_4524a9'

def setup_inputs(seed: int=0):
    np.random.seed(seed)
    _w = jnp.asarray

    def _rec_inputs():
        import jax
        import jax.numpy as jnp
        _rk = jax.random.key(seed)
        x = -0.000356955 + 1 * jax.random.normal(jax.random.fold_in(_rk, 1), (64, 3, 96, 96), jnp.float32)
        txt = -3.85354e-11 + 0.999983 * jax.random.normal(jax.random.fold_in(_rk, 2), (64, 128, 128), jnp.float32)
        return (x, txt)
    x, txt = _rec_inputs()

    def _L0_tok_setup():
        import jax, jax.numpy as jnp
        import numpy as np
        P = 16
        SHIFT = P // 2
        EPS = 1e-05

        def _shift2d(img, dy, dx):
            H, W = (img.shape[2], img.shape[3])
            pad = ((0, 0), (0, 0), (max(dy, 0), max(-dy, 0)), (max(dx, 0), max(-dx, 0)))
            z = jnp.pad(img, pad)
            return z[:, :, max(-dy, 0):max(-dy, 0) + H, max(-dx, 0):max(-dx, 0) + W]

        def _patchify(img):
            B, C, H, W = img.shape
            nH, nW = (H // P, W // P)
            t = img.reshape(B, C, nH, P, nW, P).transpose(0, 2, 4, 1, 3, 5)
            return t.reshape(B, nH * nW, C * P * P)
        key = jax.random.key(seed)
        ks = jax.random.split(key, 8)
        B, C, H, Wd = (128, 3, 224, 224)
        embed_dim = 128
        d_main = embed_dim // 2
        d_shift = embed_dim // 8
        fan_in = C * P * P
        std = 0.02
        x = jax.random.normal(ks[0], (B, C, H, Wd), dtype=jnp.float32)
        W_main = jax.random.normal(ks[1], (d_main, fan_in), dtype=jnp.float32) * std
        b_main = jnp.zeros((d_main,), dtype=jnp.float32)
        W_sx = jax.random.normal(ks[2], (d_shift, fan_in), dtype=jnp.float32) * std
        b_sx = jnp.zeros((d_shift,), dtype=jnp.float32)
        W_sy = jax.random.normal(ks[3], (d_shift, fan_in), dtype=jnp.float32) * std
        b_sy = jnp.zeros((d_shift,), dtype=jnp.float32)
        ln_g = jnp.ones((embed_dim,), dtype=jnp.float32)
        ln_b = jnp.zeros((embed_dim,), dtype=jnp.float32)
        return {'x': x, 'W_main': W_main, 'b_main': b_main, 'W_sx': W_sx, 'b_sx': b_sx, 'W_sy': W_sy, 'b_sy': b_sy, 'ln_g': ln_g, 'ln_b': ln_b}
    _L0_tok_all = _L0_tok_setup()
    _L0_tok_in = {k: v for k, v in _L0_tok_all.items() if k in ('W_main', 'b_main', 'W_sx', 'b_sx', 'W_sy', 'b_sy', 'ln_g', 'ln_b')}
    del _L0_tok_all

    def _L0_attn_setup():
        import jax, jax.numpy as jnp
        import numpy as np
        B, N, C = (2, 1024, 128)
        NUM_HEADS = 8
        HEAD_DIM = C // NUM_HEADS
        SCALE = HEAD_DIM ** (-0.5)
        THETA = 10000.0

        def _rope(x, seq_len, head_dim):
            freqs = 1.0 / THETA ** (jnp.arange(0, head_dim, 2, dtype=jnp.float32) / head_dim)
            t = jnp.arange(seq_len, dtype=jnp.float32)
            freqs_cis = jnp.outer(t, freqs)
            sin_f = jnp.sin(freqs_cis)
            cos_f = jnp.cos(freqs_cis)
            x_even = x[..., ::2]
            x_odd = x[..., 1::2]
            rot = jnp.stack([x_even * cos_f - x_odd * sin_f, x_even * sin_f + x_odd * cos_f], axis=-1)
            return rot.reshape(x.shape)
        key = jax.random.key(seed)
        ks = jax.random.split(key, 5)
        x = jax.random.normal(ks[0], (B, N, C), dtype=jnp.float32)
        Wqkv = jax.random.normal(ks[1], (3 * C, C), dtype=jnp.float32) * 0.02
        bqkv = jax.random.normal(ks[2], (3 * C,), dtype=jnp.float32) * 0.02
        Wproj = jax.random.normal(ks[3], (C, C), dtype=jnp.float32) * 0.02
        bproj = jax.random.normal(ks[4], (C,), dtype=jnp.float32) * 0.02
        return {'x': x, 'Wqkv': Wqkv, 'bqkv': bqkv, 'Wproj': Wproj, 'bproj': bproj}
    _L0_attn_all = _L0_attn_setup()
    _L0_attn_in = {k: v for k, v in _L0_attn_all.items() if k in ('Wqkv', 'bqkv', 'Wproj', 'bproj')}
    del _L0_attn_all

    def _L0_ffn_setup():
        import jax, jax.numpy as jnp
        import numpy as np
        EPS = 1e-05
        NUM_HEADS = 8
        TOP_K = 2
        CAP_FACTOR = 2

        def layernorm(x, g, b):
            m = jnp.mean(x, axis=-1, keepdims=True)
            v = jnp.var(x, axis=-1, keepdims=True)
            return (x - m) * jax.lax.rsqrt(v + EPS) * g + b
        key = jax.random.key(seed)
        ks = jax.random.split(key, 16)
        B, S, H, E, F = (2, 512, 128, 64, 512)
        s = 0.02
        return {'x': jax.random.normal(ks[0], (B, S, H), jnp.float32), 'ln1_g': jnp.ones((H,), jnp.float32), 'ln1_b': jnp.zeros((H,), jnp.float32), 'wq': jax.random.normal(ks[1], (H, H), jnp.float32) * s, 'wk': jax.random.normal(ks[2], (H, H), jnp.float32) * s, 'wv': jax.random.normal(ks[3], (H, H), jnp.float32) * s, 'wo': jax.random.normal(ks[4], (H, H), jnp.float32) * s, 'ln2_g': jnp.ones((H,), jnp.float32), 'ln2_b': jnp.zeros((H,), jnp.float32), 'wr': jax.random.normal(ks[5], (H, E), jnp.float32) * s, 'w1': jax.random.normal(ks[6], (E, H, F), jnp.float32) * s, 'b1': jnp.zeros((E, F), jnp.float32), 'w2': jax.random.normal(ks[7], (E, F, H), jnp.float32) * s, 'b2': jnp.zeros((E, H), jnp.float32)}
    _L0_ffn_all = _L0_ffn_setup()
    _L0_ffn_in = {k: v for k, v in _L0_ffn_all.items() if k in ('ln1_g', 'ln1_b', 'wq', 'wk', 'wv', 'wo', 'ln2_g', 'ln2_b', 'wr', 'w1', 'b1', 'w2', 'b2')}
    del _L0_ffn_all
    return {'x': x, 'txt': txt, 'L0_tok_W_main': _L0_tok_in['W_main'], 'L0_tok_b_main': _L0_tok_in['b_main'], 'L0_tok_W_sx': _L0_tok_in['W_sx'], 'L0_tok_b_sx': _L0_tok_in['b_sx'], 'L0_tok_W_sy': _L0_tok_in['W_sy'], 'L0_tok_b_sy': _L0_tok_in['b_sy'], 'L0_tok_ln_g': _L0_tok_in['ln_g'], 'L0_tok_ln_b': _L0_tok_in['ln_b'], 'L0_attn_Wqkv': _L0_attn_in['Wqkv'], 'L0_attn_bqkv': _L0_attn_in['bqkv'], 'L0_attn_Wproj': _L0_attn_in['Wproj'], 'L0_attn_bproj': _L0_attn_in['bproj'], 'L0_ffn_ln1_g': _L0_ffn_in['ln1_g'], 'L0_ffn_ln1_b': _L0_ffn_in['ln1_b'], 'L0_ffn_wq': _L0_ffn_in['wq'], 'L0_ffn_wk': _L0_ffn_in['wk'], 'L0_ffn_wv': _L0_ffn_in['wv'], 'L0_ffn_wo': _L0_ffn_in['wo'], 'L0_ffn_ln2_g': _L0_ffn_in['ln2_g'], 'L0_ffn_ln2_b': _L0_ffn_in['ln2_b'], 'L0_ffn_wr': _L0_ffn_in['wr'], 'L0_ffn_w1': _L0_ffn_in['w1'], 'L0_ffn_b1': _L0_ffn_in['b1'], 'L0_ffn_w2': _L0_ffn_in['w2'], 'L0_ffn_b2': _L0_ffn_in['b2']}

def reference(x, txt, L0_tok_W_main, L0_tok_b_main, L0_tok_W_sx, L0_tok_b_sx, L0_tok_W_sy, L0_tok_b_sy, L0_tok_ln_g, L0_tok_ln_b, L0_attn_Wqkv, L0_attn_bqkv, L0_attn_Wproj, L0_attn_bproj, L0_ffn_ln1_g, L0_ffn_ln1_b, L0_ffn_wq, L0_ffn_wk, L0_ffn_wv, L0_ffn_wo, L0_ffn_ln2_g, L0_ffn_ln2_b, L0_ffn_wr, L0_ffn_w1, L0_ffn_b1, L0_ffn_w2, L0_ffn_b2):
    import jax
    import jax.numpy as jnp

    def _L0_tok_ref(x, W_main, b_main, W_sx, b_sx, W_sy, b_sy, ln_g, ln_b):
        import jax, jax.numpy as jnp
        import numpy as np
        P = 16
        SHIFT = P // 2
        EPS = 1e-05

        def _shift2d(img, dy, dx):
            H, W = (img.shape[2], img.shape[3])
            pad = ((0, 0), (0, 0), (max(dy, 0), max(-dy, 0)), (max(dx, 0), max(-dx, 0)))
            z = jnp.pad(img, pad)
            return z[:, :, max(-dy, 0):max(-dy, 0) + H, max(-dx, 0):max(-dx, 0) + W]

        def _patchify(img):
            B, C, H, W = img.shape
            nH, nW = (H // P, W // P)
            t = img.reshape(B, C, nH, P, nW, P).transpose(0, 2, 4, 1, 3, 5)
            return t.reshape(B, nH * nW, C * P * P)

        def proj(img, W, b):
            return jnp.einsum('bnf,of->bno', _patchify(img), W) + b
        main = proj(x, W_main, b_main)
        xl = proj(_shift2d(x, 0, -SHIFT), W_sx, b_sx)
        xr = proj(_shift2d(x, 0, SHIFT), W_sx, b_sx)
        yu = proj(_shift2d(x, -SHIFT, 0), W_sy, b_sy)
        yd = proj(_shift2d(x, SHIFT, 0), W_sy, b_sy)
        tok = jnp.concatenate([main, xl, xr, yu, yd], axis=-1)
        mu = jnp.mean(tok, axis=-1, keepdims=True)
        var = jnp.mean(jnp.square(tok - mu), axis=-1, keepdims=True)
        return (tok - mu) * jax.lax.rsqrt(var + EPS) * ln_g + ln_b

    def _L0_attn_ref(x, Wqkv, bqkv, Wproj, bproj):
        import jax, jax.numpy as jnp
        import numpy as np
        B, N, C = (2, 1024, 128)
        NUM_HEADS = 8
        HEAD_DIM = C // NUM_HEADS
        SCALE = HEAD_DIM ** (-0.5)
        THETA = 10000.0

        def _rope(x, seq_len, head_dim):
            freqs = 1.0 / THETA ** (jnp.arange(0, head_dim, 2, dtype=jnp.float32) / head_dim)
            t = jnp.arange(seq_len, dtype=jnp.float32)
            freqs_cis = jnp.outer(t, freqs)
            sin_f = jnp.sin(freqs_cis)
            cos_f = jnp.cos(freqs_cis)
            x_even = x[..., ::2]
            x_odd = x[..., 1::2]
            rot = jnp.stack([x_even * cos_f - x_odd * sin_f, x_even * sin_f + x_odd * cos_f], axis=-1)
            return rot.reshape(x.shape)
        b, n, c = x.shape
        qkv = x @ Wqkv.T + bqkv
        qkv = qkv.reshape(b, n, 3, NUM_HEADS, HEAD_DIM)
        qkv = jnp.transpose(qkv, (2, 0, 3, 1, 4))
        q, k, v = (qkv[0], qkv[1], qkv[2])
        q = _rope(q, n, HEAD_DIM)
        k = _rope(k, n, HEAD_DIM)
        attn = jnp.einsum('bhqd,bhkd->bhqk', q, k) * SCALE
        attn = jax.nn.softmax(attn, axis=-1)
        out = jnp.einsum('bhqk,bhkd->bhqd', attn, v)
        out = jnp.transpose(out, (0, 2, 1, 3)).reshape(b, n, c)
        return out @ Wproj.T + bproj

    def _L0_ffn_ref(x, ln1_g, ln1_b, wq, wk, wv, wo, ln2_g, ln2_b, wr, w1, b1, w2, b2):
        import jax, jax.numpy as jnp
        import numpy as np
        EPS = 1e-05
        NUM_HEADS = 8
        TOP_K = 2
        CAP_FACTOR = 2

        def layernorm(x, g, b):
            m = jnp.mean(x, axis=-1, keepdims=True)
            v = jnp.var(x, axis=-1, keepdims=True)
            return (x - m) * jax.lax.rsqrt(v + EPS) * g + b
        B, S, H = x.shape
        NH = NUM_HEADS
        dh = H // NH
        x1 = layernorm(x, ln1_g, ln1_b)
        q = (x1 @ wq).reshape(B, S, NH, dh)
        k = (x1 @ wk).reshape(B, S, NH, dh)
        v = (x1 @ wv).reshape(B, S, NH, dh)
        scores = jnp.einsum('bqhd,bkhd->bhqk', q, k) * dh ** (-0.5)
        p = jax.nn.softmax(scores, axis=-1)
        attn_out = jnp.einsum('bhqk,bkhd->bqhd', p, v).reshape(B, S, H) @ wo
        x = x + attn_out
        x2 = layernorm(x, ln2_g, ln2_b).reshape(B * S, H)
        T = B * S
        E = wr.shape[1]
        C = CAP_FACTOR * (T * TOP_K // E)
        probs = jax.nn.softmax(x2 @ wr, axis=-1)
        gate_v, gate_i = jax.lax.top_k(probs, TOP_K)
        gate_v = gate_v / jnp.sum(gate_v, axis=-1, keepdims=True)
        ef = gate_i.reshape(-1)
        gf = gate_v.reshape(-1)
        oh = jax.nn.one_hot(ef, E, dtype=x2.dtype)
        pos = jnp.sum((jnp.cumsum(oh, axis=0) - oh) * oh, axis=1).astype(jnp.int32)
        keep = (pos < C).astype(x2.dtype)
        posc = jnp.minimum(pos, C - 1)
        tok = jnp.repeat(x2, TOP_K, axis=0) * keep[:, None]
        buf = jnp.zeros((E, C, H), x2.dtype).at[ef, posc].add(tok)
        h = jax.nn.gelu(jnp.einsum('ech,ehf->ecf', buf, w1) + b1[:, None, :])
        y = jnp.einsum('ecf,efh->ech', h, w2) + b2[:, None, :]
        ys = y[ef, posc] * (gf * keep)[:, None]
        moe_out = ys.reshape(T, TOP_K, H).sum(axis=1).reshape(B, S, H)
        return x + moe_out
    h = _L0_tok_ref(x, L0_tok_W_main, L0_tok_b_main, L0_tok_W_sx, L0_tok_b_sx, L0_tok_W_sy, L0_tok_b_sy, L0_tok_ln_g, L0_tok_ln_b)
    h = jnp.concatenate([h, txt], axis=1)
    h = h + _L0_attn_ref(_layernorm(h, axis=-1), L0_attn_Wqkv, L0_attn_bqkv, L0_attn_Wproj, L0_attn_bproj)
    h = h + _L0_ffn_ref(_layernorm(h, axis=-1), L0_ffn_ln1_g, L0_ffn_ln1_b, L0_ffn_wq, L0_ffn_wk, L0_ffn_wv, L0_ffn_wo, L0_ffn_ln2_g, L0_ffn_ln2_b, L0_ffn_wr, L0_ffn_w1, L0_ffn_b1, L0_ffn_w2, L0_ffn_b2)
    return h

_drawn_inputs = setup_inputs


def setup_inputs(seed=0):
    import zlib

    import numpy as np

    out = dict(_drawn_inputs(seed))
    spreads = {'L0_tok_b_main': (0.0, 0.1),
     'L0_tok_b_sx': (0.0, 0.1),
     'L0_tok_b_sy': (0.0, 0.1),
     'L0_tok_ln_g': (1.0, 0.2),
     'L0_tok_ln_b': (0.0, 0.1),
     'L0_ffn_ln1_g': (1.0, 0.6),
     'L0_ffn_ln1_b': (0.0, 0.8),
     'L0_ffn_ln2_g': (1.0, 0.6),
     'L0_ffn_ln2_b': (0.0, 1.157),
     'L0_ffn_b1': (0.0, 2.0),
     'L0_ffn_b2': (0.0, 0.8)}
    factors = {'L0_attn_Wqkv': 8.0,
     'L0_attn_bqkv': 8.0,
     'L0_attn_Wproj': 7.19,
     'L0_ffn_wq': 8.0,
     'L0_ffn_wk': 8.0,
     'L0_ffn_wv': 8.0,
     'L0_ffn_wo': 8.0,
     'L0_ffn_w1': 2.936}
    for name, (base, spread) in spreads.items():
        noise = np.random.default_rng([zlib.crc32(name.encode()), seed]).standard_normal(out[name].shape)
        drawn = base * np.exp(spread * noise) if base else spread * noise
        out[name] = jnp.asarray(drawn.astype(out[name].dtype))
    for name, factor in factors.items():
        out[name] = (out[name] * factor).astype(out[name].dtype)
    return out
```

```python
from contextlib import ExitStack

import concourse.bass as bass
from concourse import mybir

F32 = mybir.dt.float32
U32 = mybir.dt.uint32
BF16 = mybir.dt.bfloat16
ALU = mybir.AluOpType
ACT = mybir.ActivationFunctionType
AX = mybir.AxisListType

B = 64
NP = 6
IMG = 36
TXT = 128
N = IMG + TXT
H = 128
HALF = N // 2
NH = 8
HD = H // NH
E = 64
F = 512
FC = F // 128
CAP = 2 * (B * N * 2 // E)
SLOTS = E * CAP
ROW = H + 1
CHOICES = B * N * 2
SCALE = HD ** -0.5
EPS = 1e-5
GRP = 16
ROWS = GRP * NP
MAIN = CAP // 128
TAIL = CAP - MAIN * 128
BIG = 65536.0


def program(nc, x, txt, w_tok, b_tok, ln_g, ln_b, moves, ident_d, tri, rope, w_qk0, b_qk0, w_v0, b_v0,
            w_o0, w_qk1, one_row, w_v1, w_o1, g1, be1, g2, be2, w_r, w1, b1, w2, b2, out):
    with ExitStack() as ctx:
        def sb(name, shape, dt=F32):
            return ctx.enter_context(nc.sbuf_tensor(name, shape, dt))

        def sem(name):
            return ctx.enter_context(nc.semaphore(name))

        tokens = nc.dram_tensor("tokens", [B, IMG, H], F32).ap()
        slots_x = nc.dram_tensor("slots_x", [SLOTS, ROW], F32).ap()
        scratch = nc.dram_tensor("scratch", [8, E], F32).ap()
        choice_y = nc.dram_tensor("choice_y", [CHOICES, H], F32).ap()

        ps = ctx.enter_context(nc.psum_tensor("ps", [128, 8, 512], F32))

        ident = sb("ident", [128, 128])
        trif = sb("trif", [HALF, HALF])
        trib = sb("trib", [HALF, HALF], BF16)
        allb = sb("allb", [HALF, HALF], BF16)
        movem = sb("movem", [128, 4, 128])
        wtok = sb("wtok", [128, 6, 128])
        btok = sb("btok", [128, 1])
        lng = sb("lng", [2 * IMG, H])
        lnb = sb("lnb", [2 * IMG, H])
        ropet = sb("ropet", [128, 8, N])
        bqk0 = sb("bqk0", [128, 8])
        ropeb = sb("ropeb", [128, 4, N])
        wqk0 = sb("wqk0", [128, 8, 128])
        wv0 = sb("wv0", [128, 128])
        bv0 = sb("bv0", [HALF, H])
        wo0 = sb("wo0", [128, 2, H])
        wqk1 = sb("wqk1", [128, 4, 128])
        onerow = sb("onerow", [128, 1])
        wv1 = sb("wv1", [128, 128])
        wo1 = sb("wo1", [128, 2, H])
        g1c = sb("g1c", [128, 1])
        be1c = sb("be1c", [128, 1])
        g2r = sb("g2r", [HALF, H])
        be2r = sb("be2r", [HALF, H])
        wr = sb("wr", [128, E])
        iota = sb("iota", [HALF, E])
        mhalf = sb("mhalf", [128, 8])
        b1c = sb("b1c", [128, E, FC])

        def two(name, shape, dt=F32):
            return [sb(f"{name}{p}", shape, dt) for p in range(2)]

        hin = two("hin", [HALF, 2, H])
        h1 = two("h1", [HALF, 2, H])
        xin = two("xin", [HALF, 2, H])
        xm = two("xm", [HALF, 2, H])
        xh = two("xh", [HALF, 2, H])
        xh2 = two("xh2", [HALF, 2, H])
        x2 = two("x2", [HALF, 2, 2, ROW])
        ln = range(3)
        stat = [two(f"stat{l}", [HALF, 2, 6]) for l in ln]
        mv = [two(f"mv{l}", [HALF, 2, 2]) for l in ln]
        ve = [two(f"ve{l}", [HALF, 2, 2]) for l in ln]
        rs = [two(f"rs{l}", [HALF, 2, 2]) for l in ln]
        xhT = two("xhT", [128, N])
        x2T = two("x2T", [128, N])
        rt = two("rt", [128, 8, N])
        qk = two("qk", [128, 4, N])
        qkb = two("qkb", [128, 4, N], BF16)
        keys = two("keys", [128, 4, 2, N])
        qm = two("qm", [128, 2, N])
        mx = two("mx", [HALF, 2, NH * 32])
        va = two("va", [HALF, 2, NH, 32])
        big = two("big", [128, FC * CAP])
        pT = [b[0:HALF, :].rearrange("p (s h n) -> p s h n", s=2, h=NH) for b in big]
        hT = [b[:, :].rearrange("p (f c) -> p f c", f=FC) for b in big]
        dn = two("dn", [128, 2 * N])
        rc = two("rc", [128, 2 * N])
        oT = two("oT", [128, 2, N])
        lg = two("lg", [HALF, 2, E])
        v8 = two("v8", [HALF, 2, 8])
        i8 = two("i8", [HALF, 2, 8], U32)
        dif = two("dif", [HALF, 2])
        e2 = two("e2", [HALF, 2])
        ix = two("ix", [HALF, 2, 2])
        oh = two("oh", [HALF, 2, 2, E], BF16)
        ohs = two("ohs", [HALF, 2, E], BF16)
        before = two("before", [HALF, 2, E])
        taken = two("taken", [HALF, E])
        sel = two("sel", [HALF, 2, 2, E])
        pos = two("pos", [HALF, 2, 2])
        keep = two("keep", [HALF, 2, 2])
        mnp = two("mnp", [HALF, 2, 2])
        slf = two("slf", [HALF, 2, 2])
        scu = two("scu", [HALF, 2, 2], U32)
        off = two("off", [HALF, 2, 2])
        gt = two("gt", [HALF, 2, 2])

        store = sb("store", [128, 2 * B * H])
        resid = store[0:HALF, :].rearrange("p (t c) -> p t c", c=H)
        gate = sb("gate", [HALF, 2 * B * 2])

        with ExitStack() as early:
            def sa(name, shape):
                return early.enter_context(nc.sbuf_tensor(name, shape, F32))

            xs = [store[0:ROWS, i * 4608:(i + 1) * 4608].rearrange("p (c y w) -> p c y w", c=3, y=16) for i in range(2)]
            xr = store[0:ROWS, 2 * 4608:3 * 4608].rearrange("p (j f) -> p j f", j=NP)
            xT = [sa(f"xT{i}", [128, 2, 288]) for i in range(2)]
            tokT = sa("tokT", [128, 2, 288])
            gpad = sa("gpad", [128, GRP, 8, 8])
            tok = sa("tok", [2 * IMG, 8, H])
            tok2 = sa("tok2", [2 * IMG, 8, H])
            tstat = sa("tstat", [2 * IMG, 8, 6])
            tmv = sa("tmv", [2 * IMG, 8, 2])
            tve = sa("tve", [2 * IMG, 8])
            trs = sa("trs", [2 * IMG, 8])

        w1s = two("w1s", [128, F])
        w2s = two("w2s", [128, FC, H])
        b2s = two("b2s", [128, H])
        ex = two("ex", [128, MAIN, ROW])
        ext = two("ext", [TAIL, ROW])
        em = two("em", [128, MAIN + 1])
        eu = two("eu", [128, MAIN + 1], U32)
        eT = two("eT", [128, CAP])
        ey = [r[:, :, :].rearrange("p g n -> p (g n)")[:, 0:(MAIN + 1) * H].rearrange("p (c h) -> p c h", h=H) for r in rt]

        flat = [r[0:HALF, :, :].rearrange("p g n -> p (g n)") for r in rt]
        yl = [f[:, 0:4 * H].rearrange("p (t k c) -> p t k c", t=2, k=2) for f in flat]
        fin = [f[:, 4 * H:6 * H].rearrange("p (t c) -> p t c", t=2) for f in flat]
        tmpd = [f[:, 6 * H:8 * H].rearrange("p (t c) -> p t c", t=2) for f in flat]

        consts_in = sem("consts_in")
        xs_in = [sem(f"xs_in{i}") for i in range(2)]
        memset_done = sem("memset_done")
        iota_done = sem("iota_done")
        trib_ready = sem("trib_ready")
        ropeb_step = sem("ropeb_step")
        zero_ready = sem("zero_ready")
        zeros_out = sem("zeros_out")
        patch_rows = sem("patch_rows")
        patch_ps = sem("patch_ps")
        patch_sb = sem("patch_sb")
        emb_ps = sem("emb_ps")
        emb_sb = sem("emb_sb")
        tokT_ps = sem("tokT_ps")
        tokT_sb = sem("tokT_sb")
        tok_ps = sem("tok_ps")
        tok_sb = sem("tok_sb")
        tok_stat = sem("tok_stat")
        tok_mv = sem("tok_mv")
        tok_step = sem("tok_step")
        tok_rs = sem("tok_rs")
        tok_norm = sem("tok_norm")
        tok_ready = sem("tok_ready")
        tok_out = sem("tok_out")

        waits_passed = sem("waits_passed")

        def sems(name):
            return [sem(f"{name}{p}") for p in range(2)]

        hin_in = sems("hin_in")
        stat_done = [sems(f"stat_done_{l}") for l in ln]
        mv_ready = [sems(f"mv_ready_{l}") for l in ln]
        ve_ready = [sems(f"ve_ready_{l}") for l in ln]
        rs_ready = [sems(f"rs_ready_{l}") for l in ln]
        xh_ready = sems("xh_ready")
        xh2_ready = sems("xh2_ready")
        xT_ps = sems("xT_ps")
        xT_ready = sems("xT_ready")
        qkv_ps = sems("qkv_ps")
        rope_mul = sems("rope_mul")
        rope_sum = sems("rope_sum")
        qk_roped = sems("qk_roped")
        qk_copied = sems("qk_copied")
        qkb_ready = sems("qkb_ready")
        keys_ready = sems("keys_ready")
        v_ready0 = sems("v_ready0")
        v_ready1 = sems("v_ready1")
        sm_ps = sems("sm_ps")
        max_done = sems("max_done")
        mT_ps = sems("mT_ps")
        qm_ready = sems("qm_ready")
        st_ps = sems("st_ps")
        exp_done = sems("exp_done")
        o_ps = sems("o_ps")
        den_step = sems("den_step")
        oT_ready = sems("oT_ready")
        y_ps = sems("y_ps")
        h_ready = sems("h_ready")
        resid_ready = sems("resid_ready")
        x2_scaled = sems("x2_scaled")
        x2_ready = sems("x2_ready")
        x2T_ps = sems("x2T_ps")
        x2T_ready = sems("x2T_ready")
        lg_ps = sems("lg_ps")
        lg_ready = sems("lg_ready")
        top_step = sems("top_step")
        idx_ready = sems("idx_ready")
        ohs_ready = sems("ohs_ready")
        e2_ready = sems("e2_ready")
        cnt_ps = sems("cnt_ps")
        taken_ready = sem("taken_ready")
        cnt_read = sems("cnt_read")
        slot_step = sems("slot_step")
        scu_ready = sems("scu_ready")
        gate_step = sems("gate_step")
        gate_done = sems("gate_done")
        scat_out = sems("scat_out")

        w_in = sems("w_in")
        ex_in = sems("ex_in")
        eT_ps = sem("eT_ps")
        eT_ready = sem("eT_ready")
        h_ps = sem("h_ps")
        gelu_done = sem("gelu_done")
        ey_ps = sem("ey_ps")
        ey_ready = sem("ey_ready")
        em_ready = sem("em_ready")
        ey_out = sems("ey_out")

        yl_in = sems("yl_in")
        fin_step = sem("fin_step")
        fin_ready = sem("fin_ready")
        fin_out = sems("fin_out")

        consts = [
            (ident[:, :], ident_d), (trif[:, :], tri),
            (movem[:, :, :], moves.rearrange("s p n -> p s n")), (wtok[:, :, :], w_tok.rearrange("(k p) n -> p k n", p=128)),
            (btok[:, :], b_tok), (lng[:, :], ln_g.broadcast_to([2 * IMG, H])),
            (lnb[:, :], ln_b.broadcast_to([2 * IMG, H])), (ropet[:, :, :], rope), (bqk0[:, :], b_qk0),
            (wqk0[:, :, :], w_qk0), (wv0[:, :], w_v0), (bv0[:, :], b_v0.broadcast_to([HALF, H])), (wo0[:, :, :], w_o0),
            (wqk1[:, :, :], w_qk1), (onerow[:, :], one_row), (wv1[:, :], w_v1),
            (wo1[:, :, :], w_o1), (g1c[:, :], g1), (be1c[:, :], be1), (g2r[:, :], g2.broadcast_to([HALF, H])),
            (be2r[:, :], be2.broadcast_to([HALF, H])), (wr[:, :], w_r), (b1c[:, :, :], b1),
        ]
        CONSTS = 16 * len(consts)
        FILLS = -(-SLOTS * ROW // 128 // (FC * CAP)) - (-CHOICES * H // 128 // (FC * CAP))

        def c1(n):
            return n + 1

        def c2(n, a):
            return n * 2 + (a + 1)

        def c4(n, a, s):
            return n * 4 + (2 * a + s + 1)

        def c8(n, a, s, half):
            return n * 8 + (4 * a + 2 * s + half + 1)

        def n2(it, p):
            return it * 2 + (p + 1)

        def settled(eng):
            eng.sem_inc(waits_passed, 1)

        R = [ps[:, 4 * p:4 * p + 4, :] for p in range(2)]

        def bank(p, b, rows, c0, c1):
            return ps[0:rows, 4 * p + b, c0:c1]

        def schedule(eng, half, tail):
            last = B // 2 - 1

            def pair(n, more=True):
                half((1, 0, n), (0, 0, n))
                half((0, 1, n), (1, 0, n))
                half((1, 1, n), (0, 1, n))
                half((0, 0, n + 1), (1, 1, n), more)

            half((0, 0, 0), None)
            pair(0)
            with eng.Fori(1, last) as n:
                pair(n)
            pair(last, False)
            tail(last)

        def first(n):
            return isinstance(n, int) and n == 0

        block = ctx.enter_context(nc.Block())

        @block.sync
        def _(sp):
            for s in fin_out:
                sp.sem_inc(s, 16)
            for dst, src in consts:
                sp.dma_start(dst, src).then_inc(consts_in, 16)

            with sp.Fori(0, 2) as it:
                for i in range(2):
                    sp.wait_ge(patch_rows, it * 2 + 1)
                    for b in range(GRP):
                        sp.dma_start(xs[i][b * NP:(b + 1) * NP, :, :, :],
                                     x[bass.ds((it * 2 + i) * GRP + b, 1)].rearrange("b c (i y) w -> (b i) c y w", y=16)
                                     ).then_inc(xs_in[i], 16)
            sp.wait_ge(tok_out, 16 * 4 + 16)

            def load_image(p, image):
                sp.dma_start(hin[p][0:IMG, 0, :], tokens[image, :, :].rearrange("o n c -> (o n) c")).then_inc(hin_in[p], 16)
                sp.dma_start(hin[p][IMG:HALF, 0, :], txt[image, 0:HALF - IMG, :].rearrange("o n c -> (o n) c")
                             ).then_inc(hin_in[p], 16)
                sp.dma_start(hin[p][:, 1, :], txt[image, HALF - IMG:TXT, :].rearrange("o n c -> (o n) c")
                             ).then_inc(hin_in[p], 16)

            for p in range(2):
                load_image(p, bass.ds(p, 1))
            with sp.Fori(0, B // 2 - 1) as n:
                for p in range(2):
                    sp.wait_ge(h_ready[p], c2(n, 0))
                    load_image(p, bass.ds(n * 2 + (2 + p), 1))

            for p in range(2):
                sp.wait_ge(scat_out[p], 64 * (B // 2))

            def load_expert(p, e):
                sp.dma_start(w1s[p][:, :], w1[e, :, :].rearrange("o h f -> (o h) f")).then_inc(w_in[p], 16)
                sp.dma_start(w2s[p][:, :, :], w2[e, :, :].rearrange("o (q c) h -> (o q) c h", c=FC)).then_inc(w_in[p], 16)
                sp.dma_start(b2s[p][:, :], b2[e, :].broadcast_to([128, H])).then_inc(w_in[p], 16)
                rows = slots_x.rearrange("(e s) h -> e s h", s=CAP)[e, :, :]
                sp.dma_start(ex[p][:, :, :], rows[:, 0:MAIN * 128, :].rearrange("o (q c) h -> (o q) c h", c=MAIN)
                             ).then_inc(ex_in[p], 16)
                sp.dma_start(ext[p][:, :], rows[:, MAIN * 128:CAP, :].rearrange("o q h -> (o q) h")).then_inc(ex_in[p], 16)

            for p in range(2):
                load_expert(p, bass.ds(p, 1))
            with sp.Fori(0, E // 2 - 1) as it:
                for p in range(2):
                    sp.wait_ge(ey_ready, it * 2 + (p + 2))
                    load_expert(p, bass.ds(it * 2 + (2 + p), 1))

            with sp.Fori(0, B // 2) as it:
                for p in range(2):
                    sp.wait_ge(fin_ready, n2(it, p) + 1)
                    o = out[bass.ds(it * 2 + p, 1), :, :].rearrange("o (t q) c -> (o q) t c", t=2)
                    sp.dma_start(o, fin[p][:, :, :]).then_inc(fin_out[p], 16)
            for p in range(2):
                sp.wait_ge(fin_out[p], 16 * (B // 2) + 16)

        @block.tensor
        def _(pe):
            for s in (tokT_ps, tok_ps, patch_ps, emb_ps,):
                pe.sem_inc(s, 1)
            pe.wait_ge(consts_in, CONSTS)
            with pe.Fori(0, 2) as it:
                for i in range(2):
                    pe.wait_ge(patch_rows, it * 2 + (i + 1) + 1)
                    for k in range(6):
                        pe.wait_ge(patch_sb, it * 12 + (6 * i + k) + 1)
                        for j in range(NP):
                            ins = pe.transpose(ps[:, j // 3, (j % 3) * ROWS:(j % 3 + 1) * ROWS],
                                               xr[:, j, k * 128:(k + 1) * 128],
                                               ident[0:ROWS, 0:ROWS])
                        ins.then_inc(patch_ps, 1)
                        pe.wait_ge(patch_sb, it * 12 + (6 * i + k + 1) + 1)
                        for g in range(2):
                            if k == 0 and g == 0:
                                pe.wait_ge(emb_sb, it * 2 + i + 1)
                            ins = pe.matmul(ps[:, 2 + g, 0:288], wtok[:, k, :], xT[k % 2][:, g, :],
                                            start=(k == 0), stop=(k == 5))
                    ins.then_inc(emb_ps, 1)
                    pe.wait_ge(emb_sb, it * 2 + (i + 1) + 1)
                    pe.wait_ge(tokT_sb, it * 2 + i + 1)
                    for g in range(2):
                        for s, (di, dj) in enumerate([(0, 0), (0, 1), (0, -1), (1, 0), (-1, 0)]):
                            ins = pe.matmul(ps[:, 4 + g, 0:288], ident[:, :] if s == 0 else movem[:, s - 1, :],
                                            gpad[:, 8 * g:8 * g + 8, 1 + di:7 + di, 1 + dj:7 + dj],
                                            start=(s == 0), stop=(s == 4))
                    ins.then_inc(tokT_ps, 1)
                    pe.wait_ge(tokT_sb, it * 2 + (i + 1) + 1)
                    pe.wait_ge(tok_sb, it * 2 + i + 1)
                    for q in range(GRP // 2):
                        ins = pe.transpose(ps[0:2 * IMG, 6 + q // 4, (q % 4) * 128:(q % 4 + 1) * 128],
                                           tokT[:, q // 4, (q % 4) * 72:(q % 4 + 1) * 72], ident[:, :])
                    ins.then_inc(tok_ps, 1)

            pe.wait_ge(memset_done, 1)
            pe.wait_ge(trib_ready, 1)
            pe.wait_ge(tok_sb, 4 + 1)

            def turn(p, b, src, done):
                for t in range(2):
                    ins = pe.transpose(bank(p, b, 128, HALF * t, HALF * (t + 1)), src[:, t], ident[0:HALF, 0:HALF])
                ins.then_inc(done, 1)

            def scores(p, a, n, s, half, groups=(0, 1)):
                if 0 not in groups:
                    pass
                elif s == 0:
                    pe.wait_ge(keys_ready[p], c2(n, a))
                    pe.wait_ge(qm_ready[p], c2(n, a))
                    if a == 0 and half == 0 and not first(n):
                        pe.wait_ge(x2T_ready[p], c1(n - 1))
                else:
                    pe.wait_ge(exp_done[p], c8(n, a, 0, half))
                for g in groups:
                    for j in (2 * half, 2 * half + 1):
                        ins = pe.matmul(bank(p, j, HALF, g * N, (g + 1) * N), keys[p][:, j, g, s * HALF:(s + 1) * HALF],
                                        qm[p][:, g, :], start=True, stop=True)
                if 1 in groups:
                    ins.then_inc(st_ps[p], 1)

            def project(p, a, n):
                pe.wait_ge(xT_ready[p], c2(n, a))
                if a == 0:
                    if not first(n):
                        pe.wait_ge(h_ready[p], c2(n - 1, 1))
                    for g in range(8):
                        pe.matmul(bank(p, g // 2, 128, (g % 2) * N, (g % 2 + 1) * N), wqk0[:, g, :],
                                  xhT[p][:, :], start=True, stop=True)
                else:
                    if not first(n):
                        pe.wait_ge(cnt_read[p], c1(n - 1))
                    for g in range(4):
                        pe.matmul(bank(p, g // 2, 128, (g % 2) * N, (g % 2 + 1) * N), wqk1[:, g, :],
                                  xhT[p][:, :], start=True, stop=True)
                for t in range(2):
                    ins = pe.matmul(bank(p, t, HALF, 2 * N, 2 * N + H), xhT[p][:, t * HALF:(t + 1) * HALF],
                                    (wv0 if a == 0 else wv1)[:, :], start=True, stop=True)
                ins.then_inc(qkv_ps[p], 1)

            def max_scores(p, a, n, s, half):
                if s == 1:
                    pe.wait_ge(max_done[p], c8(n, a, 0, half))
                elif half == 0:
                    pe.wait_ge(qkb_ready[p], c2(n, a))
                    pe.wait_ge((v_ready0, v_ready1)[a][p], c1(n))
                for g in range(2):
                    for j in (2 * half, 2 * half + 1):
                        r = 32 * j
                        ins = pe.matmul(bank(p, j, HALF, g * N, (g + 1) * N),
                                        qkb[p][r:r + HD, g, s * HALF:(s + 1) * HALF],
                                        qkb[p][r:r + HD, 2 + g, :], start=True, stop=True)
                ins.then_inc(sm_ps[p], 1)

            def max_turn(p, a, n):
                pe.wait_ge(max_done[p], c8(n, a, 1, 1))
                for g in range(2):
                    for s in range(2):
                        ins = pe.transpose(bank(p, 0, 128, g * N + s * HALF, g * N + (s + 1) * HALF),
                                           mx[p][:, s, g * 128:(g + 1) * 128], ident[0:HALF, 0:HALF])
                ins.then_inc(mT_ps[p], 1)

            def weighted(p, a, n, part):
                heads = ((0, 4, 1, 5), (2, 6), (3, 7))[part]
                if part < 2:
                    pe.wait_ge(exp_done[p], c8(n, a, 1, part))
                for h in heads:
                    j, g = h % 4, h // 4
                    for s in range(2):
                        ins = pe.matmul(ps[32 * j:32 * j + 32, 4 * p, g * N:(g + 1) * N], va[p][:, s, h, :],
                                        pT[p][:, s, 2 * j + g, :], start=(s == 0), stop=(s == 1))
                if part == 2:
                    ins.then_inc(o_ps[p], 1)

            def out_project(p, a, n):
                pe.wait_ge(oT_ready[p], c2(n, a))
                for t in range(2):
                    for g in range(2):
                        ins = pe.matmul(bank(p, 2, HALF, t * H, (t + 1) * H), oT[p][:, g, t * HALF:(t + 1) * HALF],
                                        (wo0 if a == 0 else wo1)[:, g, :], start=(g == 0), stop=(g == 1))
                ins.then_inc(y_ps[p], 1)

            def logits(p, n):
                pe.wait_ge(x2T_ready[p], c1(n))
                for t in range(2):
                    ins = pe.matmul(bank(p, 1, HALF, t * E, (t + 1) * E), x2T[p][:, t * HALF:(t + 1) * HALF],
                                    wr[:, :], start=True, stop=True)
                ins.then_inc(lg_ps[p], 1)

            def counts(p, n):
                pe.wait_ge(ohs_ready[p], c1(n))
                o0, o1 = ohs[p][:, 0, :], ohs[p][:, 1, :]
                pe.matmul(bank(p, 1, HALF, 0, E), trib[:, :], o0, start=True, stop=True)
                pe.matmul(bank(p, 1, HALF, E, 2 * E), allb[:, :], o0, start=True, stop=False)
                pe.matmul(bank(p, 1, HALF, E, 2 * E), trib[:, :], o1, start=False, stop=True)
                pe.matmul(bank(p, 1, HALF, 2 * E, 3 * E), allb[:, :], o0, start=True, stop=False)
                pe.matmul(bank(p, 1, HALF, 2 * E, 3 * E), allb[:, :], o1, start=False, stop=True).then_inc(cnt_ps[p], 1)

            def half(light, heavy, more=True):
                lp, la, lnum = light
                if heavy:
                    hp, ha, hn = heavy
                    scores(hp, ha, hn, 0, 0)
                if la == 1:
                    out_project(lp, 0, lnum)
                elif not first(lnum):
                    out_project(lp, 1, lnum - 1)
                if heavy:
                    scores(hp, ha, hn, 0, 1)
                    scores(hp, ha, hn, 1, 0)
                if la == 1 and not first(lnum):
                    counts(lp, lnum - 1)
                if more:
                    pe.wait_ge(xh_ready[lp], c2(lnum, la))
                    turn(lp, 0, xh[lp], xT_ps[lp])
                if heavy:
                    scores(hp, ha, hn, 1, 1, (0,))
                if more:
                    project(lp, la, lnum)
                if heavy:
                    scores(hp, ha, hn, 1, 1, (1,))
                    weighted(hp, ha, hn, 0)
                if more:
                    for b in range(2):
                        max_scores(lp, la, lnum, 0, b)
                if heavy:
                    weighted(hp, ha, hn, 1)
                if more:
                    for b in range(2):
                        max_scores(lp, la, lnum, 1, b)
                if heavy:
                    weighted(hp, ha, hn, 2)
                if more:
                    max_turn(lp, la, lnum)
                if heavy and ha == 0 and not first(hn):
                    logits(hp, hn - 1)
                if la == 0 and not first(lnum):
                    pe.wait_ge(x2_ready[lp], c1(lnum - 1))
                    turn(lp, 1, x2[lp][:, :, 0, 0:H], x2T_ps[lp])

            def tail(n):
                out_project(1, 1, n)
                pe.wait_ge(x2_ready[1], c1(n))
                turn(1, 1, x2[1][:, :, 0, 0:H], x2T_ps[1])
                for p in range(2):
                    logits(p, n)
                for p in range(2):
                    pe.wait_ge(lg_ready[p], c1(n))
                    counts(p, n)

            schedule(pe, half, tail)

            with pe.Fori(0, E // 2) as it:
                for p in range(2):
                    pe.wait_ge(ex_in[p], it * 32 + 32)
                    if p == 1:
                        pe.wait_ge(eT_ready, it * 2 + 1 + 1)
                    else:
                        pe.wait_ge(eT_ready, it * 2 + 1)
                    for c in range(MAIN):
                        pe.transpose(ps[:, c // 4, (c % 4) * 128:(c % 4 + 1) * 128], ex[p][:, c, 0:H], ident[:, :])
                    pe.transpose(ps[:, 1, 128:128 + TAIL], ext[p][:, 0:H], ident[0:TAIL, 0:TAIL]).then_inc(eT_ps, 1)
                    pe.wait_ge(eT_ready, n2(it, p) + 1)
                    pe.wait_ge(w_in[p], it * 48 + 48)
                    for f in range(FC):
                        hp = 2 + 2 * (f % 2)
                        if f >= 2 or p == 1:
                            pe.wait_ge(gelu_done, it * 8 + (4 * p + f - 1) + 1)
                        else:
                            pe.wait_ge(gelu_done, it * 8 + f - 1 + 1) if f == 1 else None
                            if f == 0:
                                pe.wait_ge(ey_ready, it * 2 + 1)
                        for g in range(2):
                            ins = pe.matmul(ps[:, hp + g, 0:CAP // 2], w1s[p][:, f:F:FC], eT[p][:, g * (CAP // 2):(g + 1) * (CAP // 2)],
                                            start=True, stop=True)
                        ins.then_inc(h_ps, 1)
                    pe.wait_ge(gelu_done, it * 8 + (4 * p + 4) + 1)
                    pe.wait_ge(ey_ready, it * 2 + p + 1)
                    for c in range(MAIN + 1):
                        m = 128 if c < MAIN else TAIL
                        for f in range(FC):
                            ins = pe.matmul(ps[0:m, 6 + c // 4, (c % 4) * 128:(c % 4 + 1) * 128],
                                            hT[p][:, f, c * 128:c * 128 + m], w2s[p][:, f, :],
                                            start=(f == 0), stop=(f == FC - 1))
                    ins.then_inc(ey_ps, 1)

        @block.scalar
        def _(act):
            for s in (emb_sb, tokT_sb, gelu_done,):
                act.sem_inc(s, 1)
            act.wait_ge(zero_ready, 1)
            zeros = hT[0][:, :, :].rearrange("p f c -> p (f c)")
            width = FC * CAP
            fills = 0
            for rows in (slots_x, choice_y):
                flat = rows.rearrange("(q r) h -> q (r h)", q=128)
                for c in range(0, flat.shape[1], width):
                    m = min(width, flat.shape[1] - c)
                    act.dma_start(flat[:, c:c + m], zeros[:, 0:m]).then_inc(zeros_out, 16)
                    fills += 1
            act.wait_ge(consts_in, CONSTS)
            with act.Fori(0, 2) as it:
                for i in range(2):
                    act.wait_ge(emb_ps, it * 2 + (i + 1) + 1)
                    act.wait_ge(memset_done, 1)
                    act.wait_ge(tokT_ps, it * 2 + i + 1)
                    for j in range(NP):
                        ins = act.activation(gpad[:, :, 1:7, 1 + j],
                                             ps[:, 2 + j // 3, (j % 3) * ROWS:(j % 3 + 1) * ROWS].rearrange("p (b i) -> p b i", i=NP),
                                             ACT.Identity)
                    ins.then_inc(emb_sb, 1)
                    act.wait_ge(tokT_ps, it * 2 + (i + 1) + 1)
                    act.wait_ge(tok_ps, it * 2 + i + 1)
                    act.activation(tokT[:, :, :], ps[:, 4:6, 0:288], ACT.Identity, bias=btok[:, 0:1]).then_inc(tokT_sb, 1)
            act.wait_ge(zeros_out, 16 * fills)

            def exponentials(p, a, n, s, half):
                act.wait_ge(st_ps[p], c8(n, a, s, half))
                act.activation(pT[p][:, s, 4 * half:4 * half + 4, :].rearrange("p (b g) n -> p b (g n)", b=2),
                               R[p][0:HALF, 2 * half:2 * half + 2, 0:2 * N], ACT.Exp, scale=SCALE).then_inc(exp_done[p], 1)

            def copy_turned(p, a, n):
                act.wait_ge(xT_ps[p], c2(n, a))
                if a == 0:
                    act.activation(xhT[p][:, :], bank(p, 0, 128, 0, N), ACT.Identity).then_inc(xT_ready[p], 1)
                else:
                    act.activation(xhT[p][:, :], bank(p, 0, 128, 0, N), ACT.Identity, bias=be1c[:, 0:1],
                                   scale=g1c[:, 0:1]).then_inc(xT_ready[p], 1)

            def spread_keys(p, a, n):
                for j in range(4):
                    ins = act.activation(keys[p][32 * j:32 * j + 32, j, :, :], qk[p][32 * j:32 * j + 32, 2:4, :], ACT.Identity)
                ins.then_inc(keys_ready[p], 1)

            def half(light, heavy, more=True):
                lp, la, lnum = light
                if heavy:
                    hp, ha, hn = heavy
                    exponentials(hp, ha, hn, 0, 0)
                    exponentials(hp, ha, hn, 0, 1)
                    exponentials(hp, ha, hn, 1, 0)
                if more:
                    copy_turned(lp, la, lnum)
                if heavy and la == 0:
                    exponentials(hp, ha, hn, 1, 1)
                if la == 1:
                    act.wait_ge(qkv_ps[lp], c2(lnum, 1))
                    act.activation(qk[lp][:, 0:2, :], bank(lp, 0, 128, 0, 2 * N), ACT.Identity).then_inc(qk_copied[lp], 1)
                    act.activation(qk[lp][:, 2:4, :], bank(lp, 1, 128, 0, 2 * N), ACT.Identity, bias=onerow[:, 0:1]
                                   ).then_inc(qk_copied[lp], 1)
                    act.activation(va[lp][:, :, :, 0:HD],
                                   ps[0:HALF, 4 * lp:4 * lp + 2, 2 * N:2 * N + H].rearrange("p t (h d) -> p t h d", d=HD),
                                   ACT.Identity).then_inc(v_ready1[lp], 1)
                    if heavy:
                        exponentials(hp, ha, hn, 1, 1)
                    act.wait_ge(qk_copied[lp], lnum * 2 + 2)
                    spread_keys(lp, 1, lnum)
                elif more:
                    act.wait_ge(qk_roped[lp], c1(lnum))
                    spread_keys(lp, 0, lnum)
                if heavy and ha == 0 and not first(hn):
                    act.wait_ge(lg_ps[hp], c1(hn - 1))
                    act.activation(lg[hp][:, :, :], bank(hp, 1, HALF, 0, 2 * E).rearrange("p (t e) -> p t e", t=2),
                                   ACT.Identity).then_inc(lg_ready[hp], 1)
                if la == 0 and not first(lnum):
                    act.wait_ge(x2T_ps[lp], c1(lnum - 1))
                    act.activation(x2T[lp][:, :], bank(lp, 1, 128, 0, N), ACT.Identity).then_inc(x2T_ready[lp], 1)
                if heavy and ha == 0 and not first(hn):
                    act.wait_ge(idx_ready[hp], c1(hn - 1))
                    act.activation(e2[hp][:, :], dif[hp][:, :], ACT.Exp).then_inc(e2_ready[hp], 1)

            def tail(n):
                act.wait_ge(x2T_ps[1], c1(n))
                act.activation(x2T[1][:, :], bank(1, 1, 128, 0, N), ACT.Identity).then_inc(x2T_ready[1], 1)
                for p in range(2):
                    act.wait_ge(lg_ps[p], c1(n))
                    act.activation(lg[p][:, :, :], bank(p, 1, HALF, 0, 2 * E).rearrange("p (t e) -> p t e", t=2),
                                   ACT.Identity).then_inc(lg_ready[p], 1)
                for p in range(2):
                    act.wait_ge(idx_ready[p], c1(n))
                    act.activation(e2[p][:, :], dif[p][:, :], ACT.Exp).then_inc(e2_ready[p], 1)

            schedule(act, half, tail)

            with act.Fori(0, E // 2) as it:
                for p in range(2):
                    for f in range(FC):
                        act.wait_ge(h_ps, it * 8 + (4 * p + f + 1))
                        act.activation(hT[p][:, f, :].rearrange("p (g n) -> p g n", g=2),
                                       ps[:, 2 + 2 * (f % 2):4 + 2 * (f % 2), 0:CAP // 2], ACT.Gelu_apprx_tanh,
                                       bias=b1c[:, bass.ds(it * 2 + p, 1), f]).then_inc(gelu_done, 1)
            for p in range(2):
                act.wait_ge(ey_out[p], 96 * (E // 2) + 16)
            with act.Fori(0, B // 2) as it:
                for p in range(2):
                    act.wait_ge(fin_ready, it * 2 + 1)
                    act.dma_start(yl[p][:, :, :, :], choice_y.rearrange("(b t q k) c -> b q t k c", t=2, q=HALF, k=2)[
                        bass.ds(it * 2 + p, 1)].rearrange("b q t k c -> (b q) t k c")).then_inc(yl_in[p], 16)

        @block.gpsimd
        def _(pool):
            pool.memset(mhalf[:, :], -0.5)
            pool.iota(iota[:, :], [[1, E]], base=0, channel_multiplier=0, allow_small_or_imprecise_dtypes=True
                      ).then_inc(iota_done, 1)
            pool.wait_ge(iota_done, 1)
            settled(pool)
            for n, s in enumerate([tok_out, *ey_out]):
                pool.dma_start(scratch[n:n + 1, :], iota[0:1, :]).then_inc(s, 16)
            with pool.Fori(0, 4) as it:
                pool.wait_ge(tok_mv, it + 1)
                settled(pool)
                pool.tensor_scalar(tve[:, :], tmv[:, :, 1], EPS, None, ALU.add).then_inc(tok_step, 1)
                pool.wait_ge(tok_step, it * 2 + 1)
                pool.tensor_tensor(trs[:, :], tve[:, :], mhalf[0:2 * IMG, 0:8], ALU.pow).then_inc(tok_rs, 1)
                pool.wait_ge(tok_norm, it + 1)
                settled(pool)
                g = lng[:, None, :].broadcast_to([2 * IMG, 8, H])
                b = lnb[:, None, :].broadcast_to([2 * IMG, 8, H])
                pool.tensor_tensor(tok2[:, :, :], tok[:, :, :], g, ALU.mult).then_inc(tok_step, 1)
                pool.wait_ge(tok_step, it * 2 + 2)
                pool.tensor_tensor(tok[:, :, :], tok2[:, :, :], b, ALU.add).then_inc(tok_ready, 1)
                pool.wait_ge(tok_ready, it + 1)
                settled(pool)
                pool.dma_start(tokens[bass.ds(it * GRP, GRP), :, :].rearrange("(q b) n c -> (b n) q c", b=2),
                               tok[:, :, :]).then_inc(tok_out, 16)
                pool.wait_ge(tok_out, it * 16 + 32)
            pool.wait_ge(zeros_out, 16 * FILLS)
            settled(pool)

            def deviations(l, p, n):
                pool.wait_ge(mv_ready[l][p], c1(n))
                settled(pool)
                if l == 1:
                    pool.tensor_scalar(ve[l][p][:, :, 1], mv[l][p][:, :, 1], 1.0 + EPS, EPS * EPS, ALU.mult, ALU.add)
                w = 1 + (l == 1)
                pool.tensor_scalar(ve[l][p][:, :, 0], mv[l][p][:, :, 1], EPS, None, ALU.add).then_inc(ve_ready[l][p], 1)
                pool.wait_ge(ve_ready[l][p], c1(n))
                pool.tensor_tensor(rs[l][p][:, :, 0:w], ve[l][p][:, :, 0:w],
                                   mhalf[0:HALF, 0:4].rearrange("p (a b) -> p a b", a=2)[:, :, 0:w], ALU.pow
                                   ).then_inc(rs_ready[l][p], 1)

            def expert_rows(p, n):
                pool.wait_ge(h_ready[p], c2(n, 1))
                pool.tensor_tensor(resid[:, bass.ds(n * 4 + 2 * p, 2), :], h1[p][:, :, :], xm[p][:, :, :], ALU.add
                                   ).then_inc(resid_ready[p], 1)
                deviations(2, p, n)
                pool.wait_ge(xh2_ready[p], c1(n))
                pool.tensor_tensor(xh2[p][:, :, :], xh2[p][:, :, :], g2r[:, None, :].broadcast_to([HALF, 2, H]),
                                   ALU.mult).then_inc(x2_scaled[p], 1)
                if not first(n):
                    pool.wait_ge(scat_out[p], n * 64)
                    settled(pool)
                pool.tensor_scalar(x2[p][:, :, :, H], x2[p][:, :, :, H], float(4 * N), None, ALU.add)
                pool.wait_ge(x2_scaled[p], c1(n))
                pool.tensor_tensor(x2[p][:, :, :, 0:H], xh2[p][:, :, None, :].broadcast_to([HALF, 2, 2, H]),
                                   be2r[:, None, None, :].broadcast_to([HALF, 2, 2, H]), ALU.add).then_inc(x2_ready[p], 1)

            def scatter(p, n):
                pool.wait_ge(scu_ready[p], c1(n))
                settled(pool)
                for t in range(2):
                    for k in range(2):
                        pool.indirect_dma_start(slots_x[:, :], bass.IndirectOffsetOnAxis(ap=scu[p][:, t, k:k + 1], axis=0),
                                                x2[p][:, t, k, :], None, bounds_check=SLOTS - 1, oob_is_err=False
                                                ).then_inc(scat_out[p], 16)

            def half(light, heavy, more=True):
                lp, la, lnum = light
                if la == 1:
                    deviations(1, lp, lnum)
                elif more:
                    pool.wait_ge(rope_sum[lp], c1(lnum))
                    pool.tensor_tensor(qk[lp][:, :, :], rt[lp][:, 0:4, :], ropeb[:, :, :], ALU.add).then_inc(qk_roped[lp], 1)
                if la == 0 and not first(lnum):
                    expert_rows(lp, lnum - 1)
                if heavy and heavy[1] == 1 and not (isinstance(heavy[2], int) and heavy[2] == B // 2 - 1):
                    deviations(0, heavy[0], heavy[2] + 1)
                if la == 1 and not first(lnum):
                    scatter(lp, lnum - 1)

            def tail(n):
                expert_rows(1, n)
                for p in range(2):
                    scatter(p, n)

            for p in range(2):
                pool.iota(x2[p][:, :, :, H], [[2 * HALF, 2], [1, 2]], base=2 * N * p + 1 - 4 * N, channel_multiplier=2,
                          allow_small_or_imprecise_dtypes=True).then_inc(iota_done, 1)
            pool.wait_ge(iota_done, 3)
            for p in range(2):
                deviations(0, p, 0)
            schedule(pool, half, tail)

            with pool.Fori(0, E // 2) as it:
                for p in range(2):
                    pool.wait_ge(ey_ready, n2(it, p) + 1)
                    settled(pool)
                    for c in range(MAIN + 1):
                        m = 128 if c < MAIN else TAIL
                        pool.indirect_dma_start(choice_y[:, :], bass.IndirectOffsetOnAxis(ap=eu[p][0:m, c:c + 1], axis=0),
                                                ey[p][0:m, c, :], None, bounds_check=CHOICES - 1, oob_is_err=False
                                                ).then_inc(ey_out[p], 16)

        @block.vector
        def _(dve):
            for s in (patch_sb, tok_sb, patch_rows, eT_ready, ey_ready, fin_ready,):
                dve.sem_inc(s, 1)
            dve.memset(hT[0][:, :, :], 0.0).then_inc(zero_ready, 1)
            dve.memset(gpad[:, :, :, :], 0.0)
            dve.memset(allb[:, :], 1.0)
            dve.memset(taken[0][:, :], 0.0).then_inc(taken_ready, 1)
            for p in range(2):
                dve.memset(keys[p][:, :, :, :], 0.0)
                dve.memset(mx[p][:, :, :], 0.0)
                dve.memset(va[p][:, :, :, HD:32], 1.0)
            dve.memset(dif[0][:, :], 0.0).then_inc(memset_done, 1)
            dve.wait_ge(consts_in, CONSTS)
            dve.tensor_copy(trib[:, :], trif[:, :]).then_inc(trib_ready, 1)
            for g in range(4):
                dve.tensor_scalar(ropeb[:, g, :], ropet[:, g, :], bqk0[:, g:g + 1], None, ALU.mult)
                dve.tensor_scalar(rt[0][:, g, :], ropet[:, 4 + g, :], bqk0[:, 4 + g:5 + g], onerow[:, 0:1] if g >= 2 else 0.0,
                                  ALU.mult, ALU.add).then_inc(ropeb_step, 1)
            dve.wait_ge(ropeb_step, 4)
            dve.tensor_tensor(ropeb[:, :, :], ropeb[:, :, :], rt[0][:, 0:4, :], ALU.add).then_inc(ropeb_step, 1)

            with dve.Fori(0, 2) as it:
                for i in range(2):
                    dve.wait_ge(xs_in[i], it * (16 * GRP) + 16 * GRP)
                    dve.wait_ge(patch_ps, it * 12 + 6 * i + 1)
                    for j in range(NP):
                        ins = dve.tensor_copy(xr[:, j, :].rearrange("p (c w) -> p c w", w=16),
                                              xs[i][:, :, :, 16 * j:16 * j + 16].rearrange("p c y w -> p (c y) w"))
                    ins.then_inc(patch_rows, 1)
                    for k in range(6):
                        dve.wait_ge(patch_ps, it * 12 + (6 * i + k + 1) + 1)
                        if k < 2:
                            dve.wait_ge(emb_ps, it * 2 + i + 1)
                        dve.tensor_copy(xT[k % 2][:, :, :], ps[:, 0:2, 0:288]).then_inc(patch_sb, 1)
                    dve.wait_ge(tok_ps, it * 2 + (i + 1) + 1)
                    dve.wait_ge(tok_out, it * 32 + (16 * i + 16))
                    dve.tensor_copy(tok[:, :, :].rearrange("p (g q) c -> p g (q c)", g=2), ps[0:2 * IMG, 6:8, :]
                                    ).then_inc(tok_sb, 1)
                    dve.wait_ge(tok_sb, it * 2 + (i + 1) + 1)
                    for q in range(8):
                        ins = dve.bn_stats(tstat[:, q, :], tok[:, q, :])
                    ins.then_inc(tok_stat, 1)
                    dve.wait_ge(tok_stat, it * 2 + (i + 1))
                    settled(dve)
                    for q in range(8):
                        ins = dve.bn_aggr(tmv[:, q, :], tstat[:, q, :])
                    ins.then_inc(tok_mv, 1)
                    dve.wait_ge(tok_rs, it * 2 + (i + 1))
                    for q in range(8):
                        ins = dve.tensor_scalar(tok[:, q, :], tok[:, q, :], tmv[:, q, 0:1], trs[:, q:q + 1],
                                                ALU.subtract, ALU.mult)
                    ins.then_inc(tok_norm, 1)

            dve.wait_ge(iota_done, 1)

            def statistics(l, p, n, src):
                for t in range(2):
                    ins = dve.bn_stats(stat[l][p][:, t, :], src[p][:, t, :])
                ins.then_inc(stat_done[l][p], 1)
                dve.wait_ge(stat_done[l][p], c1(n))
                settled(dve)
                for t in range(2):
                    ins = dve.bn_aggr(mv[l][p][:, t, :], stat[l][p][:, t, :])
                ins.then_inc(mv_ready[l][p], 1)

            def normalize(l, p, n, src, c, out, done):
                dve.wait_ge(rs_ready[l][p], c1(n))
                for t in range(2):
                    ins = dve.tensor_scalar(out[p][:, t, :], src[p][:, t, :], mv[l][p][:, t, 0:1], rs[l][p][:, t, c:c + 1],
                                            ALU.subtract, ALU.mult)
                if done:
                    ins.then_inc(done[p], 1)

            def add_residual(p, a, n):
                dve.wait_ge(y_ps[p], c2(n, a))
                if a == 1 and not first(n):
                    dve.wait_ge(resid_ready[p], c1(n - 1))
                dve.tensor_tensor((h1 if a == 0 else xm)[p][:, :, :],
                                  bank(p, 2, HALF, 0, 2 * H).rearrange("p (t c) -> p t c", t=2),
                                  (hin if a == 0 else xin)[p][:, :, :], ALU.add).then_inc(h_ready[p], 1)
                dve.wait_ge(h_ready[p], c2(n, a))

            def maxima(p, a, n, s, half):
                dve.wait_ge(sm_ps[p], c8(n, a, s, half))
                dve.tensor_reduce(mx[p][:, s, :].rearrange("p (g j r) -> p j g r", g=2, j=4)[:, 2 * half:2 * half + 2, :, HD],
                                  R[p][0:HALF, 2 * half:2 * half + 2, 0:2 * N].rearrange("p b (g n) -> p b g n", g=2),
                                  AX.X, ALU.max, negate=True).then_inc(max_done[p], 1)

            def top_two(p, n):
                dve.wait_ge(lg_ready[p], c1(n))
                settled(dve)
                for t in range(2):
                    ins = dve.max(v8[p][:, t, :], lg[p][:, t, :])
                ins.then_inc(top_step[p], 1)
                dve.wait_ge(top_step[p], n * 3 + 1)
                settled(dve)
                for t in range(2):
                    dve.max_index(i8[p][:, t, :], v8[p][:, t, :], lg[p][:, t, :])
                dve.tensor_tensor(dif[p][:, :], v8[p][:, :, 1], v8[p][:, :, 0], ALU.subtract).then_inc(idx_ready[p], 1)
                dve.wait_ge(idx_ready[p], c1(n))
                dve.tensor_copy(ix[p][:, :, :], i8[p][:, :, 0:2]).then_inc(top_step[p], 1)
                dve.wait_ge(top_step[p], n * 3 + 2)
                dve.tensor_tensor(oh[p][:, :, :, :].rearrange("p t k e -> p (t k) e"),
                                  iota[:, None, :].broadcast_to([HALF, 4, E]),
                                  ix[p][:, :, :].rearrange("p t k -> p (t k)")[:, :, None].broadcast_to([HALF, 4, E]),
                                  ALU.is_equal).then_inc(top_step[p], 1)
                dve.wait_ge(top_step[p], n * 3 + 3)
                dve.tensor_tensor(ohs[p][:, :, :], oh[p][:, :, 0, :], oh[p][:, :, 1, :], ALU.add).then_inc(ohs_ready[p], 1)

            def read_counts(p, n):
                dve.wait_ge(cnt_ps[p], c1(n))
                dve.wait_ge(taken_ready, n * 2 + (p + 1))
                dve.tensor_tensor(before[p][:, :, :], bank(p, 1, HALF, 0, 2 * E).rearrange("p (t e) -> p t e", t=2),
                                  taken[p][:, None, :].broadcast_to([HALF, 2, E]), ALU.add)
                dve.tensor_tensor(taken[1 - p][:, :], bank(p, 1, HALF, 2 * E, 3 * E), taken[p][:, :], ALU.add
                                  ).then_inc(cnt_read[p], 1)
                dve.wait_ge(cnt_read[p], c1(n))
                dve.sem_inc(taken_ready, 1)

            def find_slots(p, n):
                dve.tensor_tensor(sel[p][:, :, :, :], before[p][:, :, None, :].broadcast_to([HALF, 2, 2, E]),
                                  oh[p][:, :, :, :], ALU.mult).then_inc(slot_step[p], 1)
                dve.wait_ge(slot_step[p], n * 4 + 1)
                dve.tensor_reduce(pos[p][:, :, :], sel[p][:, :, :, :], AX.X, ALU.add).then_inc(slot_step[p], 1)
                dve.wait_ge(slot_step[p], n * 4 + 2)
                dve.tensor_scalar(keep[p][:, :, :], pos[p][:, :, :], float(CAP), None, ALU.is_lt)
                dve.tensor_scalar(mnp[p][:, :, :], pos[p][:, :, :], float(CAP - 1), None, ALU.min).then_inc(slot_step[p], 1)
                dve.wait_ge(slot_step[p], n * 4 + 3)
                dve.scalar_tensor_tensor(slf[p][:, :, :], ix[p][:, :, :], float(CAP), mnp[p][:, :, :], ALU.mult, ALU.add)
                dve.tensor_scalar(off[p][:, :, :], keep[p][:, :, :], -BIG, BIG, ALU.mult, ALU.add).then_inc(slot_step[p], 1)
                dve.wait_ge(slot_step[p], n * 4 + 4)
                if not first(n):
                    dve.wait_ge(scat_out[p], n * 64)
                dve.tensor_tensor(scu[p][:, :, :], slf[p][:, :, :], off[p][:, :, :], ALU.add).then_inc(scu_ready[p], 1)
                dve.wait_ge(e2_ready[p], c1(n))
                dve.tensor_scalar(gt[p][:, :, 1], e2[p][:, :], 1.0, None, ALU.add).then_inc(gate_step[p], 1)
                dve.wait_ge(gate_step[p], n * 3 + 1)
                dve.reciprocal(gt[p][:, :, 0], gt[p][:, :, 1]).then_inc(gate_step[p], 1)
                dve.wait_ge(gate_step[p], n * 3 + 2)
                dve.tensor_tensor(gt[p][:, :, 1], gt[p][:, :, 0], e2[p][:, :], ALU.mult).then_inc(gate_step[p], 1)
                dve.wait_ge(gate_step[p], n * 3 + 3)
                dve.tensor_tensor(gate[:, bass.ds(n * 8 + 4 * p, 4)], gt[p][:, :, :].rearrange("p t k -> p (t k)"),
                                  keep[p][:, :, :].rearrange("p t k -> p (t k)"), ALU.mult).then_inc(gate_done[p], 1)

            def denominators(p, a, n):
                dve.wait_ge(o_ps[p], c2(n, a))
                settled(dve)
                dve.stream_shuffle(dn[p][:, :], bank(p, 0, 128, 0, 2 * N), [HD] * 32).then_inc(den_step[p], 1)

            def reciprocals(p, a, n, g):
                if g == 0:
                    dve.wait_ge(den_step[p], n * 6 + (3 * a + 1))
                dve.reciprocal(rc[p][:, g * N:(g + 1) * N], dn[p][:, g * N:(g + 1) * N]).then_inc(den_step[p], 1)

            def weighted_means(p, a, n):
                dve.wait_ge(den_step[p], n * 6 + (3 * a + 3))
                dve.tensor_tensor(oT[p][:, :, :].rearrange("p g n -> p (g n)"), bank(p, 0, 128, 0, 2 * N), rc[p][:, :],
                                  ALU.mult).then_inc(oT_ready[p], 1)

            def half(light, heavy, more=True):
                lp, la, lnum = light
                if la == 1:
                    add_residual(lp, 0, lnum)
                    statistics(1, lp, lnum, h1)
                    normalize(1, lp, lnum, h1, 1, xh, xh_ready)
                    if not first(lnum):
                        read_counts(lp, lnum - 1)
                    normalize(1, lp, lnum, h1, 0, xin, None)
                    if not first(lnum):
                        find_slots(lp, lnum - 1)
                    dve.wait_ge(qk_copied[lp], lnum * 2 + 2)
                    dve.tensor_copy(qkb[lp][:, :, :], qk[lp][:, :, :]).then_inc(qkb_ready[lp], 1)
                elif not first(lnum):
                    add_residual(lp, 1, lnum - 1)
                    statistics(2, lp, lnum - 1, xm)
                next_image = heavy and heavy[1] == 1 and not (isinstance(heavy[2], int) and heavy[2] == B // 2 - 1)
                if la == 0 and more:
                    dve.wait_ge(qkv_ps[lp], c2(lnum, 0))
                    dve.tensor_tensor(rt[lp][:, :, :].rearrange("p (b g) n -> p b (g n)", b=4), R[lp][:, :, 0:2 * N],
                                      ropet[:, :, :].rearrange("p (b g) n -> p b (g n)", b=4), ALU.mult
                                      ).then_inc(rope_mul[lp], 1)
                    dve.wait_ge(rope_mul[lp], c1(lnum))
                    dve.tensor_tensor(rt[lp][:, 0:4, :], rt[lp][:, 0:4, :], rt[lp][:, 4:8, :], ALU.add).then_inc(rope_sum[lp], 1)
                    dve.wait_ge(rope_sum[lp], c1(lnum))
                    dve.tensor_tensor(qkb[lp][:, :, :], rt[lp][:, 0:4, :], ropeb[:, :, :], ALU.add).then_inc(qkb_ready[lp], 1)
                    dve.tensor_tensor(va[lp][:, :, :, 0:HD],
                                      ps[0:HALF, 4 * lp:4 * lp + 2, 2 * N:2 * N + H].rearrange("p t (h d) -> p t h d", d=HD),
                                      bv0[:, :].rearrange("p (h d) -> p h d", d=HD)[:, None, :, :].broadcast_to([HALF, 2, NH, HD]),
                                      ALU.add).then_inc(v_ready0[lp], 1)
                if more:
                    for s in range(2):
                        for b in range(2):
                            maxima(lp, la, lnum, s, b)
                if heavy:
                    denominators(*heavy)
                    reciprocals(*heavy, 0)
                if more:
                    dve.wait_ge(mT_ps[lp], c2(lnum, la))
                    if la == 0:
                        dve.wait_ge(qk_roped[lp], c1(lnum))
                    dve.tensor_tensor(qm[lp][:, :, :], qk[lp][:, 0:2, :],
                                      bank(lp, 0, 128, 0, 2 * N).rearrange("p (g n) -> p g n", g=2), ALU.add
                                      ).then_inc(qm_ready[lp], 1)
                if heavy:
                    reciprocals(*heavy, 1)
                    weighted_means(*heavy)
                if la == 0 and not first(lnum):
                    normalize(2, lp, lnum - 1, xm, 0, xh2, xh2_ready)
                if next_image:
                    hp, ha, hn = heavy
                    dve.wait_ge(hin_in[hp], hn * 48 + 96)
                    statistics(0, hp, hn + 1, hin)
                if heavy and heavy[1] == 0 and not first(heavy[2]):
                    top_two(heavy[0], heavy[2] - 1)
                if next_image:
                    normalize(0, hp, hn + 1, hin, 0, xh, xh_ready)

            def tail(n):
                add_residual(1, 1, n)
                statistics(2, 1, n, xm)
                normalize(2, 1, n, xm, 0, xh2, xh2_ready)
                for p in range(2):
                    top_two(p, n)
                for p in range(2):
                    read_counts(p, n)
                    find_slots(p, n)

            for p in range(2):
                dve.wait_ge(hin_in[p], 48)
                statistics(0, p, 0, hin)
            for p in range(2):
                normalize(0, p, 0, hin, 0, xh, xh_ready)
            schedule(dve, half, tail)

            with dve.Fori(0, E // 2) as it:
                for p in range(2):
                    dve.wait_ge(eT_ps, n2(it, p))
                    dve.tensor_copy(eT[p][:, 0:512], ps[:, 0, :])
                    dve.tensor_copy(eT[p][:, 512:CAP], ps[:, 1, 0:CAP - 512]).then_inc(eT_ready, 1)
                    last = ex[p][:, :, H]
                    dve.wait_ge(ey_out[p], it * 96 + 16)
                    dve.tensor_scalar(em[p][:, 0:MAIN], last, 0.5, BIG, ALU.is_lt, ALU.mult)
                    dve.tensor_scalar(em[p][0:TAIL, MAIN:], ext[p][:, H:], 0.5, BIG, ALU.is_lt, ALU.mult).then_inc(em_ready, 1)
                    dve.wait_ge(em_ready, n2(it, p))
                    dve.scalar_tensor_tensor(eu[p][:, 0:MAIN], last, -1.0, em[p][:, 0:MAIN], ALU.add, ALU.add)
                    dve.scalar_tensor_tensor(eu[p][0:TAIL, MAIN:], ext[p][:, H:], -1.0, em[p][0:TAIL, MAIN:], ALU.add, ALU.add)
                    dve.wait_ge(ey_ps, n2(it, p))
                    dve.wait_ge(w_in[p], it * 48 + 48)
                    bb = b2s[p][:, None, :]
                    dve.tensor_tensor(ey[p][:, 0:4, :], ps[:, 6, :].rearrange("p (c h) -> p c h", c=4),
                                      bb.broadcast_to([128, 4, H]), ALU.add)
                    dve.tensor_tensor(ey[p][:, 4, :], ps[:, 7, 0:H], b2s[p][:, :], ALU.add)
                    dve.tensor_tensor(ey[p][0:TAIL, 5, :], ps[0:TAIL, 7, H:2 * H], b2s[p][0:TAIL, :], ALU.add
                                      ).then_inc(ey_ready, 1)

            for p in range(2):
                dve.wait_ge(gate_done[p], B // 2)
            with dve.Fori(0, B // 2) as it:
                for p in range(2):
                    dve.wait_ge(yl_in[p], it * 16 + 16)
                    dve.wait_ge(fin_out[p], it * 16 + 16)
                    for t in range(2):
                        ins = dve.scalar_tensor_tensor(tmpd[p][:, t, :], yl[p][:, t, 0, :],
                                                       gate[:, bass.ds(it * 8 + (4 * p + 2 * t), 1)],
                                                       resid[:, bass.ds(it * 4 + (2 * p + t), 1), :].rearrange("p o c -> p (o c)"),
                                                       ALU.mult, ALU.add)
                    ins.then_inc(fin_step, 1)
                for p in range(2):
                    dve.wait_ge(fin_step, n2(it, p))
                    for t in range(2):
                        ins = dve.scalar_tensor_tensor(fin[p][:, t, :], yl[p][:, t, 1, :],
                                                       gate[:, bass.ds(it * 8 + (4 * p + 2 * t + 1), 1)], tmpd[p][:, t, :],
                                                       ALU.mult, ALU.add)
                    ins.then_inc(fin_ready, 1)


def host_layout(i):
    import numpy as np

    f = {k: np.asarray(v) for k, v in i.items()}
    a = {"x": f["x"], "txt": f["txt"]}
    w = np.zeros((3, 16, 16, H), np.float32)
    w[..., 0:64] = f["L0_tok_W_main"].reshape(64, 3, 16, 16).transpose(1, 2, 3, 0)
    sx = f["L0_tok_W_sx"].reshape(16, 3, 16, 16).transpose(1, 2, 3, 0)
    sy = f["L0_tok_W_sy"].reshape(16, 3, 16, 16).transpose(1, 2, 3, 0)
    w[:, :, 8:, 64:80] = sx[:, :, :8]
    w[:, :, :8, 80:96] = sx[:, :, 8:]
    w[:, 8:, :, 96:112] = sy[:, :8]
    w[:, :8, :, 112:128] = sy[:, 8:]
    a["w_tok"] = w.reshape(768, H)
    a["b_tok"] = np.concatenate([f["L0_tok_b_main"], f["L0_tok_b_sx"], f["L0_tok_b_sx"], f["L0_tok_b_sy"],
                                 f["L0_tok_b_sy"]])[:, None]
    a["ln_g"], a["ln_b"] = f["L0_tok_ln_g"][None], f["L0_tok_ln_b"][None]
    moves = np.zeros((4, H, H), np.float32)
    for s, (src, dst) in enumerate([(80, 64), (64, 80), (112, 96), (96, 112)]):
        for c in range(16):
            moves[s, src + c, dst + c] = 1
    a["moves"] = moves
    a["ident_d"] = np.eye(128, dtype=np.float32)
    before = np.triu(np.ones((HALF, HALF), np.float32), 1)
    a["tri"] = before
    freqs = np.float32(1.0) / np.float32(10000.0) ** (np.arange(0, HD, 2, dtype=np.float32) / np.float32(HD))
    ang = np.outer(np.arange(N, dtype=np.float32), freqs).astype(np.float32)
    cos, sin = np.cos(ang).T, np.sin(ang).T
    rope = np.zeros((128, 8, N), np.float32)
    for j in range(4):
        for d in range(HD):
            rope[32 * j + d, 0:4] = cos[d // 2]
            rope[32 * j + d, 4:8] = sin[d // 2] if d % 2 else -sin[d // 2]
    a["rope"] = rope

    def heads(wt, other=False):
        wt = wt.reshape(wt.shape[0], NH, HD)
        if other:
            wt = wt.reshape(-1, NH, HD // 2, 2)[..., ::-1].reshape(-1, NH, HD)
        o = np.zeros((wt.shape[0], NH, 32), np.float32)
        o[:, :, :HD] = wt
        return o.reshape(-1, 2, 128)

    wq, wk, wv = (f["L0_attn_Wqkv"][n * H:(n + 1) * H].T for n in range(3))
    bq, bk, bv = (f["L0_attn_bqkv"][n * H:(n + 1) * H] for n in range(3))
    a["w_qk0"] = np.concatenate([heads(wq), heads(wk), heads(wq, True), heads(wk, True)], 1)
    a["b_qk0"] = np.concatenate([heads(bq[None]), heads(bk[None]), heads(bq[None], True), heads(bk[None], True)], 1)[0].T
    a["w_v0"], a["b_v0"] = wv, bv[None]

    def heads_in(wt):
        return heads(wt.T).transpose(2, 1, 0)

    a["w_o0"] = heads_in(f["L0_attn_Wproj"].T)
    a["w_o0"][HD, 0] = f["L0_attn_bproj"]
    a["w_qk1"] = np.concatenate([heads(f["L0_ffn_wq"]), heads(f["L0_ffn_wk"])], 1)
    one = np.zeros((128, 1), np.float32)
    one[HD::32] = 1
    a["one_row"] = one
    a["w_v1"], a["w_o1"] = f["L0_ffn_wv"], heads_in(f["L0_ffn_wo"])
    a["g1"], a["be1"] = f["L0_ffn_ln1_g"][:, None], f["L0_ffn_ln1_b"][:, None]
    a["g2"], a["be2"] = f["L0_ffn_ln2_g"][None], f["L0_ffn_ln2_b"][None]
    a["w_r"], a["w1"], a["w2"], a["b2"] = f["L0_ffn_wr"], f["L0_ffn_w1"], f["L0_ffn_w2"], f["L0_ffn_b2"]
    a["b1"] = f["L0_ffn_b1"].reshape(E, 128, FC).transpose(1, 0, 2)
    return {k: np.ascontiguousarray(v) for k, v in a.items()}


_ORDER = ["x", "txt", "w_tok", "b_tok", "ln_g", "ln_b", "moves", "ident_d", "tri", "rope", "w_qk0", "b_qk0",
          "w_v0", "b_v0", "w_o0", "w_qk1", "one_row", "w_v1", "w_o1", "g1", "be1", "g2", "be2", "w_r", "w1", "b1",
          "w2", "b2"]


def kernel(**inputs):
    import concourse.bacc as _bacc
    from concourse import mybir as _mybir
    from concourse.bass_utils import run_bass_kernel_spmd as _run

    nc = _bacc.Bacc("TRN2", target_bir_lowering=False, num_devices=1)
    arrays = {"in_" + k: v for k, v in host_layout(inputs).items()}
    args = [nc.dram_tensor("in_" + k, arrays["in_" + k].shape, _mybir.dt.from_np(arrays["in_" + k].dtype),
                           kind="ExternalInput").ap() for k in _ORDER]
    out = nc.dram_tensor("out", (B, N, H), F32, kind="ExternalOutput").ap()
    program(nc, *args, out)
    r = _run(nc, [arrays], core_ids=[0])
    return r.results[0]["out"]
```

```python
from contextlib import ExitStack

import concourse.bass as bass
from concourse import mybir

F32 = mybir.dt.float32
U32 = mybir.dt.uint32
BF16 = mybir.dt.bfloat16
ALU = mybir.AluOpType
ACT = mybir.ActivationFunctionType
AX = mybir.AxisListType

B = 64
NP = 6
IMG = 36
TXT = 128
N = IMG + TXT
H = 128
HALF = N // 2
NH = 8
HD = H // NH
E = 64
F = 512
FC = F // 128
CAP = 2 * (B * N * 2 // E)
SLOTS = E * CAP
ROW = H + 1
CHOICES = B * N * 2
SCALE = HD ** -0.5
EPS = 1e-5
GRP = 16
BLOCKS = -(-2 * N // 32)
ROWS = GRP * NP
MAIN = CAP // 128
TAIL = CAP - MAIN * 128
BIG = 65536.0


def program(nc, x, txt, w_tok, b_tok, ln_g, ln_b, moves, ident_d, tri, rope, w_qk0, b_qk0, w_v0, b_v0,
            w_o0, w_qk1, one_row, w_v1, w_o1, g1, be1, g2, be2, w_r, w1, b1, w2, b2, out):
    with ExitStack() as ctx:
        def sb(name, shape, dt=F32):
            return ctx.enter_context(nc.sbuf_tensor(name, shape, dt))

        def sem(name):
            return ctx.enter_context(nc.semaphore(name))

        tokens = nc.dram_tensor("tokens", [B, IMG, H], F32).ap()
        slots_x = nc.dram_tensor("slots_x", [SLOTS, ROW], F32).ap()
        scratch = nc.dram_tensor("scratch", [8, E], F32).ap()
        choice_y = nc.dram_tensor("choice_y", [CHOICES, H], F32).ap()

        ps = ctx.enter_context(nc.psum_tensor("ps", [128, 8, 512], F32))

        ident = sb("ident", [128, 128])
        trif = sb("trif", [HALF, HALF])
        trib = sb("trib", [HALF, HALF], BF16)
        allb = sb("allb", [HALF, HALF], BF16)
        movem = sb("movem", [128, 4, 128])
        wtok = sb("wtok", [128, 6, 128])
        btok = sb("btok", [128, 1])
        lng = sb("lng", [2 * IMG, H])
        lnb = sb("lnb", [2 * IMG, H])
        ropet = sb("ropet", [128, 8, N])
        bqk0 = sb("bqk0", [128, 8])
        ropeb = sb("ropeb", [128, 4, N])
        wqk0 = sb("wqk0", [128, 8, 128])
        wv0 = sb("wv0", [128, 128])
        bv0 = sb("bv0", [HALF, H])
        wo0 = sb("wo0", [128, 2, H])
        wqk1 = sb("wqk1", [128, 4, 128])
        onerow = sb("onerow", [128, 1])
        wv1 = sb("wv1", [128, 128])
        wo1 = sb("wo1", [128, 2, H])
        g1c = sb("g1c", [128, 1])
        be1c = sb("be1c", [128, 1])
        g2r = sb("g2r", [HALF, H])
        be2r = sb("be2r", [HALF, H])
        wr = sb("wr", [128, E])
        iota = sb("iota", [HALF, E])
        mhalf = sb("mhalf", [128, 8])
        b1c = sb("b1c", [128, E, FC])

        def two(name, shape, dt=F32):
            return [sb(f"{name}{p}", shape, dt) for p in range(2)]

        hin = two("hin", [HALF, 2, H])
        h1 = two("h1", [HALF, 2, H])
        xin = two("xin", [HALF, 2, H])
        xm = two("xm", [HALF, 2, H])
        xh = two("xh", [HALF, 2, H])
        xh2 = two("xh2", [HALF, 2, H])
        x2 = two("x2", [HALF, 2, 2, ROW])
        ln = range(3)
        stat = [two(f"stat{l}", [HALF, 2, 6]) for l in ln]
        mv = [two(f"mv{l}", [HALF, 2, 2]) for l in ln]
        ve = [two(f"ve{l}", [HALF, 2, 2]) for l in ln]
        rs = [two(f"rs{l}", [HALF, 2, 2]) for l in ln]
        xhT = two("xhT", [128, N])
        x2T = two("x2T", [128, N])
        rt = two("rt", [128, 8, N])
        qk = two("qk", [128, 4, N])
        qkb = two("qkb", [128, 4, N], BF16)
        keys = two("keys", [128, 4, 2, N])
        qm = two("qm", [128, 2, N])
        mx = two("mx", [HALF, 2, NH * 32])
        va = two("va", [HALF, 2, NH, 32])
        big = two("big", [128, FC * CAP])
        pT = [b[0:HALF, :].rearrange("p (s h n) -> p s h n", s=2, h=NH) for b in big]
        hT = [b[:, :].rearrange("p (f c) -> p f c", f=FC) for b in big]
        sums = two("sums", [128, BLOCKS, 32])
        inv = two("inv", [128, BLOCKS])
        rc = two("rc", [128, 32 * BLOCKS])
        oT = two("oT", [128, 2, N])
        lg = two("lg", [HALF, 2, E])
        v8 = two("v8", [HALF, 2, 8])
        i8 = two("i8", [HALF, 2, 8], U32)
        dif = two("dif", [HALF, 2])
        e2 = two("e2", [HALF, 2])
        ix = two("ix", [HALF, 2, 2])
        oh = two("oh", [HALF, 2, 2, E], BF16)
        ohs = two("ohs", [HALF, 2, E], BF16)
        before = two("before", [HALF, 2, E])
        taken = two("taken", [HALF, E])
        sel = two("sel", [HALF, 2, 2, E])
        pos = two("pos", [HALF, 2, 2])
        keep = two("keep", [HALF, 2, 2])
        mnp = two("mnp", [HALF, 2, 2])
        slf = two("slf", [HALF, 2, 2])
        scu = two("scu", [HALF, 2, 2], U32)
        off = two("off", [HALF, 2, 2])
        gt = two("gt", [HALF, 2, 2])

        store = sb("store", [128, 2 * B * H])
        resid = store[0:HALF, :].rearrange("p (t c) -> p t c", c=H)
        gate = sb("gate", [HALF, 2 * B * 2])

        with ExitStack() as early:
            def sa(name, shape):
                return early.enter_context(nc.sbuf_tensor(name, shape, F32))

            xs = [store[0:ROWS, i * 4608:(i + 1) * 4608].rearrange("p (c y w) -> p c y w", c=3, y=16) for i in range(2)]
            xr = store[0:ROWS, 2 * 4608:3 * 4608].rearrange("p (j f) -> p j f", j=NP)
            xT = [sa(f"xT{i}", [128, 2, 288]) for i in range(2)]
            tokT = sa("tokT", [128, 2, 288])
            gpad = sa("gpad", [128, GRP, 8, 8])
            tok = sa("tok", [2 * IMG, 8, H])
            tok2 = sa("tok2", [2 * IMG, 8, H])
            tstat = sa("tstat", [2 * IMG, 8, 6])
            tmv = sa("tmv", [2 * IMG, 8, 2])
            tve = sa("tve", [2 * IMG, 8])
            trs = sa("trs", [2 * IMG, 8])

        w1s = two("w1s", [128, F])
        w2s = two("w2s", [128, FC, H])
        b2s = two("b2s", [128, H])
        ex = two("ex", [128, MAIN, ROW])
        ext = two("ext", [TAIL, ROW])
        number = two("number", [128, MAIN + 1])
        em = two("em", [128, MAIN + 1])
        eu = two("eu", [128, MAIN + 1], U32)
        eT = two("eT", [128, CAP])
        ey = [r[:, :, :].rearrange("p g n -> p (g n)")[:, 0:(MAIN + 1) * H].rearrange("p (c h) -> p c h", h=H) for r in rt]

        flat = [r[0:HALF, :, :].rearrange("p g n -> p (g n)") for r in rt]
        yl = [f[:, 0:4 * H].rearrange("p (t k c) -> p t k c", t=2, k=2) for f in flat]
        fin = [f[:, 4 * H:6 * H].rearrange("p (t c) -> p t c", t=2) for f in flat]
        tmpd = [f[:, 6 * H:8 * H].rearrange("p (t c) -> p t c", t=2) for f in flat]

        consts_in = sem("consts_in")
        xs_in = [sem(f"xs_in{i}") for i in range(2)]
        memset_done = sem("memset_done")
        iota_done = sem("iota_done")
        trib_ready = sem("trib_ready")
        ropeb_step = sem("ropeb_step")
        zero_ready = sem("zero_ready")
        zeros_out = sem("zeros_out")
        patch_rows = sem("patch_rows")
        patch_ps = sem("patch_ps")
        patch_sb = sem("patch_sb")
        emb_ps = sem("emb_ps")
        emb_sb = sem("emb_sb")
        tokT_ps = sem("tokT_ps")
        tokT_sb = sem("tokT_sb")
        tok_ps = sem("tok_ps")
        tok_sb = sem("tok_sb")
        tok_stat = sem("tok_stat")
        tok_mv = sem("tok_mv")
        tok_step = sem("tok_step")
        tok_rs = sem("tok_rs")
        tok_norm = sem("tok_norm")
        tok_ready = sem("tok_ready")
        tok_out = sem("tok_out")

        waits_passed = sem("waits_passed")

        def sems(name):
            return [sem(f"{name}{p}") for p in range(2)]

        hin_in = sems("hin_in")
        stat_done = [sems(f"stat_done_{l}") for l in ln]
        mv_ready = [sems(f"mv_ready_{l}") for l in ln]
        ve_ready = [sems(f"ve_ready_{l}") for l in ln]
        rs_ready = [sems(f"rs_ready_{l}") for l in ln]
        xh_ready = sems("xh_ready")
        xin_ready = sems("xin_ready")
        xh2_step = sems("xh2_step")
        xT_ps = sems("xT_ps")
        xT_ready = sems("xT_ready")
        qkv_ps = sems("qkv_ps")
        rope_mul = sems("rope_mul")
        rope_sum = sems("rope_sum")
        qk_roped = sems("qk_roped")
        qk_copied = sems("qk_copied")
        qkb_ready = sems("qkb_ready")
        keys_ready = sems("keys_ready")
        v_ready0 = sems("v_ready0")
        v_ready1 = sems("v_ready1")
        sm_ps = sems("sm_ps")
        max_done = sems("max_done")
        mT_ps = sems("mT_ps")
        qm_ready = sems("qm_ready")
        st_ps = sems("st_ps")
        exp_done = sems("exp_done")
        o_ps = sems("o_ps")
        den_step = sems("den_step")
        oT_ready = sems("oT_ready")
        y_ps = sems("y_ps")
        h_ready = sems("h_ready")
        resid_ready = sems("resid_ready")
        x2_ready = sems("x2_ready")
        x2T_ps = sems("x2T_ps")
        x2T_ready = sems("x2T_ready")
        lg_ps = sems("lg_ps")
        lg_ready = sems("lg_ready")
        top_step = sems("top_step")
        idx_ready = sems("idx_ready")
        ohs_ready = sems("ohs_ready")
        e2_ready = sems("e2_ready")
        cnt_ps = sems("cnt_ps")
        taken_ready = sem("taken_ready")
        cnt_read = sems("cnt_read")
        slot_step = sems("slot_step")
        scu_ready = sems("scu_ready")
        gate_step = sems("gate_step")
        gate_done = sems("gate_done")
        scat_out = sems("scat_out")

        first_in = sems("first_in")
        second_in = sems("second_in")
        eT_ps = sem("eT_ps")
        eT_ready = sem("eT_ready")
        h_ps = sem("h_ps")
        gelu_done = sem("gelu_done")
        ey_ps = sem("ey_ps")
        ey_ready = sem("ey_ready")
        em_ready = sem("em_ready")
        rows_used = sem("rows_used")
        ey_out = sems("ey_out")

        yl_in = sems("yl_in")
        fin_step = sem("fin_step")
        fin_ready = sem("fin_ready")
        fin_out = sems("fin_out")

        consts = [
            (ident[:, :], ident_d), (trif[:, :], tri),
            (movem[:, :, :], moves.rearrange("s p n -> p s n")), (wtok[:, :, :], w_tok.rearrange("(k p) n -> p k n", p=128)),
            (btok[:, :], b_tok), (lng[:, :], ln_g.broadcast_to([2 * IMG, H])),
            (lnb[:, :], ln_b.broadcast_to([2 * IMG, H])), (ropet[:, :, :], rope), (bqk0[:, :], b_qk0),
            (wqk0[:, :, :], w_qk0), (wv0[:, :], w_v0), (bv0[:, :], b_v0.broadcast_to([HALF, H])), (wo0[:, :, :], w_o0),
            (wqk1[:, :, :], w_qk1), (onerow[:, :], one_row), (wv1[:, :], w_v1),
            (wo1[:, :, :], w_o1), (g1c[:, :], g1), (be1c[:, :], be1), (g2r[:, :], g2.broadcast_to([HALF, H])),
            (be2r[:, :], be2.broadcast_to([HALF, H])), (wr[:, :], w_r), (b1c[:, :, :], b1),
        ]
        CONSTS = 16 * len(consts)
        FILLS = -(-SLOTS * ROW // 128 // (FC * CAP)) - (-CHOICES * H // 128 // (FC * CAP))

        def c1(n):
            return n + 1

        def c2(n, a):
            return n * 2 + (a + 1)

        def c4(n, a, s):
            return n * 4 + (2 * a + s + 1)

        def c8(n, a, s, half):
            return n * 8 + (4 * a + 2 * s + half + 1)

        def n2(it, p):
            return it * 2 + (p + 1)

        def settled(eng):
            eng.sem_inc(waits_passed, 1)

        R = [ps[:, 4 * p:4 * p + 4, :] for p in range(2)]

        def bank(p, b, rows, c0, c1):
            return ps[0:rows, 4 * p + b, c0:c1]

        def schedule(eng, half, tail):
            last = B // 2 - 1

            def pair(n, more=True):
                half((1, 0, n), (0, 0, n))
                half((0, 1, n), (1, 0, n))
                half((1, 1, n), (0, 1, n))
                half((0, 0, n + 1), (1, 1, n), more)

            half((0, 0, 0), None)
            pair(0)
            with eng.Fori(1, last) as n:
                pair(n)
            pair(last, False)
            tail(last)

        def expert_order(eng, turned, first_part, second_part):
            last = E // 2 - 1
            turned(0, 0)
            first_part(0, 0)
            turned(0, 1)
            with eng.Fori(0, last) as m:
                first_part(m, 1)
                turned(m + 1, 0)
                second_part(m, 0)
                first_part(m + 1, 0)
                turned(m + 1, 1)
                second_part(m, 1)
            first_part(last, 1)
            second_part(last, 0)
            second_part(last, 1)

        def first(n):
            return isinstance(n, int) and n == 0

        block = ctx.enter_context(nc.Block())

        @block.sync
        def _(sp):
            for s in fin_out:
                sp.sem_inc(s, 16)
            for dst, src in consts:
                sp.dma_start(dst, src).then_inc(consts_in, 16)

            with sp.Fori(0, 2) as it:
                for i in range(2):
                    sp.wait_ge(patch_rows, it * 2 + 1)
                    for b in range(GRP):
                        sp.dma_start(xs[i][b * NP:(b + 1) * NP, :, :, :],
                                     x[bass.ds((it * 2 + i) * GRP + b, 1)].rearrange("b c (i y) w -> (b i) c y w", y=16)
                                     ).then_inc(xs_in[i], 16)
            sp.wait_ge(tok_out, 16 * 4 + 16)

            def load_image(p, image):
                sp.dma_start(hin[p][0:IMG, 0, :], tokens[image, :, :].rearrange("o n c -> (o n) c")).then_inc(hin_in[p], 16)
                sp.dma_start(hin[p][IMG:HALF, 0, :], txt[image, 0:HALF - IMG, :].rearrange("o n c -> (o n) c")
                             ).then_inc(hin_in[p], 16)
                sp.dma_start(hin[p][:, 1, :], txt[image, HALF - IMG:TXT, :].rearrange("o n c -> (o n) c")
                             ).then_inc(hin_in[p], 16)

            for p in range(2):
                load_image(p, bass.ds(p, 1))
            with sp.Fori(0, B // 2 - 1) as n:
                for p in range(2):
                    sp.wait_ge(h_ready[p], c2(n, 0))
                    load_image(p, bass.ds(n * 2 + (2 + p), 1))

            for p in range(2):
                sp.wait_ge(scat_out[p], 64 * (B // 2))

            def load_slots(p, e):
                rows = slots_x.rearrange("(e s) h -> e s h", s=CAP)[e, :, :]
                sp.dma_start(ex[p][:, :, :], rows[:, 0:MAIN * 128, :].rearrange("o (q c) h -> (o q) c h", c=MAIN)
                             ).then_inc(first_in[p], 16)
                sp.dma_start(ext[p][:, :], rows[:, MAIN * 128:CAP, :].rearrange("o q h -> (o q) h")
                             ).then_inc(first_in[p], 16)

            def load_first(p, e):
                sp.dma_start(w1s[p][:, :], w1[e, :, :].rearrange("o h f -> (o h) f")).then_inc(first_in[p], 16)

            def load_second(p, e):
                sp.dma_start(w2s[p][:, :, :], w2[e, :, :].rearrange("o (q c) h -> (o q) c h", c=FC)).then_inc(second_in[p], 16)
                sp.dma_start(b2s[p][:, :], b2[e, :].broadcast_to([128, H])).then_inc(second_in[p], 16)

            for p in range(2):
                load_slots(p, bass.ds(p, 1))
                load_first(p, bass.ds(p, 1))
                load_second(p, bass.ds(p, 1))

            def follow(m, p):
                sp.wait_ge(rows_used, n2(m, p))
                load_slots(p, bass.ds(m * 2 + (2 + p), 1))
                sp.wait_ge(h_ps, m * 8 + (4 * p + 4))
                load_first(p, bass.ds(m * 2 + (2 + p), 1))

            def follow_second(m, p):
                sp.wait_ge(ey_ready, m * 2 + (p + 2))
                load_second(p, bass.ds(m * 2 + (2 + p), 1))

            last = E // 2 - 2
            follow(0, 0)
            with sp.Fori(0, last) as it:
                follow(it, 1)
                follow_second(it, 0)
                follow(it + 1, 0)
                follow_second(it, 1)
            follow(last, 1)
            follow_second(last, 0)
            follow_second(last, 1)

            with sp.Fori(0, B // 2) as it:
                for p in range(2):
                    sp.wait_ge(fin_ready, n2(it, p) + 1)
                    o = out[bass.ds(it * 2 + p, 1), :, :].rearrange("o (t q) c -> (o q) t c", t=2)
                    sp.dma_start(o, fin[p][:, :, :]).then_inc(fin_out[p], 16)
            for p in range(2):
                sp.wait_ge(fin_out[p], 16 * (B // 2) + 16)

        @block.tensor
        def _(pe):
            for s in (tokT_ps, tok_ps, patch_ps, emb_ps,):
                pe.sem_inc(s, 1)
            pe.wait_ge(consts_in, CONSTS)
            with pe.Fori(0, 2) as it:
                for i in range(2):
                    pe.wait_ge(patch_rows, it * 2 + (i + 1) + 1)
                    for k in range(6):
                        pe.wait_ge(patch_sb, it * 12 + (6 * i + k) + 1)
                        for j in range(NP):
                            ins = pe.transpose(ps[:, j // 3, (j % 3) * ROWS:(j % 3 + 1) * ROWS],
                                               xr[:, j, k * 128:(k + 1) * 128],
                                               ident[0:ROWS, 0:ROWS])
                        ins.then_inc(patch_ps, 1)
                        pe.wait_ge(patch_sb, it * 12 + (6 * i + k + 1) + 1)
                        for g in range(2):
                            if k == 0 and g == 0:
                                pe.wait_ge(emb_sb, it * 2 + i + 1)
                            ins = pe.matmul(ps[:, 2 + g, 0:288], wtok[:, k, :], xT[k % 2][:, g, :],
                                            start=(k == 0), stop=(k == 5))
                    ins.then_inc(emb_ps, 1)
                    pe.wait_ge(emb_sb, it * 2 + (i + 1) + 1)
                    pe.wait_ge(tokT_sb, it * 2 + i + 1)
                    for g in range(2):
                        for s, (di, dj) in enumerate([(0, 0), (0, 1), (0, -1), (1, 0), (-1, 0)]):
                            ins = pe.matmul(ps[:, 4 + g, 0:288], ident[:, :] if s == 0 else movem[:, s - 1, :],
                                            gpad[:, 8 * g:8 * g + 8, 1 + di:7 + di, 1 + dj:7 + dj],
                                            start=(s == 0), stop=(s == 4))
                    ins.then_inc(tokT_ps, 1)
                    pe.wait_ge(tokT_sb, it * 2 + (i + 1) + 1)
                    pe.wait_ge(tok_sb, it * 2 + i + 1)
                    for q in range(GRP // 2):
                        ins = pe.transpose(ps[0:2 * IMG, 6 + q // 4, (q % 4) * 128:(q % 4 + 1) * 128],
                                           tokT[:, q // 4, (q % 4) * 72:(q % 4 + 1) * 72], ident[:, :])
                    ins.then_inc(tok_ps, 1)

            pe.wait_ge(memset_done, 1)
            pe.wait_ge(trib_ready, 1)
            pe.wait_ge(tok_sb, 4 + 1)

            def turn(p, b, src, done):
                for t in range(2):
                    ins = pe.transpose(bank(p, b, 128, HALF * t, HALF * (t + 1)), src[:, t], ident[0:HALF, 0:HALF])
                ins.then_inc(done, 1)

            def scores(p, a, n, s, half):
                if s == 0:
                    pe.wait_ge(keys_ready[p], c2(n, a))
                    pe.wait_ge(qm_ready[p], c2(n, a))
                else:
                    pe.wait_ge(exp_done[p], c8(n, a, 0, half))
                for g in range(2):
                    for j in (2 * half, 2 * half + 1):
                        ins = pe.matmul(bank(p, j, HALF, g * N, (g + 1) * N), keys[p][:, j, g, s * HALF:(s + 1) * HALF],
                                        qm[p][:, g, :], start=True, stop=True)
                ins.then_inc(st_ps[p], 1)

            def project(p, a, n):
                pe.wait_ge(xT_ready[p], c2(n, a))
                if not first(n) and a == 1:
                    pe.wait_ge(cnt_read[p], c1(n - 1))
                for g in range(4):
                    pe.matmul(bank(p, g // 2, 128, (g % 2) * N, (g % 2 + 1) * N), (wqk0 if a == 0 else wqk1)[:, g, :],
                              xhT[p][:, :], start=True, stop=True)
                for t in range(2):
                    ins = pe.matmul(bank(p, t, HALF, 2 * N, 2 * N + H), xhT[p][:, t * HALF:(t + 1) * HALF],
                                    (wv0 if a == 0 else wv1)[:, :], start=True, stop=True)
                ins.then_inc(qkv_ps[p], 1)

            def project_partners(p, n):
                if not first(n):
                    pe.wait_ge(h_ready[p], c2(n - 1, 1))
                for g in range(4, 8):
                    ins = pe.matmul(bank(p, g // 2, 128, (g % 2) * N, (g % 2 + 1) * N), wqk0[:, g, :],
                                    xhT[p][:, :], start=True, stop=True)
                ins.then_inc(qkv_ps[p], 1)

            def max_scores(p, a, n, s, i):
                if s == 1:
                    pe.wait_ge(max_done[p], c8(n, a, 0, i))
                elif i == 0:
                    pe.wait_ge(qkb_ready[p], c2(n, a))
                else:
                    pe.wait_ge((v_ready0, v_ready1)[a][p], c1(n))
                    if a == 1:
                        pe.wait_ge(qk_copied[p], n * 2 + 2)
                for g in range(2):
                    for j in (2 - 2 * i, 3 - 2 * i):
                        r = 32 * j
                        ins = pe.matmul(bank(p, j, HALF, g * N, (g + 1) * N),
                                        qkb[p][r:r + HD, g, s * HALF:(s + 1) * HALF],
                                        qkb[p][r:r + HD, 2 + g, :], start=True, stop=True)
                ins.then_inc(sm_ps[p], 1)

            def max_turn(p, a, n):
                pe.wait_ge(max_done[p], c8(n, a, 1, 1))
                for g in range(2):
                    for s in range(2):
                        ins = pe.transpose(bank(p, 0, 128, g * N + s * HALF, g * N + (s + 1) * HALF),
                                           mx[p][:, s, g * 128:(g + 1) * 128], ident[0:HALF, 0:HALF])
                ins.then_inc(mT_ps[p], 1)

            def weighted(p, a, n, part):
                heads = ((0, 4, 1, 5), (2, 6), (3, 7))[part]
                if part < 2:
                    pe.wait_ge(exp_done[p], c8(n, a, 1, part))
                for h in heads:
                    j, g = h % 4, h // 4
                    for s in range(2):
                        ins = pe.matmul(ps[32 * j:32 * j + 32, 4 * p, g * N:(g + 1) * N], va[p][:, s, h, :],
                                        pT[p][:, s, 2 * j + g, :], start=(s == 0), stop=(s == 1))
                if part == 2:
                    ins.then_inc(o_ps[p], 1)

            def out_project(p, a, n):
                pe.wait_ge(oT_ready[p], c2(n, a))
                for t in range(2):
                    for g in range(2):
                        ins = pe.matmul(bank(p, 2, HALF, t * H, (t + 1) * H), oT[p][:, g, t * HALF:(t + 1) * HALF],
                                        (wo0 if a == 0 else wo1)[:, g, :], start=(g == 0), stop=(g == 1))
                ins.then_inc(y_ps[p], 1)

            def turn_rows(p, n):
                pe.wait_ge(x2_ready[p], c1(n))
                turn(p, 1, x2[p][:, :, 0, 0:H], x2T_ps[p])

            def logits(p, n):
                pe.wait_ge(x2T_ready[p], c1(n))
                for t in range(2):
                    ins = pe.matmul(bank(p, 1, HALF, t * E, (t + 1) * E), x2T[p][:, t * HALF:(t + 1) * HALF],
                                    wr[:, :], start=True, stop=True)
                ins.then_inc(lg_ps[p], 1)

            def counts(p, n):
                pe.wait_ge(ohs_ready[p], c1(n))
                o0, o1 = ohs[p][:, 0, :], ohs[p][:, 1, :]
                pe.matmul(bank(p, 1, HALF, 0, E), trib[:, :], o0, start=True, stop=True)
                pe.matmul(bank(p, 1, HALF, E, 2 * E), allb[:, :], o0, start=True, stop=False)
                pe.matmul(bank(p, 1, HALF, E, 2 * E), trib[:, :], o1, start=False, stop=True)
                pe.matmul(bank(p, 1, HALF, 2 * E, 3 * E), allb[:, :], o0, start=True, stop=False)
                pe.matmul(bank(p, 1, HALF, 2 * E, 3 * E), allb[:, :], o1, start=False, stop=True).then_inc(cnt_ps[p], 1)

            def half(light, heavy, more=True):
                lp, la, lnum = light
                if heavy:
                    hp, ha, hn = heavy
                    scores(hp, ha, hn, 0, 0)
                if la == 1:
                    out_project(lp, 0, lnum)
                    if heavy:
                        scores(hp, ha, hn, 0, 1)
                        scores(hp, ha, hn, 1, 0)
                    if not first(lnum):
                        counts(lp, lnum - 1)
                    if heavy:
                        scores(hp, ha, hn, 1, 1)
                    pe.wait_ge(xh_ready[lp], c2(lnum, 1))
                    turn(lp, 0, xh[lp], xT_ps[lp])
                    if heavy:
                        weighted(hp, ha, hn, 0)
                    project(lp, 1, lnum)
                else:
                    if more:
                        pe.wait_ge(xh_ready[lp], c2(lnum, 0))
                        if not first(lnum):
                            pe.wait_ge(oT_ready[lp], c2(lnum - 1, 1))
                        turn(lp, 0, xh[lp], xT_ps[lp])
                    if not first(lnum):
                        out_project(lp, 1, lnum - 1)
                    if more:
                        project(lp, 0, lnum)
                    if heavy:
                        scores(hp, ha, hn, 0, 1)
                    if more:
                        project_partners(lp, lnum)
                    if heavy:
                        scores(hp, ha, hn, 1, 0)
                        scores(hp, ha, hn, 1, 1)
                        weighted(hp, ha, hn, 0)
                if heavy:
                    if ha == 0 and not first(hn):
                        turn_rows(hp, hn - 1)
                    weighted(hp, ha, hn, 1)
                    weighted(hp, ha, hn, 2)
                if more:
                    for s in range(2):
                        for i in range(2):
                            max_scores(lp, la, lnum, s, i)
                if heavy and ha == 0 and not first(hn):
                    logits(hp, hn - 1)
                if more:
                    max_turn(lp, la, lnum)

            def tail(n):
                out_project(1, 1, n)
                for p in range(2):
                    turn_rows(p, n)
                for p in range(2):
                    logits(p, n)
                for p in range(2):
                    pe.wait_ge(lg_ready[p], c1(n))
                    counts(p, n)

            schedule(pe, half, tail)

            def turn_slots(m, p):
                pe.wait_ge(first_in[p], m * 48 + 48)
                pe.wait_ge(eT_ready, m * 2 + p + 1)
                for c in range(MAIN):
                    pe.transpose(ps[:, c // 4, (c % 4) * 128:(c % 4 + 1) * 128], ex[p][:, c, 0:H], ident[:, :])
                pe.transpose(ps[:, 1, 128:128 + TAIL], ext[p][:, 0:H], ident[0:TAIL, 0:TAIL]).then_inc(eT_ps, 1)

            def first_product(m, p):
                pe.wait_ge(eT_ready, n2(m, p) + 1)
                for f in range(FC):
                    if not (first(m) and p == 0 and f == 0):
                        pe.wait_ge(gelu_done, m * 8 + (4 * p + f))
                    hp = 2 + 2 * (f % 2)
                    for g in range(2):
                        ins = pe.matmul(ps[:, hp + g, 0:CAP // 2], w1s[p][:, f:F:FC],
                                        eT[p][:, g * (CAP // 2):(g + 1) * (CAP // 2)], start=True, stop=True)
                    ins.then_inc(h_ps, 1)

            def second_product(m, p):
                pe.wait_ge(second_in[p], m * 32 + 32)
                pe.wait_ge(gelu_done, m * 8 + (4 * p + 4) + 1)
                pe.wait_ge(ey_ready, m * 2 + p + 1)
                for c in range(MAIN + 1):
                    rows = 128 if c < MAIN else TAIL
                    for f in range(FC):
                        ins = pe.matmul(ps[0:rows, 6 + c // 4, (c % 4) * 128:(c % 4 + 1) * 128],
                                        hT[p][:, f, c * 128:c * 128 + rows], w2s[p][:, f, :],
                                        start=(f == 0), stop=(f == FC - 1))
                ins.then_inc(ey_ps, 1)

            expert_order(pe, turn_slots, first_product, second_product)

        @block.scalar
        def _(act):
            for s in (emb_sb, tokT_sb, gelu_done,):
                act.sem_inc(s, 1)
            act.wait_ge(zero_ready, 1)
            zeros = hT[0][:, :, :].rearrange("p f c -> p (f c)")
            width = FC * CAP
            fills = 0
            for rows in (slots_x, choice_y):
                flat = rows.rearrange("(q r) h -> q (r h)", q=128)
                for c in range(0, flat.shape[1], width):
                    m = min(width, flat.shape[1] - c)
                    act.dma_start(flat[:, c:c + m], zeros[:, 0:m]).then_inc(zeros_out, 16)
                    fills += 1
            act.wait_ge(consts_in, CONSTS)
            with act.Fori(0, 2) as it:
                for i in range(2):
                    act.wait_ge(emb_ps, it * 2 + (i + 1) + 1)
                    act.wait_ge(memset_done, 1)
                    act.wait_ge(tokT_ps, it * 2 + i + 1)
                    for j in range(NP):
                        ins = act.activation(gpad[:, :, 1:7, 1 + j],
                                             ps[:, 2 + j // 3, (j % 3) * ROWS:(j % 3 + 1) * ROWS].rearrange("p (b i) -> p b i", i=NP),
                                             ACT.Identity)
                    ins.then_inc(emb_sb, 1)
                    act.wait_ge(tokT_ps, it * 2 + (i + 1) + 1)
                    act.wait_ge(tok_ps, it * 2 + i + 1)
                    act.activation(tokT[:, :, :], ps[:, 4:6, 0:288], ACT.Identity, bias=btok[:, 0:1]).then_inc(tokT_sb, 1)
            act.wait_ge(zeros_out, 16 * fills)

            def exponentials(p, a, n, s, half):
                act.wait_ge(st_ps[p], c8(n, a, s, half))
                act.activation(pT[p][:, s, 4 * half:4 * half + 4, :].rearrange("p (b g) n -> p b (g n)", b=2),
                               R[p][0:HALF, 2 * half:2 * half + 2, 0:2 * N], ACT.Exp, scale=SCALE).then_inc(exp_done[p], 1)

            def copy_turned(p, a, n):
                act.wait_ge(xT_ps[p], c2(n, a))
                if a == 0:
                    act.activation(xhT[p][:, :], bank(p, 0, 128, 0, N), ACT.Identity).then_inc(xT_ready[p], 1)
                else:
                    act.activation(xhT[p][:, :], bank(p, 0, 128, 0, N), ACT.Identity, bias=be1c[:, 0:1],
                                   scale=g1c[:, 0:1]).then_inc(xT_ready[p], 1)

            def copy_rows(p, n):
                act.wait_ge(x2T_ps[p], c1(n))
                act.activation(x2T[p][:, :], bank(p, 1, 128, 0, N), ACT.Identity).then_inc(x2T_ready[p], 1)

            def copy_logits(p, n):
                act.wait_ge(lg_ps[p], c1(n))
                act.activation(lg[p][:, :, :], bank(p, 1, HALF, 0, 2 * E).rearrange("p (t e) -> p t e", t=2),
                               ACT.Identity).then_inc(lg_ready[p], 1)

            def spread_keys(p, a, n):
                for j in range(4):
                    ins = act.activation(keys[p][32 * j:32 * j + 32, j, :, :], qk[p][32 * j:32 * j + 32, 2:4, :], ACT.Identity)
                ins.then_inc(keys_ready[p], 1)

            def half(light, heavy, more=True):
                lp, la, lnum = light
                if heavy:
                    hp, ha, hn = heavy
                    exponentials(hp, ha, hn, 0, 0)
                if la == 0 and more:
                    copy_turned(lp, 0, lnum)
                if heavy:
                    exponentials(hp, ha, hn, 0, 1)
                    exponentials(hp, ha, hn, 1, 0)
                if la == 1:
                    copy_turned(lp, 1, lnum)
                if heavy:
                    exponentials(hp, ha, hn, 1, 1)
                    if ha == 0 and not first(hn):
                        copy_rows(hp, hn - 1)
                if la == 1:
                    act.wait_ge(qkv_ps[lp], lnum * 3 + 3)
                    act.activation(qkb[lp][:, :, :].rearrange("p (b g) n -> p b (g n)", b=2), R[lp][:, 0:2, 0:2 * N],
                                   ACT.Identity).then_inc(qkb_ready[lp], 1)
                    act.activation(qk[lp][:, 0:2, :], bank(lp, 0, 128, 0, 2 * N), ACT.Identity).then_inc(qk_copied[lp], 1)
                    act.activation(qk[lp][:, 2:4, :], bank(lp, 1, 128, 0, 2 * N), ACT.Identity, bias=onerow[:, 0:1]
                                   ).then_inc(qk_copied[lp], 1)
                    act.activation(va[lp][:, :, :, 0:HD],
                                   ps[0:HALF, 4 * lp:4 * lp + 2, 2 * N:2 * N + H].rearrange("p t (h d) -> p t h d", d=HD),
                                   ACT.Identity).then_inc(v_ready1[lp], 1)
                    act.wait_ge(qk_copied[lp], lnum * 2 + 2)
                    spread_keys(lp, 1, lnum)
                elif more:
                    act.wait_ge(qk_roped[lp], c1(lnum))
                    spread_keys(lp, 0, lnum)
                if heavy and ha == 0 and not first(hn):
                    copy_logits(hp, hn - 1)
                    act.wait_ge(idx_ready[hp], c1(hn - 1))
                    act.activation(e2[hp][:, :], dif[hp][:, :], ACT.Exp).then_inc(e2_ready[hp], 1)

            def tail(n):
                for p in range(2):
                    copy_rows(p, n)
                for p in range(2):
                    copy_logits(p, n)
                for p in range(2):
                    act.wait_ge(idx_ready[p], c1(n))
                    act.activation(e2[p][:, :], dif[p][:, :], ACT.Exp).then_inc(e2_ready[p], 1)

            schedule(act, half, tail)

            def hidden(m, p):
                for f in range(FC):
                    act.wait_ge(h_ps, m * 8 + (4 * p + f + 1))
                    act.activation(hT[p][:, f, :].rearrange("p (g n) -> p g n", g=2),
                                   ps[:, 2 + 2 * (f % 2):4 + 2 * (f % 2), 0:CAP // 2], ACT.Gelu_apprx_tanh,
                                   bias=b1c[:, bass.ds(m * 2 + p, 1), f]).then_inc(gelu_done, 1)

            expert_order(act, lambda m, p: None, hidden, lambda m, p: None)

            for p in range(2):
                act.wait_ge(ey_out[p], 96 * (E // 2) + 16)
            with act.Fori(0, B // 2) as it:
                for p in range(2):
                    act.wait_ge(fin_ready, it * 2 + 1)
                    act.dma_start(yl[p][:, :, :, :], choice_y.rearrange("(b t q k) c -> b q t k c", t=2, q=HALF, k=2)[
                        bass.ds(it * 2 + p, 1)].rearrange("b q t k c -> (b q) t k c")).then_inc(yl_in[p], 16)

        @block.gpsimd
        def _(pool):
            pool.memset(mhalf[:, :], -0.5)
            pool.iota(iota[:, :], [[1, E]], base=0, channel_multiplier=0, allow_small_or_imprecise_dtypes=True
                      ).then_inc(iota_done, 1)
            pool.wait_ge(iota_done, 1)
            settled(pool)
            for n, s in enumerate([tok_out, *ey_out]):
                pool.dma_start(scratch[n:n + 1, :], iota[0:1, :]).then_inc(s, 16)
            with pool.Fori(0, 4) as it:
                pool.wait_ge(tok_mv, it + 1)
                settled(pool)
                pool.tensor_scalar(tve[:, :], tmv[:, :, 1], EPS, None, ALU.add).then_inc(tok_step, 1)
                pool.wait_ge(tok_step, it * 2 + 1)
                pool.tensor_tensor(trs[:, :], tve[:, :], mhalf[0:2 * IMG, 0:8], ALU.pow).then_inc(tok_rs, 1)
                pool.wait_ge(tok_norm, it + 1)
                settled(pool)
                g = lng[:, None, :].broadcast_to([2 * IMG, 8, H])
                b = lnb[:, None, :].broadcast_to([2 * IMG, 8, H])
                pool.tensor_tensor(tok2[:, :, :], tok[:, :, :], g, ALU.mult).then_inc(tok_step, 1)
                pool.wait_ge(tok_step, it * 2 + 2)
                pool.tensor_tensor(tok[:, :, :], tok2[:, :, :], b, ALU.add).then_inc(tok_ready, 1)
                pool.wait_ge(tok_ready, it + 1)
                settled(pool)
                pool.dma_start(tokens[bass.ds(it * GRP, GRP), :, :].rearrange("(q b) n c -> (b n) q c", b=2),
                               tok[:, :, :]).then_inc(tok_out, 16)
                pool.wait_ge(tok_out, it * 16 + 32)
            pool.wait_ge(zeros_out, 16 * FILLS)
            settled(pool)

            def deviations(l, p, n):
                pool.wait_ge(mv_ready[l][p], c1(n))
                settled(pool)
                if l == 1:
                    pool.tensor_scalar(ve[l][p][:, :, 1], mv[l][p][:, :, 1], 1.0 + EPS, EPS * EPS, ALU.mult, ALU.add)
                w = 1 + (l == 1)
                pool.tensor_scalar(ve[l][p][:, :, 0], mv[l][p][:, :, 1], EPS, None, ALU.add).then_inc(ve_ready[l][p], 1)
                pool.wait_ge(ve_ready[l][p], c1(n))
                pool.tensor_tensor(rs[l][p][:, :, 0:w], ve[l][p][:, :, 0:w],
                                   mhalf[0:HALF, 0:4].rearrange("p (a b) -> p a b", a=2)[:, :, 0:w], ALU.pow
                                   ).then_inc(rs_ready[l][p], 1)

            def normalize(l, p, n, src, out, done):
                pool.wait_ge(rs_ready[l][p], c1(n))
                settled(pool)
                for t in range(2):
                    ins = pool.tensor_scalar(out[p][:, t, :], src[p][:, t, :], mv[l][p][:, t, 0:1], rs[l][p][:, t, 0:1],
                                             ALU.subtract, ALU.mult)
                ins.then_inc(done[p], 1)

            def expert_rows(p, n):
                pool.wait_ge(h_ready[p], c2(n, 1))
                pool.tensor_tensor(resid[:, bass.ds(n * 4 + 2 * p, 2), :], h1[p][:, :, :], xm[p][:, :, :], ALU.add
                                   ).then_inc(resid_ready[p], 1)
                deviations(2, p, n)
                normalize(2, p, n, xm, xh2, xh2_step)
                pool.wait_ge(xh2_step[p], n * 2 + 1)
                pool.tensor_tensor(xh2[p][:, :, :], xh2[p][:, :, :], g2r[:, None, :].broadcast_to([HALF, 2, H]),
                                   ALU.mult).then_inc(xh2_step[p], 1)
                if not first(n):
                    pool.wait_ge(scat_out[p], n * 64)
                    settled(pool)
                pool.tensor_scalar(x2[p][:, :, :, H], x2[p][:, :, :, H], float(4 * N), None, ALU.add)
                pool.wait_ge(xh2_step[p], n * 2 + 2)
                pool.tensor_tensor(x2[p][:, :, :, 0:H], xh2[p][:, :, None, :].broadcast_to([HALF, 2, 2, H]),
                                   be2r[:, None, None, :].broadcast_to([HALF, 2, 2, H]), ALU.add).then_inc(x2_ready[p], 1)

            def scatter(p, n):
                pool.wait_ge(scu_ready[p], c1(n))
                settled(pool)
                for t in range(2):
                    for k in range(2):
                        pool.indirect_dma_start(slots_x[:, :], bass.IndirectOffsetOnAxis(ap=scu[p][:, t, k:k + 1], axis=0),
                                                x2[p][:, t, k, :], None, bounds_check=SLOTS - 1, oob_is_err=False
                                                ).then_inc(scat_out[p], 16)

            def half(light, heavy, more=True):
                lp, la, lnum = light
                next_image = heavy and heavy[1] == 1 and not (isinstance(heavy[2], int) and heavy[2] == B // 2 - 1)
                if la == 1:
                    deviations(1, lp, lnum)
                if next_image:
                    deviations(0, heavy[0], heavy[2] + 1)
                if la == 1:
                    normalize(1, lp, lnum, h1, xin, xin_ready)
                    if not first(lnum):
                        scatter(lp, lnum - 1)
                else:
                    if more:
                        pool.wait_ge(rope_sum[lp], c1(lnum))
                        pool.tensor_tensor(qk[lp][:, :, :], rt[lp][:, 0:4, :], ropeb[:, :, :], ALU.add
                                           ).then_inc(qk_roped[lp], 1)
                    if not first(lnum):
                        expert_rows(lp, lnum - 1)

            def tail(n):
                expert_rows(1, n)
                for p in range(2):
                    scatter(p, n)

            for p in range(2):
                pool.iota(x2[p][:, :, :, H], [[2 * HALF, 2], [1, 2]], base=2 * N * p + 1 - 4 * N, channel_multiplier=2,
                          allow_small_or_imprecise_dtypes=True).then_inc(iota_done, 1)
            pool.wait_ge(iota_done, 3)
            for p in range(2):
                deviations(0, p, 0)
            schedule(pool, half, tail)

            with pool.Fori(0, E // 2) as it:
                for p in range(2):
                    pool.wait_ge(ey_ready, n2(it, p) + 1)
                    settled(pool)
                    for c in range(MAIN + 1):
                        m = 128 if c < MAIN else TAIL
                        pool.indirect_dma_start(choice_y[:, :], bass.IndirectOffsetOnAxis(ap=eu[p][0:m, c:c + 1], axis=0),
                                                ey[p][0:m, c, :], None, bounds_check=CHOICES - 1, oob_is_err=False
                                                ).then_inc(ey_out[p], 16)

        @block.vector
        def _(dve):
            for s in (patch_sb, tok_sb, patch_rows, eT_ready, ey_ready, fin_ready,):
                dve.sem_inc(s, 1)
            dve.memset(hT[0][:, :, :], 0.0).then_inc(zero_ready, 1)
            dve.memset(gpad[:, :, :, :], 0.0)
            dve.memset(allb[:, :], 1.0)
            dve.memset(taken[0][:, :], 0.0).then_inc(taken_ready, 1)
            for p in range(2):
                dve.memset(bank(p, 0, 128, 2 * N, 32 * BLOCKS), 1.0)
                dve.memset(keys[p][:, :, :, :], 0.0)
                dve.memset(mx[p][:, :, :], 0.0)
                dve.memset(va[p][:, :, :, HD:32], 1.0)
            dve.memset(dif[0][:, :], 0.0).then_inc(memset_done, 1)
            dve.wait_ge(consts_in, CONSTS)
            dve.tensor_copy(trib[:, :], trif[:, :]).then_inc(trib_ready, 1)
            for g in range(4):
                dve.tensor_scalar(ropeb[:, g, :], ropet[:, g, :], bqk0[:, g:g + 1], None, ALU.mult)
                dve.tensor_scalar(rt[0][:, g, :], ropet[:, 4 + g, :], bqk0[:, 4 + g:5 + g], onerow[:, 0:1] if g >= 2 else 0.0,
                                  ALU.mult, ALU.add).then_inc(ropeb_step, 1)
            dve.wait_ge(ropeb_step, 4)
            dve.tensor_tensor(ropeb[:, :, :], ropeb[:, :, :], rt[0][:, 0:4, :], ALU.add).then_inc(ropeb_step, 1)

            with dve.Fori(0, 2) as it:
                for i in range(2):
                    dve.wait_ge(xs_in[i], it * (16 * GRP) + 16 * GRP)
                    dve.wait_ge(patch_ps, it * 12 + 6 * i + 1)
                    for j in range(NP):
                        ins = dve.tensor_copy(xr[:, j, :].rearrange("p (c w) -> p c w", w=16),
                                              xs[i][:, :, :, 16 * j:16 * j + 16].rearrange("p c y w -> p (c y) w"))
                    ins.then_inc(patch_rows, 1)
                    for k in range(6):
                        dve.wait_ge(patch_ps, it * 12 + (6 * i + k + 1) + 1)
                        if k < 2:
                            dve.wait_ge(emb_ps, it * 2 + i + 1)
                        dve.tensor_copy(xT[k % 2][:, :, :], ps[:, 0:2, 0:288]).then_inc(patch_sb, 1)
                    dve.wait_ge(tok_ps, it * 2 + (i + 1) + 1)
                    dve.wait_ge(tok_out, it * 32 + (16 * i + 16))
                    dve.tensor_copy(tok[:, :, :].rearrange("p (g q) c -> p g (q c)", g=2), ps[0:2 * IMG, 6:8, :]
                                    ).then_inc(tok_sb, 1)
                    dve.wait_ge(tok_sb, it * 2 + (i + 1) + 1)
                    for q in range(8):
                        ins = dve.bn_stats(tstat[:, q, :], tok[:, q, :])
                    ins.then_inc(tok_stat, 1)
                    dve.wait_ge(tok_stat, it * 2 + (i + 1))
                    settled(dve)
                    for q in range(8):
                        ins = dve.bn_aggr(tmv[:, q, :], tstat[:, q, :])
                    ins.then_inc(tok_mv, 1)
                    dve.wait_ge(tok_rs, it * 2 + (i + 1))
                    for q in range(8):
                        ins = dve.tensor_scalar(tok[:, q, :], tok[:, q, :], tmv[:, q, 0:1], trs[:, q:q + 1],
                                                ALU.subtract, ALU.mult)
                    ins.then_inc(tok_norm, 1)

            dve.wait_ge(iota_done, 1)

            def statistics(l, p, n, src):
                for t in range(2):
                    ins = dve.bn_stats(stat[l][p][:, t, :], src[p][:, t, :])
                ins.then_inc(stat_done[l][p], 1)
                dve.wait_ge(stat_done[l][p], c1(n))
                settled(dve)
                for t in range(2):
                    ins = dve.bn_aggr(mv[l][p][:, t, :], stat[l][p][:, t, :])
                ins.then_inc(mv_ready[l][p], 1)

            def normalize(l, p, n, src, c, out, done):
                dve.wait_ge(rs_ready[l][p], c1(n))
                for t in range(2):
                    ins = dve.tensor_scalar(out[p][:, t, :], src[p][:, t, :], mv[l][p][:, t, 0:1], rs[l][p][:, t, c:c + 1],
                                            ALU.subtract, ALU.mult)
                ins.then_inc(done[p], 1)

            def add_residual(p, a, n):
                dve.wait_ge(y_ps[p], c2(n, a))
                if a == 1:
                    dve.wait_ge(xin_ready[p], c1(n))
                    if not first(n):
                        dve.wait_ge(resid_ready[p], c1(n - 1))
                        dve.wait_ge(xh2_step[p], n * 2)
                dve.tensor_tensor((h1 if a == 0 else xm)[p][:, :, :],
                                  bank(p, 2, HALF, 0, 2 * H).rearrange("p (t c) -> p t c", t=2),
                                  (hin if a == 0 else xin)[p][:, :, :], ALU.add).then_inc(h_ready[p], 1)
                dve.wait_ge(h_ready[p], c2(n, a))

            def maxima(p, a, n, s, i):
                dve.wait_ge(sm_ps[p], c8(n, a, s, i))
                b = 2 - 2 * i
                dve.tensor_reduce(mx[p][:, s, :].rearrange("p (g j r) -> p j g r", g=2, j=4)[:, b:b + 2, :, HD],
                                  R[p][0:HALF, b:b + 2, 0:2 * N].rearrange("p b (g n) -> p b g n", g=2),
                                  AX.X, ALU.max, negate=True).then_inc(max_done[p], 1)

            def top_two(p, n):
                dve.wait_ge(lg_ready[p], c1(n))
                settled(dve)
                for t in range(2):
                    ins = dve.max(v8[p][:, t, :], lg[p][:, t, :])
                ins.then_inc(top_step[p], 1)
                dve.wait_ge(top_step[p], n * 3 + 1)
                settled(dve)
                for t in range(2):
                    dve.max_index(i8[p][:, t, :], v8[p][:, t, :], lg[p][:, t, :])
                dve.tensor_tensor(dif[p][:, :], v8[p][:, :, 1], v8[p][:, :, 0], ALU.subtract).then_inc(idx_ready[p], 1)
                dve.wait_ge(idx_ready[p], c1(n))
                dve.tensor_copy(ix[p][:, :, :], i8[p][:, :, 0:2]).then_inc(top_step[p], 1)
                dve.wait_ge(top_step[p], n * 3 + 2)
                dve.tensor_tensor(oh[p][:, :, :, :].rearrange("p t k e -> p (t k) e"),
                                  iota[:, None, :].broadcast_to([HALF, 4, E]),
                                  ix[p][:, :, :].rearrange("p t k -> p (t k)")[:, :, None].broadcast_to([HALF, 4, E]),
                                  ALU.is_equal).then_inc(top_step[p], 1)
                dve.wait_ge(top_step[p], n * 3 + 3)
                dve.tensor_tensor(ohs[p][:, :, :], oh[p][:, :, 0, :], oh[p][:, :, 1, :], ALU.add).then_inc(ohs_ready[p], 1)

            def read_counts(p, n):
                dve.wait_ge(cnt_ps[p], c1(n))
                dve.wait_ge(taken_ready, n * 2 + (p + 1))
                dve.tensor_tensor(before[p][:, :, :], bank(p, 1, HALF, 0, 2 * E).rearrange("p (t e) -> p t e", t=2),
                                  taken[p][:, None, :].broadcast_to([HALF, 2, E]), ALU.add)
                dve.tensor_tensor(taken[1 - p][:, :], bank(p, 1, HALF, 2 * E, 3 * E), taken[p][:, :], ALU.add
                                  ).then_inc(cnt_read[p], 1)
                dve.wait_ge(cnt_read[p], c1(n))
                dve.sem_inc(taken_ready, 1)

            def find_slots(p, n):
                dve.tensor_tensor(sel[p][:, :, :, :], before[p][:, :, None, :].broadcast_to([HALF, 2, 2, E]),
                                  oh[p][:, :, :, :], ALU.mult).then_inc(slot_step[p], 1)
                dve.wait_ge(slot_step[p], n * 4 + 1)
                dve.tensor_reduce(pos[p][:, :, :], sel[p][:, :, :, :], AX.X, ALU.add).then_inc(slot_step[p], 1)
                dve.wait_ge(slot_step[p], n * 4 + 2)
                dve.tensor_scalar(keep[p][:, :, :], pos[p][:, :, :], float(CAP), None, ALU.is_lt)
                dve.tensor_scalar(mnp[p][:, :, :], pos[p][:, :, :], float(CAP - 1), None, ALU.min).then_inc(slot_step[p], 1)
                dve.wait_ge(slot_step[p], n * 4 + 3)
                dve.scalar_tensor_tensor(slf[p][:, :, :], ix[p][:, :, :], float(CAP), mnp[p][:, :, :], ALU.mult, ALU.add)
                dve.tensor_scalar(off[p][:, :, :], keep[p][:, :, :], -BIG, BIG, ALU.mult, ALU.add).then_inc(slot_step[p], 1)
                dve.wait_ge(slot_step[p], n * 4 + 4)
                if not first(n):
                    dve.wait_ge(scat_out[p], n * 64)
                dve.tensor_tensor(scu[p][:, :, :], slf[p][:, :, :], off[p][:, :, :], ALU.add).then_inc(scu_ready[p], 1)
                dve.wait_ge(e2_ready[p], c1(n))
                dve.tensor_scalar(gt[p][:, :, 1], e2[p][:, :], 1.0, None, ALU.add).then_inc(gate_step[p], 1)
                dve.wait_ge(gate_step[p], n * 3 + 1)
                dve.reciprocal(gt[p][:, :, 0], gt[p][:, :, 1]).then_inc(gate_step[p], 1)
                dve.wait_ge(gate_step[p], n * 3 + 2)
                dve.tensor_tensor(gt[p][:, :, 1], gt[p][:, :, 0], e2[p][:, :], ALU.mult).then_inc(gate_step[p], 1)
                dve.wait_ge(gate_step[p], n * 3 + 3)
                dve.tensor_tensor(gate[:, bass.ds(n * 8 + 4 * p, 4)], gt[p][:, :, :].rearrange("p t k -> p (t k)"),
                                  keep[p][:, :, :].rearrange("p t k -> p (t k)"), ALU.mult).then_inc(gate_done[p], 1)

            def denominators(p, a, n):
                dve.wait_ge(o_ps[p], c2(n, a))
                dve.transpose(sums[p][:, :, :].rearrange("p b c -> p (b c)"), bank(p, 0, 128, 0, 32 * BLOCKS)
                              ).then_inc(den_step[p], 1)

            def reciprocals(p, a, n):
                dve.wait_ge(den_step[p], n * 6 + (3 * a + 1))
                dve.reciprocal(inv[p][:, :], sums[p][:, :, HD]).then_inc(den_step[p], 1)
                dve.wait_ge(den_step[p], n * 6 + (3 * a + 2))
                dve.transpose(rc[p][:, :], inv[p][:, :, None].broadcast_to([128, BLOCKS, 32])).then_inc(den_step[p], 1)

            def start_image(p, n):
                dve.wait_ge(hin_in[p], n * 48 + 48)
                statistics(0, p, n, hin)
                normalize(0, p, n, hin, 0, xh, xh_ready)

            def rotate(p, n):
                for m in range(2):
                    dve.wait_ge(qkv_ps[p], n * 3 + (m + 1))
                    dve.tensor_tensor(rt[p][:, 4 * m:4 * m + 4, :].rearrange("p (b g) n -> p b (g n)", b=2),
                                      R[p][:, 2 * m:2 * m + 2, 0:2 * N],
                                      ropet[:, 4 * m:4 * m + 4, :].rearrange("p (b g) n -> p b (g n)", b=2), ALU.mult
                                      ).then_inc(rope_mul[p], 1)
                dve.wait_ge(rope_mul[p], n * 2 + 2)
                dve.tensor_tensor(rt[p][:, 0:4, :], rt[p][:, 0:4, :], rt[p][:, 4:8, :], ALU.add).then_inc(rope_sum[p], 1)
                dve.wait_ge(rope_sum[p], c1(n))
                dve.tensor_tensor(qkb[p][:, :, :], rt[p][:, 0:4, :], ropeb[:, :, :], ALU.add).then_inc(qkb_ready[p], 1)
                dve.tensor_tensor(va[p][:, :, :, 0:HD],
                                  ps[0:HALF, 4 * p:4 * p + 2, 2 * N:2 * N + H].rearrange("p t (h d) -> p t h d", d=HD),
                                  bv0[:, :].rearrange("p (h d) -> p h d", d=HD)[:, None, :, :].broadcast_to([HALF, 2, NH, HD]),
                                  ALU.add).then_inc(v_ready0[p], 1)

            def weighted_means(p, a, n):
                dve.wait_ge(den_step[p], n * 6 + (3 * a + 3))
                dve.tensor_tensor(oT[p][:, :, :].rearrange("p g n -> p (g n)"), bank(p, 0, 128, 0, 2 * N), rc[p][:, 0:2 * N],
                                  ALU.mult).then_inc(oT_ready[p], 1)

            def half(light, heavy, more=True):
                lp, la, lnum = light
                next_image = heavy and heavy[1] == 1 and not (isinstance(heavy[2], int) and heavy[2] == B // 2 - 1)
                if la == 1:
                    add_residual(lp, 0, lnum)
                    statistics(1, lp, lnum, h1)
                    normalize(1, lp, lnum, h1, 1, xh, xh_ready)
                    if next_image:
                        start_image(heavy[0], heavy[2] + 1)
                    if not first(lnum):
                        read_counts(lp, lnum - 1)
                        find_slots(lp, lnum - 1)
                else:
                    if next_image:
                        start_image(heavy[0], heavy[2] + 1)
                    if not first(lnum):
                        add_residual(lp, 1, lnum - 1)
                        statistics(2, lp, lnum - 1, xm)
                    if more:
                        rotate(lp, lnum)
                if heavy:
                    denominators(*heavy)
                if more:
                    for s in range(2):
                        for i in range(2):
                            maxima(lp, la, lnum, s, i)
                if heavy:
                    reciprocals(*heavy)
                if more:
                    dve.wait_ge(mT_ps[lp], c2(lnum, la))
                    if la == 0:
                        dve.wait_ge(qk_roped[lp], c1(lnum))
                    dve.tensor_tensor(qm[lp][:, :, :], qk[lp][:, 0:2, :],
                                      bank(lp, 0, 128, 0, 2 * N).rearrange("p (g n) -> p g n", g=2), ALU.add
                                      ).then_inc(qm_ready[lp], 1)
                if heavy:
                    weighted_means(*heavy)
                if heavy and heavy[1] == 0 and not first(heavy[2]):
                    top_two(heavy[0], heavy[2] - 1)

            def tail(n):
                add_residual(1, 1, n)
                statistics(2, 1, n, xm)
                for p in range(2):
                    top_two(p, n)
                for p in range(2):
                    read_counts(p, n)
                    find_slots(p, n)

            for p in range(2):
                dve.wait_ge(hin_in[p], 48)
                statistics(0, p, 0, hin)
            for p in range(2):
                normalize(0, p, 0, hin, 0, xh, xh_ready)
            schedule(dve, half, tail)

            def copy_slots(m, p):
                dve.wait_ge(eT_ps, n2(m, p))
                dve.tensor_copy(eT[p][:, 0:512], ps[:, 0, :])
                dve.tensor_copy(eT[p][:, 512:CAP], ps[:, 1, 0:CAP - 512]).then_inc(eT_ready, 1)
                dve.wait_ge(first_in[p], m * 48 + 48)
                dve.tensor_copy(number[p][:, 0:MAIN], ex[p][:, :, H])
                dve.tensor_copy(number[p][0:TAIL, MAIN:], ext[p][:, H:]).then_inc(rows_used, 1)

            def destinations(m, p):
                dve.wait_ge(rows_used, n2(m, p))
                dve.wait_ge(ey_out[p], m * 96 + 16)
                dve.tensor_scalar(em[p][:, 0:MAIN], number[p][:, 0:MAIN], 0.5, BIG, ALU.is_lt, ALU.mult)
                dve.tensor_scalar(em[p][0:TAIL, MAIN:], number[p][0:TAIL, MAIN:], 0.5, BIG, ALU.is_lt, ALU.mult
                                  ).then_inc(em_ready, 1)
                dve.wait_ge(em_ready, n2(m, p))
                dve.scalar_tensor_tensor(eu[p][:, 0:MAIN], number[p][:, 0:MAIN], -1.0, em[p][:, 0:MAIN], ALU.add, ALU.add)
                dve.scalar_tensor_tensor(eu[p][0:TAIL, MAIN:], number[p][0:TAIL, MAIN:], -1.0, em[p][0:TAIL, MAIN:],
                                         ALU.add, ALU.add)

            def results(m, p):
                dve.wait_ge(ey_ps, n2(m, p))
                dve.wait_ge(second_in[p], m * 32 + 32)
                bb = b2s[p][:, None, :]
                dve.tensor_tensor(ey[p][:, 0:4, :], ps[:, 6, :].rearrange("p (c h) -> p c h", c=4),
                                  bb.broadcast_to([128, 4, H]), ALU.add)
                dve.tensor_tensor(ey[p][:, 4, :], ps[:, 7, 0:H], b2s[p][:, :], ALU.add)
                dve.tensor_tensor(ey[p][0:TAIL, 5, :], ps[0:TAIL, 7, H:2 * H], b2s[p][0:TAIL, :], ALU.add
                                  ).then_inc(ey_ready, 1)

            expert_order(dve, copy_slots, destinations, results)

            for p in range(2):
                dve.wait_ge(gate_done[p], B // 2)
            with dve.Fori(0, B // 2) as it:
                for p in range(2):
                    dve.wait_ge(yl_in[p], it * 16 + 16)
                    dve.wait_ge(fin_out[p], it * 16 + 16)
                    for t in range(2):
                        ins = dve.scalar_tensor_tensor(tmpd[p][:, t, :], yl[p][:, t, 0, :],
                                                       gate[:, bass.ds(it * 8 + (4 * p + 2 * t), 1)],
                                                       resid[:, bass.ds(it * 4 + (2 * p + t), 1), :].rearrange("p o c -> p (o c)"),
                                                       ALU.mult, ALU.add)
                    ins.then_inc(fin_step, 1)
                for p in range(2):
                    dve.wait_ge(fin_step, n2(it, p))
                    for t in range(2):
                        ins = dve.scalar_tensor_tensor(fin[p][:, t, :], yl[p][:, t, 1, :],
                                                       gate[:, bass.ds(it * 8 + (4 * p + 2 * t + 1), 1)], tmpd[p][:, t, :],
                                                       ALU.mult, ALU.add)
                    ins.then_inc(fin_ready, 1)


def host_layout(i):
    import numpy as np

    f = {k: np.asarray(v) for k, v in i.items()}
    a = {"x": f["x"], "txt": f["txt"]}
    w = np.zeros((3, 16, 16, H), np.float32)
    w[..., 0:64] = f["L0_tok_W_main"].reshape(64, 3, 16, 16).transpose(1, 2, 3, 0)
    sx = f["L0_tok_W_sx"].reshape(16, 3, 16, 16).transpose(1, 2, 3, 0)
    sy = f["L0_tok_W_sy"].reshape(16, 3, 16, 16).transpose(1, 2, 3, 0)
    w[:, :, 8:, 64:80] = sx[:, :, :8]
    w[:, :, :8, 80:96] = sx[:, :, 8:]
    w[:, 8:, :, 96:112] = sy[:, :8]
    w[:, :8, :, 112:128] = sy[:, 8:]
    a["w_tok"] = w.reshape(768, H)
    a["b_tok"] = np.concatenate([f["L0_tok_b_main"], f["L0_tok_b_sx"], f["L0_tok_b_sx"], f["L0_tok_b_sy"],
                                 f["L0_tok_b_sy"]])[:, None]
    a["ln_g"], a["ln_b"] = f["L0_tok_ln_g"][None], f["L0_tok_ln_b"][None]
    moves = np.zeros((4, H, H), np.float32)
    for s, (src, dst) in enumerate([(80, 64), (64, 80), (112, 96), (96, 112)]):
        for c in range(16):
            moves[s, src + c, dst + c] = 1
    a["moves"] = moves
    a["ident_d"] = np.eye(128, dtype=np.float32)
    before = np.triu(np.ones((HALF, HALF), np.float32), 1)
    a["tri"] = before
    freqs = np.float32(1.0) / np.float32(10000.0) ** (np.arange(0, HD, 2, dtype=np.float32) / np.float32(HD))
    ang = np.outer(np.arange(N, dtype=np.float32), freqs).astype(np.float32)
    cos, sin = np.cos(ang).T, np.sin(ang).T
    rope = np.zeros((128, 8, N), np.float32)
    for j in range(4):
        for d in range(HD):
            rope[32 * j + d, 0:4] = cos[d // 2]
            rope[32 * j + d, 4:8] = sin[d // 2] if d % 2 else -sin[d // 2]
    a["rope"] = rope

    def heads(wt, other=False):
        wt = wt.reshape(wt.shape[0], NH, HD)
        if other:
            wt = wt.reshape(-1, NH, HD // 2, 2)[..., ::-1].reshape(-1, NH, HD)
        o = np.zeros((wt.shape[0], NH, 32), np.float32)
        o[:, :, :HD] = wt
        return o.reshape(-1, 2, 128)

    wq, wk, wv = (f["L0_attn_Wqkv"][n * H:(n + 1) * H].T for n in range(3))
    bq, bk, bv = (f["L0_attn_bqkv"][n * H:(n + 1) * H] for n in range(3))
    a["w_qk0"] = np.concatenate([heads(wq), heads(wk), heads(wq, True), heads(wk, True)], 1)
    a["b_qk0"] = np.concatenate([heads(bq[None]), heads(bk[None]), heads(bq[None], True), heads(bk[None], True)], 1)[0].T
    a["w_v0"], a["b_v0"] = wv, bv[None]

    def heads_in(wt):
        return heads(wt.T).transpose(2, 1, 0)

    a["w_o0"] = heads_in(f["L0_attn_Wproj"].T)
    a["w_o0"][HD, 0] = f["L0_attn_bproj"]
    a["w_qk1"] = np.concatenate([heads(f["L0_ffn_wq"]), heads(f["L0_ffn_wk"])], 1)
    one = np.zeros((128, 1), np.float32)
    one[HD::32] = 1
    a["one_row"] = one
    a["w_v1"], a["w_o1"] = f["L0_ffn_wv"], heads_in(f["L0_ffn_wo"])
    a["g1"], a["be1"] = f["L0_ffn_ln1_g"][:, None], f["L0_ffn_ln1_b"][:, None]
    a["g2"], a["be2"] = f["L0_ffn_ln2_g"][None], f["L0_ffn_ln2_b"][None]
    a["w_r"], a["w1"], a["w2"], a["b2"] = f["L0_ffn_wr"], f["L0_ffn_w1"], f["L0_ffn_w2"], f["L0_ffn_b2"]
    a["b1"] = f["L0_ffn_b1"].reshape(E, 128, FC).transpose(1, 0, 2)
    return {k: np.ascontiguousarray(v) for k, v in a.items()}


_ORDER = ["x", "txt", "w_tok", "b_tok", "ln_g", "ln_b", "moves", "ident_d", "tri", "rope", "w_qk0", "b_qk0",
          "w_v0", "b_v0", "w_o0", "w_qk1", "one_row", "w_v1", "w_o1", "g1", "be1", "g2", "be2", "w_r", "w1", "b1",
          "w2", "b2"]


def kernel(**inputs):
    import concourse.bacc as _bacc
    from concourse import mybir as _mybir
    from concourse.bass_utils import run_bass_kernel_spmd as _run

    nc = _bacc.Bacc("TRN2", target_bir_lowering=False, num_devices=1)
    arrays = {"in_" + k: v for k, v in host_layout(inputs).items()}
    args = [nc.dram_tensor("in_" + k, arrays["in_" + k].shape, _mybir.dt.from_np(arrays["in_" + k].dtype),
                           kind="ExternalInput").ap() for k in _ORDER]
    out = nc.dram_tensor("out", (B, N, H), F32, kind="ExternalOutput").ap()
    program(nc, *args, out)
    r = _run(nc, [arrays], core_ids=[0])
    return r.results[0]["out"]
```

```python
from contextlib import ExitStack

import concourse.bass as bass
from concourse import mybir

F32 = mybir.dt.float32
U32 = mybir.dt.uint32
BF16 = mybir.dt.bfloat16
ALU = mybir.AluOpType
ACT = mybir.ActivationFunctionType
AX = mybir.AxisListType

B = 64
NP = 6
IMG = 36
TXT = 128
N = IMG + TXT
H = 128
HALF = N // 2
NH = 8
HD = H // NH
E = 64
F = 512
FC = F // 128
CAP = 2 * (B * N * 2 // E)
SLOTS = E * CAP
ROW = H + 1
CHOICES = B * N * 2
SCALE = HD ** -0.5
EPS = 1e-5
GRP = 16
BLOCKS = -(-2 * N // 32)
ROWS = GRP * NP
MAIN = CAP // 128
TAIL = CAP - MAIN * 128
BIG = 65536.0


def program(nc, x, txt, w_tok, b_tok, ln_g, ln_b, moves, ident_d, tri, rope, w_qk0, b_qk0, w_v0, b_v0,
            w_o0, w_qk1, one_row, w_v1, w_o1, g1, be1, g2, be2, w_r, w1, b1, w2, b2, out):
    with ExitStack() as ctx:
        def sb(name, shape, dt=F32):
            return ctx.enter_context(nc.sbuf_tensor(name, shape, dt))

        def sem(name):
            return ctx.enter_context(nc.semaphore(name))

        tokens = nc.dram_tensor("tokens", [B, IMG, H], F32).ap()
        slots_x = nc.dram_tensor("slots_x", [SLOTS, ROW], F32).ap()
        scratch = nc.dram_tensor("scratch", [8, E], F32).ap()
        choice_y = nc.dram_tensor("choice_y", [CHOICES, H], F32).ap()

        ps = ctx.enter_context(nc.psum_tensor("ps", [128, 8, 512], F32))

        ident = sb("ident", [128, 128])
        trif = sb("trif", [HALF, HALF])
        trib = sb("trib", [HALF, HALF], BF16)
        allb = sb("allb", [HALF, HALF], BF16)
        movem = sb("movem", [128, 4, 128])
        wtok = sb("wtok", [128, 6, 128])
        btok = sb("btok", [128, 1])
        lng = sb("lng", [2 * IMG, H])
        lnb = sb("lnb", [2 * IMG, H])
        ropet = sb("ropet", [128, 8, N])
        bqk0 = sb("bqk0", [128, 8])
        ropeb = sb("ropeb", [128, 4, N])
        wqk0 = sb("wqk0", [128, 8, 128])
        wv0 = sb("wv0", [128, 128])
        bv0 = sb("bv0", [HALF, H])
        wo0 = sb("wo0", [128, 2, H])
        wqk1 = sb("wqk1", [128, 4, 128])
        onerow = sb("onerow", [128, 1])
        wv1 = sb("wv1", [128, 128])
        wo1 = sb("wo1", [128, 2, H])
        g1c = sb("g1c", [128, 1])
        be1c = sb("be1c", [128, 1])
        g2r = sb("g2r", [HALF, H])
        be2r = sb("be2r", [HALF, H])
        wr = sb("wr", [128, E])
        iota = sb("iota", [HALF, E])
        zeros = sb("zeros", [128, 2 * ROW])
        mhalf = sb("mhalf", [128, 8])
        b1c = sb("b1c", [128, E, FC])

        def two(name, shape, dt=F32):
            return [sb(f"{name}{p}", shape, dt) for p in range(2)]

        hin = two("hin", [HALF, 2, H])
        h1 = two("h1", [HALF, 2, H])
        xin = two("xin", [HALF, 2, H])
        xm = two("xm", [HALF, 2, H])
        xh = two("xh", [HALF, 2, H])
        xh2 = two("xh2", [HALF, 2, H])
        x2 = two("x2", [HALF, 2, 2, ROW])
        ln = range(3)
        stat = [two(f"stat{l}", [HALF, 2, 6]) for l in ln]
        mv = [two(f"mv{l}", [HALF, 2, 2]) for l in ln]
        ve = [two(f"ve{l}", [HALF, 2, 2]) for l in ln]
        rs = [two(f"rs{l}", [HALF, 2, 2]) for l in ln]
        xhT = two("xhT", [128, N])
        x2T = two("x2T", [128, N])
        rt = two("rt", [128, 8, N])
        qk = two("qk", [128, 4, N])
        qkb = two("qkb", [128, 4, N], BF16)
        keys = two("keys", [128, 4, 2, N])
        qm = two("qm", [128, 2, N])
        mx = two("mx", [HALF, 2, NH * 32])
        va = two("va", [HALF, 2, NH, 32])
        big = two("big", [128, FC * CAP])
        pT = [b[0:HALF, :].rearrange("p (s h n) -> p s h n", s=2, h=NH) for b in big]
        hT = [b[:, :].rearrange("p (f c) -> p f c", f=FC) for b in big]
        sums = two("sums", [128, BLOCKS, 32])
        inv = two("inv", [128, BLOCKS])
        rc = two("rc", [128, 32 * BLOCKS])
        oT = two("oT", [128, 2, N])
        lg = two("lg", [HALF, 2, E])
        v8 = two("v8", [HALF, 2, 8])
        i8 = two("i8", [HALF, 2, 8], U32)
        dif = two("dif", [HALF, 2])
        e2 = two("e2", [HALF, 2])
        ix = two("ix", [HALF, 2, 2])
        oh = two("oh", [HALF, 2, 2, E], BF16)
        ohs = two("ohs", [HALF, 2, E], BF16)
        before = two("before", [HALF, 2, E])
        taken = two("taken", [HALF, E])
        sel = two("sel", [HALF, 2, 2, E])
        pos = two("pos", [HALF, 2, 2])
        keep = two("keep", [HALF, 2, 2])
        mnp = two("mnp", [HALF, 2, 2])
        slf = two("slf", [HALF, 2, 2])
        scu = two("scu", [HALF, 2, 2], U32)
        off = two("off", [HALF, 2, 2])
        gt = two("gt", [HALF, 2, 2])

        store = sb("store", [128, 2 * B * H])
        resid = store[0:HALF, :].rearrange("p (t c) -> p t c", c=H)
        gate = sb("gate", [HALF, 2 * B * 2])

        with ExitStack() as early:
            def sa(name, shape):
                return early.enter_context(nc.sbuf_tensor(name, shape, F32))

            xs = [store[0:ROWS, i * 4608:(i + 1) * 4608].rearrange("p (c y w) -> p c y w", c=3, y=16) for i in range(2)]
            xr = store[0:ROWS, 2 * 4608:3 * 4608].rearrange("p (j f) -> p j f", j=NP)
            xT = [sa(f"xT{i}", [128, 2, 288]) for i in range(2)]
            tokT = sa("tokT", [128, 2, 288])
            gpad = sa("gpad", [128, GRP, 8, 8])
            tok = sa("tok", [2 * IMG, 8, H])
            tok2 = sa("tok2", [2 * IMG, 8, H])
            tstat = sa("tstat", [2 * IMG, 8, 6])
            tmv = sa("tmv", [2 * IMG, 8, 2])
            tve = sa("tve", [2 * IMG, 8])
            trs = sa("trs", [2 * IMG, 8])

        w1s = two("w1s", [128, F])
        w2s = two("w2s", [128, FC, H])
        b2s = two("b2s", [128, H])
        ex = two("ex", [128, MAIN, ROW])
        ext = two("ext", [TAIL, ROW])
        number = two("number", [128, MAIN + 1])
        em = two("em", [128, MAIN + 1])
        eu = two("eu", [128, MAIN + 1], U32)
        eT = [k[:, :, :, :].rearrange("p j g n -> p (j g n)")[:, 0:CAP] for k in keys]
        ey = [r[:, :, :].rearrange("p g n -> p (g n)")[:, 0:(MAIN + 1) * H].rearrange("p (c h) -> p c h", h=H) for r in rt]

        flat = [b[0:HALF, :] for b in big]
        yl = [f[:, 0:8 * H].rearrange("p (t k c) -> p t k c", t=4, k=2) for f in flat]
        fin = [f[:, 8 * H:12 * H].rearrange("p (t c) -> p t c", t=4) for f in flat]
        tmpd = [f[:, 12 * H:16 * H].rearrange("p (t c) -> p t c", t=4) for f in flat]

        patch_consts_in = sem("patch_consts_in")
        consts_in = sem("consts_in")
        xs_in = [sem(f"xs_in{i}") for i in range(2)]
        memset_done = sem("memset_done")
        iota_done = sem("iota_done")
        tables_step = sem("tables_step")
        slots_zeroed = sem("slots_zeroed")
        choices_zeroed = sem("choices_zeroed")
        patch_rows = sem("patch_rows")
        patch_ps = sem("patch_ps")
        patch_sb = sem("patch_sb")
        emb_ps = sem("emb_ps")
        emb_sb = sem("emb_sb")
        tokT_ps = sem("tokT_ps")
        tokT_sb = sem("tokT_sb")
        tok_ps = sem("tok_ps")
        tok_sb = sem("tok_sb")
        tok_stat = sem("tok_stat")
        tok_mv = sem("tok_mv")
        tok_step = sem("tok_step")
        tok_rs = sem("tok_rs")
        tok_norm = sem("tok_norm")
        tok_ready = sem("tok_ready")
        tok_out = sem("tok_out")

        waits_passed = sem("waits_passed")

        def sems(name):
            return [sem(f"{name}{p}") for p in range(2)]

        hin_in = sems("hin_in")
        stat_done = [sems(f"stat_done_{l}") for l in ln]
        mv_ready = [sems(f"mv_ready_{l}") for l in ln]
        ve_ready = [sems(f"ve_ready_{l}") for l in ln]
        rs_ready = [sems(f"rs_ready_{l}") for l in ln]
        xh_ready = sems("xh_ready")
        xin_ready = sems("xin_ready")
        xh2_step = sems("xh2_step")
        xT_ps = sems("xT_ps")
        xT_ready = sems("xT_ready")
        qkv_ps = sems("qkv_ps")
        rope_step = sems("rope_step")
        qk_roped = sems("qk_roped")
        qk_copied = sems("qk_copied")
        qkb_ready = sems("qkb_ready")
        keys_ready = sems("keys_ready")
        v_ready0 = sems("v_ready0")
        v_ready1 = sems("v_ready1")
        sm_ps = sems("sm_ps")
        max_done = sems("max_done")
        mT_ps = sems("mT_ps")
        qm_ready = sems("qm_ready")
        st_ps = sems("st_ps")
        exp_done = sems("exp_done")
        o_ps = sems("o_ps")
        den_step = sems("den_step")
        oT_ready = sems("oT_ready")
        y_ps = sems("y_ps")
        h_ready = sems("h_ready")
        resid_ready = sems("resid_ready")
        x2_ready = sems("x2_ready")
        x2T_ps = sems("x2T_ps")
        x2T_ready = sems("x2T_ready")
        lg_ps = sems("lg_ps")
        lg_ready = sems("lg_ready")
        top_step = sems("top_step")
        idx_ready = sems("idx_ready")
        ohs_ready = sems("ohs_ready")
        e2_ready = sems("e2_ready")
        cnt_ps = sems("cnt_ps")
        taken_ready = sem("taken_ready")
        cnt_read = sems("cnt_read")
        slot_step = sems("slot_step")
        scu_ready = sems("scu_ready")
        gate_step = sems("gate_step")
        gate_done = sems("gate_done")
        scat_out = sems("scat_out")

        first_in = sems("first_in")
        second_in = sems("second_in")
        eT_ps = sem("eT_ps")
        eT_ready = sem("eT_ready")
        h_ps = sem("h_ps")
        gelu_done = sem("gelu_done")
        ey_ps = sem("ey_ps")
        ey_ready = sem("ey_ready")
        em_ready = sem("em_ready")
        rows_used = sem("rows_used")
        ey_out = sems("ey_out")

        yl_in = sems("yl_in")
        fin_step = sem("fin_step")
        fin_ready = sem("fin_ready")
        fin_out = sems("fin_out")

        patch_consts = [
            (ident[:, :], ident_d), (movem[:, :, :], moves.rearrange("s p n -> p s n")),
            (wtok[:, :, :], w_tok.rearrange("(k p) n -> p k n", p=128)), (btok[:, :], b_tok),
            (lng[:, :], ln_g.broadcast_to([2 * IMG, H])), (lnb[:, :], ln_b.broadcast_to([2 * IMG, H])),
        ]
        consts = [
            (trif[:, :], tri), (ropet[:, :, :], rope), (bqk0[:, :], b_qk0),
            (wqk0[:, :, :], w_qk0), (wv0[:, :], w_v0), (bv0[:, :], b_v0.broadcast_to([HALF, H])), (wo0[:, :, :], w_o0),
            (wqk1[:, :, :], w_qk1), (onerow[:, :], one_row), (wv1[:, :], w_v1),
            (wo1[:, :, :], w_o1), (g1c[:, :], g1), (be1c[:, :], be1), (g2r[:, :], g2.broadcast_to([HALF, H])),
            (be2r[:, :], be2.broadcast_to([HALF, H])), (wr[:, :], w_r), (b1c[:, :, :], b1),
        ]

        def c1(n):
            return n + 1

        def c2(n, a):
            return n * 2 + (a + 1)

        def c4(n, a, s):
            return n * 4 + (2 * a + s + 1)

        def c8(n, a, s, half):
            return n * 8 + (4 * a + 2 * s + half + 1)

        def n2(it, p):
            return it * 2 + (p + 1)

        def settled(eng):
            eng.sem_inc(waits_passed, 1)

        R = [ps[:, 4 * p:4 * p + 4, :] for p in range(2)]

        def bank(p, b, rows, c0, c1):
            return ps[0:rows, 4 * p + b, c0:c1]

        def schedule(eng, half, tail):
            last = B // 2 - 1

            def pair(n, more=True):
                half((1, 0, n), (0, 0, n))
                half((0, 1, n), (1, 0, n))
                half((1, 1, n), (0, 1, n))
                half((0, 0, n + 1), (1, 1, n), more)

            half((0, 0, 0), None)
            pair(0)
            with eng.Fori(1, last) as n:
                pair(n)
            pair(last, False)
            tail(last)

        def patch_order(eng, patches, tokens_of):
            last = B // GRP // 2 - 1
            patches(0, 0)
            with eng.Fori(0, last) as m:
                patches(m, 1)
                tokens_of(m, 0)
                patches(m + 1, 0)
                tokens_of(m, 1)
            patches(last, 1)
            tokens_of(last, 0, False)
            tokens_of(last, 1, False)

        def expert_order(eng, turned, first_part, second_part):
            last = E // 2 - 1
            turned(0, 0)
            first_part(0, 0)
            turned(0, 1)
            with eng.Fori(0, last) as m:
                first_part(m, 1)
                turned(m + 1, 0)
                second_part(m, 0)
                first_part(m + 1, 0)
                turned(m + 1, 1)
                second_part(m, 1)
            first_part(last, 1)
            second_part(last, 0)
            second_part(last, 1)

        def first(n):
            return isinstance(n, int) and n == 0

        block = ctx.enter_context(nc.Block())

        @block.sync
        def _(sp):
            for s in fin_out:
                sp.sem_inc(s, 16)
            for dst, src in patch_consts:
                sp.dma_start(dst, src).then_inc(patch_consts_in, 16)

            def load_patches(m, i):
                for b in range(GRP):
                    sp.dma_start(xs[i][b * NP:(b + 1) * NP, :, :, :],
                                 x[bass.ds((m * 2 + i) * GRP + b, 1)].rearrange("b c (i y) w -> (b i) c y w", y=16)
                                 ).then_inc(xs_in[i], 16)

            for i in range(2):
                load_patches(0, i)
            for dst, src in consts:
                sp.dma_start(dst, src).then_inc(consts_in, 16)
            with sp.Fori(0, B // GRP // 2 - 1) as m:
                for i in range(2):
                    sp.wait_ge(patch_rows, n2(m, i) + 1)
                    load_patches(m + 1, i)
            def load_image(p, image):
                sp.dma_start(hin[p][0:IMG, 0, :], tokens[image, :, :].rearrange("o n c -> (o n) c")).then_inc(hin_in[p], 16)
                sp.dma_start(hin[p][IMG:HALF, 0, :], txt[image, 0:HALF - IMG, :].rearrange("o n c -> (o n) c")
                             ).then_inc(hin_in[p], 16)
                sp.dma_start(hin[p][:, 1, :], txt[image, HALF - IMG:TXT, :].rearrange("o n c -> (o n) c")
                             ).then_inc(hin_in[p], 16)

            sp.wait_ge(tok_out, 16 + 16)
            for p in range(2):
                load_image(p, bass.ds(p, 1))
            sp.wait_ge(tok_out, 16 * 4 + 16)
            with sp.Fori(0, B // 2 - 1) as n:
                for p in range(2):
                    sp.wait_ge(h_ready[p], c2(n, 0))
                    load_image(p, bass.ds(n * 2 + (2 + p), 1))

            for p in range(2):
                sp.wait_ge(scat_out[p], 64 * (B // 2))

            def load_slots(p, e):
                rows = slots_x.rearrange("(e s) h -> e s h", s=CAP)[e, :, :]
                sp.dma_start(ex[p][:, :, :], rows[:, 0:MAIN * 128, :].rearrange("o (q c) h -> (o q) c h", c=MAIN)
                             ).then_inc(first_in[p], 16)
                sp.dma_start(ext[p][:, :], rows[:, MAIN * 128:CAP, :].rearrange("o q h -> (o q) h")
                             ).then_inc(first_in[p], 16)

            def load_first(p, e):
                sp.dma_start(w1s[p][:, :], w1[e, :, :].rearrange("o h f -> (o h) f")).then_inc(first_in[p], 16)

            def load_second(p, e):
                sp.dma_start(w2s[p][:, :, :], w2[e, :, :].rearrange("o (q c) h -> (o q) c h", c=FC)).then_inc(second_in[p], 16)
                sp.dma_start(b2s[p][:, :], b2[e, :].broadcast_to([128, H])).then_inc(second_in[p], 16)

            for p in range(2):
                load_slots(p, bass.ds(p, 1))
                load_first(p, bass.ds(p, 1))
                load_second(p, bass.ds(p, 1))

            def follow(m, p):
                sp.wait_ge(rows_used, n2(m, p))
                load_slots(p, bass.ds(m * 2 + (2 + p), 1))
                sp.wait_ge(h_ps, m * 8 + (4 * p + 4))
                load_first(p, bass.ds(m * 2 + (2 + p), 1))

            def follow_second(m, p):
                sp.wait_ge(ey_ready, m * 2 + (p + 2))
                load_second(p, bass.ds(m * 2 + (2 + p), 1))

            last = E // 2 - 2
            follow(0, 0)
            with sp.Fori(0, last) as it:
                follow(it, 1)
                follow_second(it, 0)
                follow(it + 1, 0)
                follow_second(it, 1)
            follow(last, 1)
            follow_second(last, 0)
            follow_second(last, 1)

            with sp.Fori(0, B // 4) as it:
                for p in range(2):
                    sp.wait_ge(fin_ready, n2(it, p) + 2)
                    o = out.rearrange("b (t q) c -> q (b t) c", t=2)
                    sp.dma_start(o[:, bass.ds(it * 8 + 4 * p, 4), :], fin[p][:, :, :]).then_inc(fin_out[p], 16)
            for p in range(2):
                sp.wait_ge(fin_out[p], 16 * (B // 4) + 16)

        @block.tensor
        def _(pe):
            for s in (tokT_ps, tok_ps, patch_ps, emb_ps,):
                pe.sem_inc(s, 1)
            pe.wait_ge(patch_consts_in, 16 * len(patch_consts))
            def patches(m, i):
                def turn_chunk(k):
                    if not (first(m) and i == 0):
                        pe.wait_ge(patch_sb, m * 12 + (6 * i + k))
                        pe.wait_ge(tok_sb, m * 2 + i)
                    elif k > 1:
                        pe.wait_ge(patch_sb, k)
                    for j in range(NP):
                        ins = pe.transpose(ps[:, 6 * (k % 2) + j // 3, (j % 3) * ROWS:(j % 3 + 1) * ROWS],
                                           xr[:, j, k * 128:(k + 1) * 128], ident[0:ROWS, 0:ROWS])
                    ins.then_inc(patch_ps, 1)

                pe.wait_ge(patch_rows, n2(m, i) + 1)
                turn_chunk(0)
                for k in range(6):
                    if k < 5:
                        turn_chunk(k + 1)
                    pe.wait_ge(patch_sb, m * 12 + (6 * i + k + 1) + 1)
                    if k == 0:
                        pe.wait_ge(emb_sb, m * 2 + i + 1)
                    for g in range(2):
                        ins = pe.matmul(ps[:, 2 + g, 0:288], wtok[:, k, :], xT[k % 2][:, g, :],
                                        start=(k == 0), stop=(k == 5))
                ins.then_inc(emb_ps, 1)

            def tokens_of(m, i, more=True):
                pe.wait_ge(emb_sb, m * 2 + (i + 1) + 1)
                pe.wait_ge(tokT_sb, m * 2 + i + 1)
                for g in range(2):
                    for s, (di, dj) in enumerate([(0, 0), (0, 1), (0, -1), (1, 0), (-1, 0)]):
                        ins = pe.matmul(ps[:, 4 + g, 0:288], ident[:, :] if s == 0 else movem[:, s - 1, :],
                                        gpad[:, 8 * g:8 * g + 8, 1 + di:7 + di, 1 + dj:7 + dj],
                                        start=(s == 0), stop=(s == 4))
                ins.then_inc(tokT_ps, 1)
                pe.wait_ge(tokT_sb, m * 2 + (i + 1) + 1)
                pe.wait_ge(tok_sb, m * 2 + i + 1)
                for q in range(GRP // 2):
                    ins = pe.transpose(ps[0:2 * IMG, 6 + q // 4, (q % 4) * 128:(q % 4 + 1) * 128],
                                       tokT[:, q // 4, (q % 4) * 72:(q % 4 + 1) * 72], ident[:, :])
                ins.then_inc(tok_ps, 1)

            patch_order(pe, patches, tokens_of)

            pe.wait_ge(memset_done, 1)
            pe.wait_ge(tables_step, 6)
            pe.wait_ge(consts_in, 16 * len(consts))
            pe.wait_ge(tok_sb, 4 + 1)

            def turn(p, b, src, done):
                for t in range(2):
                    ins = pe.transpose(bank(p, b, 128, HALF * t, HALF * (t + 1)), src[:, t], ident[0:HALF, 0:HALF])
                ins.then_inc(done, 1)

            def scores(p, a, n, s, half):
                if s == 0:
                    pe.wait_ge(keys_ready[p], c2(n, a))
                    pe.wait_ge(qm_ready[p], c2(n, a))
                else:
                    pe.wait_ge(exp_done[p], c8(n, a, 0, half))
                for g in range(2):
                    for j in (2 * half, 2 * half + 1):
                        ins = pe.matmul(bank(p, j, HALF, g * N, (g + 1) * N), keys[p][:, j, g, s * HALF:(s + 1) * HALF],
                                        qm[p][:, g, :], start=True, stop=True)
                ins.then_inc(st_ps[p], 1)

            def project(p, a, n):
                pe.wait_ge(xT_ready[p], c2(n, a))
                if not first(n) and a == 1:
                    pe.wait_ge(cnt_read[p], c1(n - 1))
                for g in range(4):
                    pe.matmul(bank(p, g // 2, 128, (g % 2) * N, (g % 2 + 1) * N), (wqk0 if a == 0 else wqk1)[:, g, :],
                              xhT[p][:, :], start=True, stop=True)
                for t in range(2):
                    ins = pe.matmul(bank(p, t, HALF, 2 * N, 2 * N + H), xhT[p][:, t * HALF:(t + 1) * HALF],
                                    (wv0 if a == 0 else wv1)[:, :], start=True, stop=True)
                ins.then_inc(qkv_ps[p], 1)

            def project_partners(p, n):
                if not first(n):
                    pe.wait_ge(h_ready[p], c2(n - 1, 1))
                for g in range(4, 8):
                    ins = pe.matmul(bank(p, g // 2, 128, (g % 2) * N, (g % 2 + 1) * N), wqk0[:, g, :],
                                    xhT[p][:, :], start=True, stop=True)
                ins.then_inc(qkv_ps[p], 1)

            def max_scores(p, a, n, s, i):
                if s == 1:
                    pe.wait_ge(max_done[p], c8(n, a, 0, i))
                elif i == 0:
                    pe.wait_ge(qkb_ready[p], c2(n, a))
                else:
                    pe.wait_ge((v_ready0, v_ready1)[a][p], c1(n))
                    if a == 1:
                        pe.wait_ge(qk_copied[p], n * 2 + 2)
                for g in range(2):
                    for j in (2 - 2 * i, 3 - 2 * i):
                        r = 32 * j
                        ins = pe.matmul(bank(p, j, HALF, g * N, (g + 1) * N),
                                        qkb[p][r:r + HD, g, s * HALF:(s + 1) * HALF],
                                        qkb[p][r:r + HD, 2 + g, :], start=True, stop=True)
                ins.then_inc(sm_ps[p], 1)

            def max_turn(p, a, n):
                pe.wait_ge(max_done[p], c8(n, a, 1, 1))
                for g in range(2):
                    for s in range(2):
                        ins = pe.transpose(bank(p, 0, 128, g * N + s * HALF, g * N + (s + 1) * HALF),
                                           mx[p][:, s, g * 128:(g + 1) * 128], ident[0:HALF, 0:HALF])
                ins.then_inc(mT_ps[p], 1)

            def weighted(p, a, n, part):
                heads = ((0, 4, 1, 5), (2, 6), (3, 7))[part]
                if part < 2:
                    pe.wait_ge(exp_done[p], c8(n, a, 1, part))
                for h in heads:
                    j, g = h % 4, h // 4
                    for s in range(2):
                        ins = pe.matmul(ps[32 * j:32 * j + 32, 4 * p, g * N:(g + 1) * N], va[p][:, s, h, :],
                                        pT[p][:, s, 2 * j + g, :], start=(s == 0), stop=(s == 1))
                if part == 2:
                    ins.then_inc(o_ps[p], 1)

            def out_project(p, a, n):
                pe.wait_ge(oT_ready[p], c2(n, a))
                for t in range(2):
                    for g in range(2):
                        ins = pe.matmul(bank(p, 2, HALF, t * H, (t + 1) * H), oT[p][:, g, t * HALF:(t + 1) * HALF],
                                        (wo0 if a == 0 else wo1)[:, g, :], start=(g == 0), stop=(g == 1))
                ins.then_inc(y_ps[p], 1)

            def turn_rows(p, n):
                pe.wait_ge(x2_ready[p], c1(n))
                turn(p, 1, x2[p][:, :, 0, 0:H], x2T_ps[p])

            def logits(p, n):
                pe.wait_ge(x2T_ready[p], c1(n))
                for t in range(2):
                    ins = pe.matmul(bank(p, 1, HALF, t * E, (t + 1) * E), x2T[p][:, t * HALF:(t + 1) * HALF],
                                    wr[:, :], start=True, stop=True)
                ins.then_inc(lg_ps[p], 1)

            def counts(p, n):
                pe.wait_ge(ohs_ready[p], c1(n))
                o0, o1 = ohs[p][:, 0, :], ohs[p][:, 1, :]
                pe.matmul(bank(p, 1, HALF, 0, E), trib[:, :], o0, start=True, stop=True)
                pe.matmul(bank(p, 1, HALF, E, 2 * E), allb[:, :], o0, start=True, stop=False)
                pe.matmul(bank(p, 1, HALF, E, 2 * E), trib[:, :], o1, start=False, stop=True)
                pe.matmul(bank(p, 1, HALF, 2 * E, 3 * E), allb[:, :], o0, start=True, stop=False)
                pe.matmul(bank(p, 1, HALF, 2 * E, 3 * E), allb[:, :], o1, start=False, stop=True).then_inc(cnt_ps[p], 1)

            def half(light, heavy, more=True):
                lp, la, lnum = light
                if heavy:
                    hp, ha, hn = heavy
                    scores(hp, ha, hn, 0, 0)
                if la == 1:
                    out_project(lp, 0, lnum)
                    if heavy:
                        scores(hp, ha, hn, 0, 1)
                        scores(hp, ha, hn, 1, 0)
                    if not first(lnum):
                        counts(lp, lnum - 1)
                    if heavy:
                        scores(hp, ha, hn, 1, 1)
                    pe.wait_ge(xh_ready[lp], c2(lnum, 1))
                    turn(lp, 0, xh[lp], xT_ps[lp])
                    if heavy:
                        weighted(hp, ha, hn, 0)
                    project(lp, 1, lnum)
                    for s in range(2):
                        for i in range(2):
                            max_scores(lp, 1, lnum, s, i)
                        if heavy:
                            weighted(hp, ha, hn, 1 + s)
                        if heavy and ha == 0 and not first(hn) and s == 0:
                            turn_rows(hp, hn - 1)
                else:
                    if more:
                        pe.wait_ge(xh_ready[lp], c2(lnum, 0))
                        if not first(lnum):
                            pe.wait_ge(oT_ready[lp], c2(lnum - 1, 1))
                        turn(lp, 0, xh[lp], xT_ps[lp])
                    if not first(lnum):
                        out_project(lp, 1, lnum - 1)
                    if more:
                        project(lp, 0, lnum)
                        project_partners(lp, lnum)
                    if heavy:
                        scores(hp, ha, hn, 0, 1)
                        scores(hp, ha, hn, 1, 0)
                    if more:
                        for i in range(2):
                            max_scores(lp, 0, lnum, 0, i)
                    if heavy:
                        scores(hp, ha, hn, 1, 1)
                    if more:
                        for i in range(2):
                            max_scores(lp, 0, lnum, 1, i)
                    if heavy:
                        weighted(hp, ha, hn, 0)
                        if ha == 0 and not first(hn):
                            turn_rows(hp, hn - 1)
                        weighted(hp, ha, hn, 1)
                        weighted(hp, ha, hn, 2)
                if heavy and ha == 0 and not first(hn) and la == 1:
                    logits(hp, hn - 1)
                if more:
                    max_turn(lp, la, lnum)
                if heavy and ha == 0 and not first(hn) and la == 0:
                    logits(hp, hn - 1)

            def tail(n):
                out_project(1, 1, n)
                for p in range(2):
                    turn_rows(p, n)
                for p in range(2):
                    logits(p, n)
                for p in range(2):
                    pe.wait_ge(lg_ready[p], c1(n))
                    counts(p, n)

            schedule(pe, half, tail)

            def turn_slots(m, p):
                pe.wait_ge(first_in[p], m * 48 + 48)
                pe.wait_ge(eT_ready, m * 2 + p + 1)
                for c in range(MAIN):
                    pe.transpose(ps[:, c // 4, (c % 4) * 128:(c % 4 + 1) * 128], ex[p][:, c, 0:H], ident[:, :])
                pe.transpose(ps[:, 1, 128:128 + TAIL], ext[p][:, 0:H], ident[0:TAIL, 0:TAIL]).then_inc(eT_ps, 1)

            def first_product(m, p):
                pe.wait_ge(eT_ready, n2(m, p) + 1)
                for f in range(FC):
                    if not (first(m) and p == 0 and f == 0):
                        pe.wait_ge(gelu_done, m * 8 + (4 * p + f))
                    hp = 2 + 2 * (f % 2)
                    for g in range(2):
                        ins = pe.matmul(ps[:, hp + g, 0:CAP // 2], w1s[p][:, f:F:FC],
                                        eT[p][:, g * (CAP // 2):(g + 1) * (CAP // 2)], start=True, stop=True)
                    ins.then_inc(h_ps, 1)

            def second_product(m, p):
                pe.wait_ge(second_in[p], m * 32 + 32)
                pe.wait_ge(gelu_done, m * 8 + (4 * p + 4) + 1)
                pe.wait_ge(ey_ready, m * 2 + p + 1)
                for c in range(MAIN + 1):
                    rows = 128 if c < MAIN else TAIL
                    for f in range(FC):
                        ins = pe.matmul(ps[0:rows, 6 + c // 4, (c % 4) * 128:(c % 4 + 1) * 128],
                                        hT[p][:, f, c * 128:c * 128 + rows], w2s[p][:, f, :],
                                        start=(f == 0), stop=(f == FC - 1))
                ins.then_inc(ey_ps, 1)

            expert_order(pe, turn_slots, first_product, second_product)

        @block.scalar
        def _(act):
            for s in (emb_sb, tokT_sb, gelu_done,):
                act.sem_inc(s, 1)
            act.wait_ge(memset_done, 1)
            act.wait_ge(patch_consts_in, 16 * len(patch_consts))
            with act.Fori(0, 2) as it:
                for i in range(2):
                    act.wait_ge(emb_ps, it * 2 + (i + 1) + 1)
                    act.wait_ge(tokT_ps, it * 2 + i + 1)
                    for j in range(NP):
                        ins = act.activation(gpad[:, :, 1:7, 1 + j],
                                             ps[:, 2 + j // 3, (j % 3) * ROWS:(j % 3 + 1) * ROWS].rearrange("p (b i) -> p b i", i=NP),
                                             ACT.Identity)
                    ins.then_inc(emb_sb, 1)
                    part = SLOTS // 128 // (B // GRP)
                    act.dma_start(slots_x.rearrange("(q s w) h -> q s (w h)", q=128, w=2)[
                        :, bass.ds((it * 2 + i) * (part // 2), part // 2), :],
                        zeros[:, None, :].broadcast_to([128, part // 2, 2 * ROW])).then_inc(slots_zeroed, 16)
                    act.wait_ge(tokT_ps, it * 2 + (i + 1) + 1)
                    act.wait_ge(tok_ps, it * 2 + i + 1)
                    act.activation(tokT[:, :, :], ps[:, 4:6, 0:288], ACT.Identity, bias=btok[:, 0:1]).then_inc(tokT_sb, 1)
            act.wait_ge(consts_in, 16 * len(consts))

            def exponentials(p, a, n, s, half):
                act.wait_ge(st_ps[p], c8(n, a, s, half))
                act.activation(pT[p][:, s, 4 * half:4 * half + 4, :].rearrange("p (b g) n -> p b (g n)", b=2),
                               R[p][0:HALF, 2 * half:2 * half + 2, 0:2 * N], ACT.Exp, scale=SCALE).then_inc(exp_done[p], 1)

            def copy_turned(p, a, n):
                act.wait_ge(xT_ps[p], c2(n, a))
                if a == 0:
                    act.activation(xhT[p][:, :], bank(p, 0, 128, 0, N), ACT.Identity).then_inc(xT_ready[p], 1)
                else:
                    act.activation(xhT[p][:, :], bank(p, 0, 128, 0, N), ACT.Identity, bias=be1c[:, 0:1],
                                   scale=g1c[:, 0:1]).then_inc(xT_ready[p], 1)

            def copy_rows(p, n):
                act.wait_ge(x2T_ps[p], c1(n))
                act.activation(x2T[p][:, :], bank(p, 1, 128, 0, N), ACT.Identity).then_inc(x2T_ready[p], 1)

            def copy_logits(p, n):
                act.wait_ge(lg_ps[p], c1(n))
                act.activation(lg[p][:, :, :], bank(p, 1, HALF, 0, 2 * E).rearrange("p (t e) -> p t e", t=2),
                               ACT.Identity).then_inc(lg_ready[p], 1)

            def spread_keys(p, a, n):
                for j in range(4):
                    ins = act.activation(keys[p][32 * j:32 * j + 32, j, :, :], qk[p][32 * j:32 * j + 32, 2:4, :], ACT.Identity)
                ins.then_inc(keys_ready[p], 1)

            def half(light, heavy, more=True):
                lp, la, lnum = light
                if heavy:
                    hp, ha, hn = heavy
                    exponentials(hp, ha, hn, 0, 0)
                if la == 0 and more:
                    copy_turned(lp, 0, lnum)
                if heavy:
                    exponentials(hp, ha, hn, 0, 1)
                    exponentials(hp, ha, hn, 1, 0)
                if la == 1:
                    copy_turned(lp, 1, lnum)
                if heavy and la == 1:
                    exponentials(hp, ha, hn, 1, 1)
                if la == 1:
                    act.wait_ge(qkv_ps[lp], lnum * 3 + 3)
                    act.activation(qkb[lp][:, :, :].rearrange("p (b g) n -> p b (g n)", b=2), R[lp][:, 0:2, 0:2 * N],
                                   ACT.Identity).then_inc(qkb_ready[lp], 1)
                    act.activation(qk[lp][:, 0:2, :], bank(lp, 0, 128, 0, 2 * N), ACT.Identity).then_inc(qk_copied[lp], 1)
                    act.activation(qk[lp][:, 2:4, :], bank(lp, 1, 128, 0, 2 * N), ACT.Identity, bias=onerow[:, 0:1]
                                   ).then_inc(qk_copied[lp], 1)
                    act.activation(va[lp][:, :, :, 0:HD],
                                   ps[0:HALF, 4 * lp:4 * lp + 2, 2 * N:2 * N + H].rearrange("p t (h d) -> p t h d", d=HD),
                                   ACT.Identity).then_inc(v_ready1[lp], 1)
                if heavy and la == 0:
                    exponentials(hp, ha, hn, 1, 1)
                if heavy and ha == 0 and not first(hn) and la == 1:
                    copy_rows(hp, hn - 1)
                if la == 1:
                    act.wait_ge(qk_copied[lp], lnum * 2 + 2)
                    spread_keys(lp, 1, lnum)
                    if lp == 1:
                        act.dma_start(choice_y.rearrange("(n q r) c -> n q r c", q=HALF, r=8)[bass.ds(lnum, 1)].rearrange(
                            "o q r c -> (o q) r c"), zeros[0:HALF, None, 0:H].broadcast_to([HALF, 8, H])
                        ).then_inc(choices_zeroed, 16)
                elif more:
                    act.wait_ge(qk_roped[lp], c1(lnum))
                    spread_keys(lp, 0, lnum)
                if heavy and ha == 0 and not first(hn) and la == 0:
                    copy_rows(hp, hn - 1)
                if heavy and ha == 0 and not first(hn):
                    copy_logits(hp, hn - 1)
                    act.wait_ge(idx_ready[hp], c1(hn - 1))
                    act.activation(e2[hp][:, :], dif[hp][:, :], ACT.Exp).then_inc(e2_ready[hp], 1)

            def tail(n):
                for p in range(2):
                    copy_rows(p, n)
                for p in range(2):
                    copy_logits(p, n)
                for p in range(2):
                    act.wait_ge(idx_ready[p], c1(n))
                    act.activation(e2[p][:, :], dif[p][:, :], ACT.Exp).then_inc(e2_ready[p], 1)

            schedule(act, half, tail)

            def hidden(m, p):
                for f in range(FC):
                    act.wait_ge(h_ps, m * 8 + (4 * p + f + 1))
                    act.activation(hT[p][:, f, :].rearrange("p (g n) -> p g n", g=2),
                                   ps[:, 2 + 2 * (f % 2):4 + 2 * (f % 2), 0:CAP // 2], ACT.Gelu_apprx_tanh,
                                   bias=b1c[:, bass.ds(m * 2 + p, 1), f]).then_inc(gelu_done, 1)

            expert_order(act, lambda m, p: None, hidden, lambda m, p: None)

            for p in range(2):
                act.wait_ge(ey_out[p], 96 * (E // 2) + 16)
            with act.Fori(0, B // 4) as it:
                for p in range(2):
                    act.wait_ge(fin_ready, it * 2 + (p + 1))
                    act.dma_start(yl[p][:, :, :, :], choice_y.rearrange("(t q k) c -> q t k c", q=HALF, k=2)[
                        :, bass.ds(it * 8 + 4 * p, 4)]).then_inc(yl_in[p], 16)

        @block.gpsimd
        def _(pool):
            pool.memset(mhalf[:, :], -0.5)
            pool.iota(iota[:, :], [[1, E]], base=0, channel_multiplier=0, allow_small_or_imprecise_dtypes=True
                      ).then_inc(iota_done, 1)
            pool.wait_ge(iota_done, 1)
            settled(pool)
            for n, s in enumerate([tok_out, *ey_out]):
                pool.dma_start(scratch[n:n + 1, :], iota[0:1, :]).then_inc(s, 16)
            with pool.Fori(0, 4) as it:
                pool.wait_ge(tok_mv, it + 1)
                settled(pool)
                pool.tensor_scalar(tve[:, :], tmv[:, :, 1], EPS, None, ALU.add).then_inc(tok_step, 1)
                pool.wait_ge(tok_step, it * 2 + 1)
                pool.tensor_tensor(trs[:, :], tve[:, :], mhalf[0:2 * IMG, 0:8], ALU.pow).then_inc(tok_rs, 1)
                pool.wait_ge(tok_norm, it + 1)
                settled(pool)
                g = lng[:, None, :].broadcast_to([2 * IMG, 8, H])
                b = lnb[:, None, :].broadcast_to([2 * IMG, 8, H])
                pool.tensor_tensor(tok2[:, :, :], tok[:, :, :], g, ALU.mult).then_inc(tok_step, 1)
                pool.wait_ge(tok_step, it * 2 + 2)
                pool.tensor_tensor(tok[:, :, :], tok2[:, :, :], b, ALU.add).then_inc(tok_ready, 1)
                pool.wait_ge(tok_ready, it + 1)
                settled(pool)
                pool.dma_start(tokens[bass.ds(it * GRP, GRP), :, :].rearrange("(q b) n c -> (b n) q c", b=2),
                               tok[:, :, :]).then_inc(tok_out, 16)
            pool.wait_ge(consts_in, 16 * len(consts))
            settled(pool)

            def deviations(l, p, n):
                pool.wait_ge(mv_ready[l][p], c1(n))
                settled(pool)
                pool.tensor_scalar(ve[l][p][:, :, 0], mv[l][p][:, :, 1], EPS, None, ALU.add).then_inc(ve_ready[l][p], 1)
                count = n * 2 + 2 if l == 1 else c1(n)
                pool.wait_ge(ve_ready[l][p], count)
                pool.tensor_tensor(rs[l][p][:, :, 0], ve[l][p][:, :, 0], mhalf[0:HALF, 0:2], ALU.pow
                                   ).then_inc(rs_ready[l][p], 1)

            def deviations_twice(p, n):
                pool.wait_ge(mv_ready[1][p], c1(n))
                settled(pool)
                pool.tensor_scalar(ve[1][p][:, :, 1], mv[1][p][:, :, 1], 1.0 + EPS, EPS * EPS, ALU.mult, ALU.add
                                   ).then_inc(ve_ready[1][p], 1)
                pool.wait_ge(ve_ready[1][p], n * 2 + 1)
                pool.tensor_tensor(rs[1][p][:, :, 1], ve[1][p][:, :, 1], mhalf[0:HALF, 0:2], ALU.pow
                                   ).then_inc(rs_ready[1][p], 1)

            def normalize(l, p, n, src, out, done):
                pool.wait_ge(rs_ready[l][p], n * 2 + 2 if l == 1 else c1(n))
                settled(pool)
                for t in range(2):
                    ins = pool.tensor_scalar(out[p][:, t, :], src[p][:, t, :], mv[l][p][:, t, 0:1], rs[l][p][:, t, 0:1],
                                             ALU.subtract, ALU.mult)
                ins.then_inc(done[p], 1)

            def expert_rows(p, n):
                pool.wait_ge(h_ready[p], c2(n, 1))
                pool.tensor_tensor(resid[:, bass.ds(n * 4 + 2 * p, 2), :], h1[p][:, :, :], xm[p][:, :, :], ALU.add
                                   ).then_inc(resid_ready[p], 1)
                deviations(2, p, n)
                normalize(2, p, n, xm, xh2, xh2_step)
                pool.wait_ge(xh2_step[p], n * 2 + 1)
                pool.tensor_tensor(xh2[p][:, :, :], xh2[p][:, :, :], g2r[:, None, :].broadcast_to([HALF, 2, H]),
                                   ALU.mult).then_inc(xh2_step[p], 1)
                if not first(n):
                    pool.wait_ge(scat_out[p], n * 64)
                    settled(pool)
                pool.tensor_scalar(x2[p][:, :, :, H], x2[p][:, :, :, H], float(4 * N), None, ALU.add)
                pool.wait_ge(xh2_step[p], n * 2 + 2)
                pool.tensor_tensor(x2[p][:, :, :, 0:H], xh2[p][:, :, None, :].broadcast_to([HALF, 2, 2, H]),
                                   be2r[:, None, None, :].broadcast_to([HALF, 2, 2, H]), ALU.add).then_inc(x2_ready[p], 1)

            def scatter(p, n):
                pool.wait_ge(scu_ready[p], c1(n))
                pool.wait_ge(slots_zeroed, 16 * (B // GRP))
                settled(pool)
                for t in range(2):
                    for k in range(2):
                        pool.indirect_dma_start(slots_x[:, :], bass.IndirectOffsetOnAxis(ap=scu[p][:, t, k:k + 1], axis=0),
                                                x2[p][:, t, k, :], None, bounds_check=SLOTS - 1, oob_is_err=False
                                                ).then_inc(scat_out[p], 16)

            def half(light, heavy, more=True):
                lp, la, lnum = light
                next_image = heavy and heavy[1] == 1 and not (isinstance(heavy[2], int) and heavy[2] == B // 2 - 1)
                if la == 1:
                    deviations_twice(lp, lnum)
                if next_image:
                    deviations(0, heavy[0], heavy[2] + 1)
                if la == 1:
                    deviations(1, lp, lnum)
                    normalize(1, lp, lnum, h1, xin, xin_ready)
                    if not first(lnum):
                        scatter(lp, lnum - 1)
                else:
                    if more:
                        pool.wait_ge(rope_step[lp], lnum * 3 + 3)
                        pool.tensor_tensor(qk[lp][:, :, :], rt[lp][:, 0:4, :], rt[lp][:, 4:8, :], ALU.add
                                           ).then_inc(qk_roped[lp], 1)
                    if not first(lnum):
                        expert_rows(lp, lnum - 1)

            def tail(n):
                expert_rows(1, n)
                for p in range(2):
                    scatter(p, n)

            for p in range(2):
                pool.iota(x2[p][:, :, :, H], [[2 * HALF, 2], [1, 2]], base=2 * N * p + 1 - 4 * N, channel_multiplier=2,
                          allow_small_or_imprecise_dtypes=True).then_inc(iota_done, 1)
            pool.wait_ge(iota_done, 3)
            for p in range(2):
                deviations(0, p, 0)
            schedule(pool, half, tail)

            pool.wait_ge(choices_zeroed, 16 * (B // 2))
            settled(pool)
            with pool.Fori(0, E // 2) as it:
                for p in range(2):
                    pool.wait_ge(ey_ready, n2(it, p) + 1)
                    settled(pool)
                    for c in range(MAIN + 1):
                        m = 128 if c < MAIN else TAIL
                        pool.indirect_dma_start(choice_y[:, :], bass.IndirectOffsetOnAxis(ap=eu[p][0:m, c:c + 1], axis=0),
                                                ey[p][0:m, c, :], None, bounds_check=CHOICES - 1, oob_is_err=False
                                                ).then_inc(ey_out[p], 16)

        @block.vector
        def _(dve):
            for s in (patch_sb, tok_sb, patch_rows, eT_ready, ey_ready, fin_ready, fin_ready):
                dve.sem_inc(s, 1)
            dve.memset(zeros[:, :], 0.0)
            dve.memset(gpad[:, :, :, :], 0.0)
            dve.memset(allb[:, :], 1.0)
            dve.memset(taken[0][:, :], 0.0).then_inc(taken_ready, 1)
            for p in range(2):
                dve.memset(bank(p, 0, 128, 2 * N, 32 * BLOCKS), 1.0)
                dve.memset(keys[p][:, :, :, :], 0.0)
                dve.memset(mx[p][:, :, :], 0.0)
                dve.memset(va[p][:, :, :, HD:32], 1.0)
            dve.memset(dif[0][:, :], 0.0).then_inc(memset_done, 1)
            def gather_patches(m, i):
                dve.wait_ge(xs_in[i], m * (16 * GRP) + 16 * GRP)
                dve.wait_ge(patch_ps, m * 12 + 6 * i + 1)
                for j in range(NP):
                    ins = dve.tensor_copy(xr[:, j, :].rearrange("p (c w) -> p c w", w=16),
                                          xs[i][:, :, :, 16 * j:16 * j + 16].rearrange("p c y w -> p (c y) w"))
                ins.then_inc(patch_rows, 1)

            def patches(m, i):
                for k in range(6):
                    dve.wait_ge(patch_ps, m * 12 + (6 * i + k + 1) + 1)
                    if k < 2:
                        dve.wait_ge(emb_ps, m * 2 + i + 1)
                    b = 6 * (k % 2)
                    dve.tensor_copy(xT[k % 2][:, :, :], ps[:, b:b + 2, 0:288]).then_inc(patch_sb, 1)

            def tokens_of(m, i, more=True):
                dve.wait_ge(tok_ps, m * 2 + (i + 1) + 1)
                dve.wait_ge(tok_out, m * 32 + (16 * i + 16))
                dve.tensor_copy(tok[:, :, :].rearrange("p (g q) c -> p g (q c)", g=2), ps[0:2 * IMG, 6:8, :]
                                ).then_inc(tok_sb, 1)
                dve.wait_ge(tok_sb, m * 2 + (i + 1) + 1)
                for q in range(8):
                    ins = dve.bn_stats(tstat[:, q, :], tok[:, q, :])
                ins.then_inc(tok_stat, 1)
                dve.wait_ge(tok_stat, m * 2 + (i + 1))
                settled(dve)
                for q in range(8):
                    ins = dve.bn_aggr(tmv[:, q, :], tstat[:, q, :])
                ins.then_inc(tok_mv, 1)
                if more:
                    gather_patches(m + 1, i)
                dve.wait_ge(tok_rs, m * 2 + (i + 1))
                for q in range(8):
                    ins = dve.tensor_scalar(tok[:, q, :], tok[:, q, :], tmv[:, q, 0:1], trs[:, q:q + 1],
                                            ALU.subtract, ALU.mult)
                ins.then_inc(tok_norm, 1)

            gather_patches(0, 0)
            def first_patches(m, i):
                patches(m, i)
                if first(m) and i == 0:
                    gather_patches(0, 1)

            patch_order(dve, first_patches, tokens_of)

            dve.wait_ge(consts_in, 16 * len(consts))
            dve.tensor_copy(trib[:, :], trif[:, :]).then_inc(tables_step, 1)
            for g in range(4):
                dve.tensor_scalar(ropeb[:, g, :], ropet[:, g, :], bqk0[:, g:g + 1], None, ALU.mult)
                dve.tensor_scalar(rt[0][:, g, :], ropet[:, 4 + g, :], bqk0[:, 4 + g:5 + g], onerow[:, 0:1] if g >= 2 else 0.0,
                                  ALU.mult, ALU.add).then_inc(tables_step, 1)
            dve.wait_ge(tables_step, 5)
            dve.tensor_tensor(ropeb[:, :, :], ropeb[:, :, :], rt[0][:, 0:4, :], ALU.add).then_inc(tables_step, 1)
            dve.wait_ge(iota_done, 1)

            def statistics(l, p, n, src):
                for t in range(2):
                    ins = dve.bn_stats(stat[l][p][:, t, :], src[p][:, t, :])
                ins.then_inc(stat_done[l][p], 1)
                dve.wait_ge(stat_done[l][p], c1(n))
                settled(dve)
                for t in range(2):
                    ins = dve.bn_aggr(mv[l][p][:, t, :], stat[l][p][:, t, :])
                ins.then_inc(mv_ready[l][p], 1)

            def normalize(l, p, n, src, c, out, done):
                dve.wait_ge(rs_ready[l][p], n * 2 + 1 if l == 1 else c1(n))
                for t in range(2):
                    ins = dve.tensor_scalar(out[p][:, t, :], src[p][:, t, :], mv[l][p][:, t, 0:1], rs[l][p][:, t, c:c + 1],
                                            ALU.subtract, ALU.mult)
                ins.then_inc(done[p], 1)

            def add_residual(p, a, n):
                dve.wait_ge(y_ps[p], c2(n, a))
                if a == 1:
                    dve.wait_ge(xin_ready[p], c1(n))
                    if not first(n):
                        dve.wait_ge(resid_ready[p], c1(n - 1))
                        dve.wait_ge(xh2_step[p], n * 2)
                dve.tensor_tensor((h1 if a == 0 else xm)[p][:, :, :],
                                  bank(p, 2, HALF, 0, 2 * H).rearrange("p (t c) -> p t c", t=2),
                                  (hin if a == 0 else xin)[p][:, :, :], ALU.add).then_inc(h_ready[p], 1)
                dve.wait_ge(h_ready[p], c2(n, a))

            def maxima(p, a, n, s, i):
                dve.wait_ge(sm_ps[p], c8(n, a, s, i))
                b = 2 - 2 * i
                dve.tensor_reduce(mx[p][:, s, :].rearrange("p (g j r) -> p j g r", g=2, j=4)[:, b:b + 2, :, HD],
                                  R[p][0:HALF, b:b + 2, 0:2 * N].rearrange("p b (g n) -> p b g n", g=2),
                                  AX.X, ALU.max, negate=True).then_inc(max_done[p], 1)

            def top_two(p, n):
                dve.wait_ge(lg_ready[p], c1(n))
                settled(dve)
                for t in range(2):
                    ins = dve.max(v8[p][:, t, :], lg[p][:, t, :])
                ins.then_inc(top_step[p], 1)
                dve.wait_ge(top_step[p], n * 3 + 1)
                settled(dve)
                for t in range(2):
                    dve.max_index(i8[p][:, t, :], v8[p][:, t, :], lg[p][:, t, :])
                dve.tensor_tensor(dif[p][:, :], v8[p][:, :, 1], v8[p][:, :, 0], ALU.subtract).then_inc(idx_ready[p], 1)
                dve.wait_ge(idx_ready[p], c1(n))
                dve.tensor_copy(ix[p][:, :, :], i8[p][:, :, 0:2]).then_inc(top_step[p], 1)
                dve.wait_ge(top_step[p], n * 3 + 2)
                dve.tensor_tensor(oh[p][:, :, :, :].rearrange("p t k e -> p (t k) e"),
                                  iota[:, None, :].broadcast_to([HALF, 4, E]),
                                  ix[p][:, :, :].rearrange("p t k -> p (t k)")[:, :, None].broadcast_to([HALF, 4, E]),
                                  ALU.is_equal).then_inc(top_step[p], 1)
                dve.wait_ge(top_step[p], n * 3 + 3)
                dve.tensor_tensor(ohs[p][:, :, :], oh[p][:, :, 0, :], oh[p][:, :, 1, :], ALU.add).then_inc(ohs_ready[p], 1)

            def read_counts(p, n):
                dve.wait_ge(cnt_ps[p], c1(n))
                dve.wait_ge(taken_ready, n * 2 + (p + 1))
                dve.tensor_tensor(before[p][:, :, :], bank(p, 1, HALF, 0, 2 * E).rearrange("p (t e) -> p t e", t=2),
                                  taken[p][:, None, :].broadcast_to([HALF, 2, E]), ALU.add)
                dve.tensor_tensor(taken[1 - p][:, :], bank(p, 1, HALF, 2 * E, 3 * E), taken[p][:, :], ALU.add
                                  ).then_inc(cnt_read[p], 1)
                dve.wait_ge(cnt_read[p], c1(n))
                dve.sem_inc(taken_ready, 1)

            def find_slots(p, n):
                dve.tensor_tensor(sel[p][:, :, :, :], before[p][:, :, None, :].broadcast_to([HALF, 2, 2, E]),
                                  oh[p][:, :, :, :], ALU.mult).then_inc(slot_step[p], 1)
                dve.wait_ge(slot_step[p], n * 4 + 1)
                dve.tensor_reduce(pos[p][:, :, :], sel[p][:, :, :, :], AX.X, ALU.add).then_inc(slot_step[p], 1)
                dve.wait_ge(slot_step[p], n * 4 + 2)
                dve.tensor_scalar(keep[p][:, :, :], pos[p][:, :, :], float(CAP), None, ALU.is_lt)
                dve.tensor_scalar(mnp[p][:, :, :], pos[p][:, :, :], float(CAP - 1), None, ALU.min).then_inc(slot_step[p], 1)
                dve.wait_ge(slot_step[p], n * 4 + 3)
                dve.scalar_tensor_tensor(slf[p][:, :, :], ix[p][:, :, :], float(CAP), mnp[p][:, :, :], ALU.mult, ALU.add)
                dve.tensor_scalar(off[p][:, :, :], keep[p][:, :, :], -BIG, BIG, ALU.mult, ALU.add).then_inc(slot_step[p], 1)
                dve.wait_ge(slot_step[p], n * 4 + 4)
                if not first(n):
                    dve.wait_ge(scat_out[p], n * 64)
                dve.tensor_tensor(scu[p][:, :, :], slf[p][:, :, :], off[p][:, :, :], ALU.add).then_inc(scu_ready[p], 1)
                dve.wait_ge(e2_ready[p], c1(n))
                dve.tensor_scalar(gt[p][:, :, 1], e2[p][:, :], 1.0, None, ALU.add).then_inc(gate_step[p], 1)
                dve.wait_ge(gate_step[p], n * 3 + 1)
                dve.reciprocal(gt[p][:, :, 0], gt[p][:, :, 1]).then_inc(gate_step[p], 1)
                dve.wait_ge(gate_step[p], n * 3 + 2)
                dve.tensor_tensor(gt[p][:, :, 1], gt[p][:, :, 0], e2[p][:, :], ALU.mult).then_inc(gate_step[p], 1)
                dve.wait_ge(gate_step[p], n * 3 + 3)
                dve.tensor_tensor(gate[:, bass.ds(n * 8 + 4 * p, 4)], gt[p][:, :, :].rearrange("p t k -> p (t k)"),
                                  keep[p][:, :, :].rearrange("p t k -> p (t k)"), ALU.mult).then_inc(gate_done[p], 1)

            def denominators(p, a, n):
                dve.wait_ge(o_ps[p], c2(n, a))
                dve.transpose(sums[p][:, :, :].rearrange("p b c -> p (b c)"), bank(p, 0, 128, 0, 32 * BLOCKS)
                              ).then_inc(den_step[p], 1)

            def reciprocals(p, a, n):
                dve.wait_ge(den_step[p], n * 6 + (3 * a + 1))
                dve.reciprocal(inv[p][:, :], sums[p][:, :, HD]).then_inc(den_step[p], 1)
                dve.wait_ge(den_step[p], n * 6 + (3 * a + 2))
                dve.transpose(rc[p][:, :], inv[p][:, :, None].broadcast_to([128, BLOCKS, 32])).then_inc(den_step[p], 1)

            def look_at_image(p, n):
                dve.wait_ge(hin_in[p], n * 48 + 48)
                statistics(0, p, n, hin)

            def normalize_image(p, n):
                normalize(0, p, n, hin, 0, xh, xh_ready)

            def rotate(p, n):
                for m in range(2):
                    dve.wait_ge(qkv_ps[p], n * 3 + (m + 1))
                    dve.tensor_tensor(rt[p][:, 4 * m:4 * m + 4, :].rearrange("p (b g) n -> p b (g n)", b=2),
                                      R[p][:, 2 * m:2 * m + 2, 0:2 * N],
                                      ropet[:, 4 * m:4 * m + 4, :].rearrange("p (b g) n -> p b (g n)", b=2), ALU.mult
                                      ).then_inc(rope_step[p], 1)
                    if m == 0:
                        dve.wait_ge(rope_step[p], n * 3 + 1)
                        dve.tensor_tensor(rt[p][:, 0:4, :], rt[p][:, 0:4, :], ropeb[:, :, :], ALU.add).then_inc(rope_step[p], 1)
                dve.wait_ge(rope_step[p], n * 3 + 3)
                dve.tensor_tensor(qkb[p][:, :, :], rt[p][:, 0:4, :], rt[p][:, 4:8, :], ALU.add).then_inc(qkb_ready[p], 1)
                dve.tensor_tensor(va[p][:, :, :, 0:HD],
                                  ps[0:HALF, 4 * p:4 * p + 2, 2 * N:2 * N + H].rearrange("p t (h d) -> p t h d", d=HD),
                                  bv0[:, :].rearrange("p (h d) -> p h d", d=HD)[:, None, :, :].broadcast_to([HALF, 2, NH, HD]),
                                  ALU.add).then_inc(v_ready0[p], 1)

            def weighted_means(p, a, n):
                dve.wait_ge(den_step[p], n * 6 + (3 * a + 3))
                dve.tensor_tensor(oT[p][:, :, :].rearrange("p g n -> p (g n)"), bank(p, 0, 128, 0, 2 * N), rc[p][:, 0:2 * N],
                                  ALU.mult).then_inc(oT_ready[p], 1)

            def half(light, heavy, more=True):
                lp, la, lnum = light
                next_image = heavy and heavy[1] == 1 and not (isinstance(heavy[2], int) and heavy[2] == B // 2 - 1)
                if la == 1:
                    add_residual(lp, 0, lnum)
                    statistics(1, lp, lnum, h1)
                    normalize(1, lp, lnum, h1, 1, xh, xh_ready)
                    if not first(lnum):
                        read_counts(lp, lnum - 1)
                    if next_image:
                        look_at_image(heavy[0], heavy[2] + 1)
                    if not first(lnum):
                        find_slots(lp, lnum - 1)
                    if next_image:
                        normalize_image(heavy[0], heavy[2] + 1)
                else:
                    if next_image:
                        look_at_image(heavy[0], heavy[2] + 1)
                        normalize_image(heavy[0], heavy[2] + 1)
                    if not first(lnum):
                        add_residual(lp, 1, lnum - 1)
                        statistics(2, lp, lnum - 1, xm)
                    if more:
                        rotate(lp, lnum)
                if more:
                    for s in range(2):
                        for i in range(2):
                            maxima(lp, la, lnum, s, i)
                if heavy:
                    denominators(*heavy)
                if more:
                    dve.wait_ge(mT_ps[lp], c2(lnum, la))
                    if la == 0:
                        dve.wait_ge(qk_roped[lp], c1(lnum))
                    dve.tensor_tensor(qm[lp][:, :, :], qk[lp][:, 0:2, :],
                                      bank(lp, 0, 128, 0, 2 * N).rearrange("p (g n) -> p g n", g=2), ALU.add
                                      ).then_inc(qm_ready[lp], 1)
                if heavy:
                    reciprocals(*heavy)
                    weighted_means(*heavy)
                if heavy and heavy[1] == 0 and not first(heavy[2]):
                    top_two(heavy[0], heavy[2] - 1)

            def tail(n):
                add_residual(1, 1, n)
                statistics(2, 1, n, xm)
                for p in range(2):
                    top_two(p, n)
                for p in range(2):
                    read_counts(p, n)
                    find_slots(p, n)

            for p in range(2):
                dve.wait_ge(hin_in[p], 48)
                statistics(0, p, 0, hin)
            for p in range(2):
                normalize(0, p, 0, hin, 0, xh, xh_ready)
            schedule(dve, half, tail)

            def copy_slots(m, p):
                dve.wait_ge(eT_ps, n2(m, p))
                dve.tensor_copy(eT[p][:, 0:512], ps[:, 0, :])
                dve.tensor_copy(eT[p][:, 512:CAP], ps[:, 1, 0:CAP - 512]).then_inc(eT_ready, 1)
                dve.wait_ge(first_in[p], m * 48 + 48)
                dve.tensor_copy(number[p][:, 0:MAIN], ex[p][:, :, H])
                dve.tensor_copy(number[p][0:TAIL, MAIN:], ext[p][:, H:]).then_inc(rows_used, 1)

            def destinations(m, p):
                dve.wait_ge(rows_used, n2(m, p))
                dve.wait_ge(ey_out[p], m * 96 + 16)
                dve.tensor_scalar(em[p][:, 0:MAIN], number[p][:, 0:MAIN], 0.5, BIG, ALU.is_lt, ALU.mult)
                dve.tensor_scalar(em[p][0:TAIL, MAIN:], number[p][0:TAIL, MAIN:], 0.5, BIG, ALU.is_lt, ALU.mult
                                  ).then_inc(em_ready, 1)
                dve.wait_ge(em_ready, n2(m, p))
                dve.scalar_tensor_tensor(eu[p][:, 0:MAIN], number[p][:, 0:MAIN], -1.0, em[p][:, 0:MAIN], ALU.add, ALU.add)
                dve.scalar_tensor_tensor(eu[p][0:TAIL, MAIN:], number[p][0:TAIL, MAIN:], -1.0, em[p][0:TAIL, MAIN:],
                                         ALU.add, ALU.add)

            def results(m, p):
                dve.wait_ge(ey_ps, n2(m, p))
                dve.wait_ge(second_in[p], m * 32 + 32)
                bb = b2s[p][:, None, :]
                dve.tensor_tensor(ey[p][:, 0:4, :], ps[:, 6, :].rearrange("p (c h) -> p c h", c=4),
                                  bb.broadcast_to([128, 4, H]), ALU.add)
                dve.tensor_tensor(ey[p][:, 4, :], ps[:, 7, 0:H], b2s[p][:, :], ALU.add)
                dve.tensor_tensor(ey[p][0:TAIL, 5, :], ps[0:TAIL, 7, H:2 * H], b2s[p][0:TAIL, :], ALU.add
                                  ).then_inc(ey_ready, 1)

            expert_order(dve, copy_slots, destinations, results)

            for p in range(2):
                dve.wait_ge(gate_done[p], B // 2)
            with dve.Fori(0, B // 4) as it:
                for p in range(2):
                    dve.wait_ge(yl_in[p], it * 16 + 16)
                    dve.wait_ge(fin_out[p], it * 16 + 16)
                    for t in range(4):
                        ins = dve.scalar_tensor_tensor(tmpd[p][:, t, :], yl[p][:, t, 0, :],
                                                       gate[:, bass.ds(it * 16 + (8 * p + 2 * t), 1)],
                                                       resid[:, bass.ds(it * 8 + (4 * p + t), 1), :].rearrange("p o c -> p (o c)"),
                                                       ALU.mult, ALU.add)
                    ins.then_inc(fin_step, 1)
                    dve.wait_ge(fin_step, n2(it, p))
                    for t in range(4):
                        ins = dve.scalar_tensor_tensor(fin[p][:, t, :], yl[p][:, t, 1, :],
                                                       gate[:, bass.ds(it * 16 + (8 * p + 2 * t + 1), 1)], tmpd[p][:, t, :],
                                                       ALU.mult, ALU.add)
                    ins.then_inc(fin_ready, 1)


def host_layout(i):
    import numpy as np

    f = {k: np.asarray(v) for k, v in i.items()}
    a = {"x": f["x"], "txt": f["txt"]}
    w = np.zeros((3, 16, 16, H), np.float32)
    w[..., 0:64] = f["L0_tok_W_main"].reshape(64, 3, 16, 16).transpose(1, 2, 3, 0)
    sx = f["L0_tok_W_sx"].reshape(16, 3, 16, 16).transpose(1, 2, 3, 0)
    sy = f["L0_tok_W_sy"].reshape(16, 3, 16, 16).transpose(1, 2, 3, 0)
    w[:, :, 8:, 64:80] = sx[:, :, :8]
    w[:, :, :8, 80:96] = sx[:, :, 8:]
    w[:, 8:, :, 96:112] = sy[:, :8]
    w[:, :8, :, 112:128] = sy[:, 8:]
    a["w_tok"] = w.reshape(768, H)
    a["b_tok"] = np.concatenate([f["L0_tok_b_main"], f["L0_tok_b_sx"], f["L0_tok_b_sx"], f["L0_tok_b_sy"],
                                 f["L0_tok_b_sy"]])[:, None]
    a["ln_g"], a["ln_b"] = f["L0_tok_ln_g"][None], f["L0_tok_ln_b"][None]
    moves = np.zeros((4, H, H), np.float32)
    for s, (src, dst) in enumerate([(80, 64), (64, 80), (112, 96), (96, 112)]):
        for c in range(16):
            moves[s, src + c, dst + c] = 1
    a["moves"] = moves
    a["ident_d"] = np.eye(128, dtype=np.float32)
    before = np.triu(np.ones((HALF, HALF), np.float32), 1)
    a["tri"] = before
    freqs = np.float32(1.0) / np.float32(10000.0) ** (np.arange(0, HD, 2, dtype=np.float32) / np.float32(HD))
    ang = np.outer(np.arange(N, dtype=np.float32), freqs).astype(np.float32)
    cos, sin = np.cos(ang).T, np.sin(ang).T
    rope = np.zeros((128, 8, N), np.float32)
    for j in range(4):
        for d in range(HD):
            rope[32 * j + d, 0:4] = cos[d // 2]
            rope[32 * j + d, 4:8] = sin[d // 2] if d % 2 else -sin[d // 2]
    a["rope"] = rope

    def heads(wt, other=False):
        wt = wt.reshape(wt.shape[0], NH, HD)
        if other:
            wt = wt.reshape(-1, NH, HD // 2, 2)[..., ::-1].reshape(-1, NH, HD)
        o = np.zeros((wt.shape[0], NH, 32), np.float32)
        o[:, :, :HD] = wt
        return o.reshape(-1, 2, 128)

    wq, wk, wv = (f["L0_attn_Wqkv"][n * H:(n + 1) * H].T for n in range(3))
    bq, bk, bv = (f["L0_attn_bqkv"][n * H:(n + 1) * H] for n in range(3))
    a["w_qk0"] = np.concatenate([heads(wq), heads(wk), heads(wq, True), heads(wk, True)], 1)
    a["b_qk0"] = np.concatenate([heads(bq[None]), heads(bk[None]), heads(bq[None], True), heads(bk[None], True)], 1)[0].T
    a["w_v0"], a["b_v0"] = wv, bv[None]

    def heads_in(wt):
        return heads(wt.T).transpose(2, 1, 0)

    a["w_o0"] = heads_in(f["L0_attn_Wproj"].T)
    a["w_o0"][HD, 0] = f["L0_attn_bproj"]
    a["w_qk1"] = np.concatenate([heads(f["L0_ffn_wq"]), heads(f["L0_ffn_wk"])], 1)
    one = np.zeros((128, 1), np.float32)
    one[HD::32] = 1
    a["one_row"] = one
    a["w_v1"], a["w_o1"] = f["L0_ffn_wv"], heads_in(f["L0_ffn_wo"])
    a["g1"], a["be1"] = f["L0_ffn_ln1_g"][:, None], f["L0_ffn_ln1_b"][:, None]
    a["g2"], a["be2"] = f["L0_ffn_ln2_g"][None], f["L0_ffn_ln2_b"][None]
    a["w_r"], a["w1"], a["w2"], a["b2"] = f["L0_ffn_wr"], f["L0_ffn_w1"], f["L0_ffn_w2"], f["L0_ffn_b2"]
    a["b1"] = f["L0_ffn_b1"].reshape(E, 128, FC).transpose(1, 0, 2)
    return {k: np.ascontiguousarray(v) for k, v in a.items()}


_ORDER = ["x", "txt", "w_tok", "b_tok", "ln_g", "ln_b", "moves", "ident_d", "tri", "rope", "w_qk0", "b_qk0",
          "w_v0", "b_v0", "w_o0", "w_qk1", "one_row", "w_v1", "w_o1", "g1", "be1", "g2", "be2", "w_r", "w1", "b1",
          "w2", "b2"]


def kernel(**inputs):
    import concourse.bacc as _bacc
    from concourse import mybir as _mybir
    from concourse.bass_utils import run_bass_kernel_spmd as _run

    nc = _bacc.Bacc("TRN2", target_bir_lowering=False, num_devices=1)
    arrays = {"in_" + k: v for k, v in host_layout(inputs).items()}
    args = [nc.dram_tensor("in_" + k, arrays["in_" + k].shape, _mybir.dt.from_np(arrays["in_" + k].dtype),
                           kind="ExternalInput").ap() for k in _ORDER]
    out = nc.dram_tensor("out", (B, N, H), F32, kind="ExternalOutput").ap()
    program(nc, *args, out)
    r = _run(nc, [arrays], core_ids=[0])
    return r.results[0]["out"]
```
